# Optimizing a Trainium2 kernel written in Bass

```python
import numpy as np
import jax
import jax.numpy as jnp

def _softmax(x, axis=-1):
    return jax.nn.softmax(x, axis=axis)

def _gelu(x):
    return jax.nn.gelu(x, approximate=True)

def _silu(x):
    return jax.nn.silu(x)

def _sigmoid(x):
    return jax.nn.sigmoid(x)

def _layernorm(x, axis=-1, eps=1e-05):
    m = jnp.mean(x, axis=axis, keepdims=True)
    v = jnp.var(x, axis=axis, keepdims=True)
    return (x - m) / jnp.sqrt(v + eps)

def _scatter_add(tgt, idx, src, axis=0):
    return tgt.at[idx].add(src)

def _segment_sum(src, seg, n):
    return jax.ops.segment_sum(src, seg, n)
kernel_name = 'mk_hybrid_d1_jaxref_r8_a35934'

def setup_inputs(seed: int=0):
    np.random.seed(seed)
    _w = jnp.asarray

    def _L0_attn_a_setup():
        import jax, jax.numpy as jnp
        import numpy as np
        B, L, D, N = (4, 256, 128, 16)

        def _layernorm(x, g, b, eps=1e-05):
            mu = jnp.mean(x, axis=-1, keepdims=True)
            var = jnp.mean(jnp.square(x - mu), axis=-1, keepdims=True)
            return (x - mu) * jax.lax.rsqrt(var + eps) * g + b

        def _silu(x):
            return x * jax.nn.sigmoid(x)

        def _depthwise_conv(x, w):
            xc = x.transpose(0, 2, 1)
            y = jax.lax.conv_general_dilated(xc, w, window_strides=(1,), padding=[(1, 1)], feature_group_count=xc.shape[1], dimension_numbers=('NCH', 'OIH', 'NCH'))
            return y.transpose(0, 2, 1)

        def _selective_scan(u, A_log, D_skip, W_dt, b_dt, W_B, W_C):
            A = -jnp.exp(A_log)
            dt = jax.nn.softplus(u @ W_dt + b_dt)
            Bt = u @ W_B
            Ct = u @ W_C

            def step(h, inp):
                dt_t, B_t, C_t, u_t = inp
                dA = jnp.exp(dt_t[..., None] * A)
                h = dA * h + (dt_t * u_t)[..., None] * B_t[:, None, :]
                y = jnp.einsum('bdn,bn->bd', h, C_t)
                return (h, y)
            h0 = jnp.zeros((u.shape[0], u.shape[2], A.shape[1]), u.dtype)
            xs = (dt.transpose(1, 0, 2), Bt.transpose(1, 0, 2), Ct.transpose(1, 0, 2), u.transpose(1, 0, 2))
            _, ys = jax.lax.scan(step, h0, xs)
            return ys.transpose(1, 0, 2) + u * D_skip
        key = jax.random.key(seed)
        ks = jax.random.split(key, 12)
        s = 1.0 / np.sqrt(D)
        inp = {'x': jax.random.normal(ks[0], (B, L, D), jnp.float32), 'ln_g': jnp.ones((D,), jnp.float32), 'ln_b': jnp.zeros((D,), jnp.float32), 'w1_w': jax.random.normal(ks[1], (D, D), jnp.float32) * s, 'w1_b': jnp.zeros((D,), jnp.float32), 'v1_w': jax.random.normal(ks[2], (D, D), jnp.float32) * s, 'v1_b': jnp.zeros((D,), jnp.float32), 'w2_w': jax.random.normal(ks[3], (D, D), jnp.float32) * s, 'w2_b': jnp.zeros((D,), jnp.float32), 'conv_w': jax.random.normal(ks[4], (D, 1, 3), jnp.float32) * (1.0 / np.sqrt(3.0)), 'A_log': jnp.log(jnp.broadcast_to(jnp.arange(1, N + 1, dtype=jnp.float32), (D, N))), 'D_skip': jnp.ones((D,), jnp.float32), 'W_dt': jax.random.normal(ks[5], (D, D), jnp.float32) * (s * 0.1), 'b_dt': jnp.full((D,), -4.0, jnp.float32), 'W_B': jax.random.normal(ks[6], (D, N), jnp.float32) * s, 'W_C': jax.random.normal(ks[7], (D, N), jnp.float32) * s}
        return inp
    _L0_attn_a_in = _L0_attn_a_setup()

    def _L0_attn_b_setup():
        import jax, jax.numpy as jnp
        import numpy as np
        B, T, DIM, H = (4, 128, 128, 16)
        D = DIM // H

        def _lin(x, Wt, bias):
            return x @ Wt.T + bias

        def _l2norm(x, eps=1e-12):
            n = jnp.sqrt(jnp.sum(x * x, axis=-1, keepdims=True))
            return x / jnp.maximum(n, eps)
        key = jax.random.key(seed)
        ks = jax.random.split(key, 18)
        W = lambda k: jax.random.normal(k, (DIM, DIM), jnp.float32) * 0.02
        b = lambda k: jax.random.normal(k, (DIM,), jnp.float32) * 0.02
        return {'x': jax.random.normal(ks[0], (B, T, DIM), jnp.float32), 'Wsq': W(ks[1]), 'bsq': b(ks[2]), 'Wsk': W(ks[3]), 'bsk': b(ks[4]), 'Wsv': W(ks[5]), 'bsv': b(ks[6]), 'Wg': jax.random.normal(ks[7], (H, DIM), jnp.float32) * 0.02, 'bg': jax.random.normal(ks[8], (H,), jnp.float32) * 0.02, 'Wq': W(ks[9]), 'bq': b(ks[10]), 'Wk': W(ks[11]), 'bk': b(ks[12]), 'Wv': W(ks[13]), 'bv': b(ks[14]), 'Wo': W(ks[15]), 'bo': b(ks[16]), 'temp': jnp.ones((1, H, 1, 1), jnp.float32)}
    _L0_attn_b_in = _L0_attn_b_setup()

    def _L0_ffn_setup():
        import jax, jax.numpy as jnp
        import numpy as np
        from jax import lax
        B, N, D, H, E, K = (16, 128, 128, 512, 8, 2)
        key = jax.random.key(seed)
        ks = jax.random.split(key, 12)
        s = 0.02
        return {'x': jax.random.normal(ks[0], (B, N, D), jnp.float32), 'alpha': jnp.asarray(0.9, jnp.float32), 'w_gate': jax.random.normal(ks[1], (D, E), jnp.float32) * s, 'b_gate': jnp.zeros((E,), jnp.float32), 'W1m': jax.random.normal(ks[2], (D, H), jnp.float32) * s, 'b1m': jnp.zeros((H,), jnp.float32), 'W2m': jax.random.normal(ks[3], (H, D), jnp.float32) * s, 'b2m': jnp.zeros((D,), jnp.float32), 'W1e': jax.random.normal(ks[4], (E, D, H), jnp.float32) * s, 'b1e': jnp.zeros((E, H), jnp.float32), 'W2e': jax.random.normal(ks[5], (E, H, D), jnp.float32) * s, 'b2e': jnp.zeros((E, D), jnp.float32)}
    _L0_ffn_in = _L0_ffn_setup()
    _d = {'L0_attn_a_x': _L0_attn_a_in['x'], 'L0_attn_a_ln_g': _L0_attn_a_in['ln_g'], 'L0_attn_a_ln_b': _L0_attn_a_in['ln_b'], 'L0_attn_a_w1_w': _L0_attn_a_in['w1_w'], 'L0_attn_a_w1_b': _L0_attn_a_in['w1_b'], 'L0_attn_a_v1_w': _L0_attn_a_in['v1_w'], 'L0_attn_a_v1_b': _L0_attn_a_in['v1_b'], 'L0_attn_a_w2_w': _L0_attn_a_in['w2_w'], 'L0_attn_a_w2_b': _L0_attn_a_in['w2_b'], 'L0_attn_a_conv_w': _L0_attn_a_in['conv_w'], 'L0_attn_a_A_log': _L0_attn_a_in['A_log'], 'L0_attn_a_D_skip': _L0_attn_a_in['D_skip'], 'L0_attn_a_W_dt': _L0_attn_a_in['W_dt'], 'L0_attn_a_b_dt': _L0_attn_a_in['b_dt'], 'L0_attn_a_W_B': _L0_attn_a_in['W_B'], 'L0_attn_a_W_C': _L0_attn_a_in['W_C'], 'L0_attn_b_Wsq': _L0_attn_b_in['Wsq'], 'L0_attn_b_bsq': _L0_attn_b_in['bsq'], 'L0_attn_b_Wsk': _L0_attn_b_in['Wsk'], 'L0_attn_b_bsk': _L0_attn_b_in['bsk'], 'L0_attn_b_Wsv': _L0_attn_b_in['Wsv'], 'L0_attn_b_bsv': _L0_attn_b_in['bsv'], 'L0_attn_b_Wg': _L0_attn_b_in['Wg'], 'L0_attn_b_bg': _L0_attn_b_in['bg'], 'L0_attn_b_Wq': _L0_attn_b_in['Wq'], 'L0_attn_b_bq': _L0_attn_b_in['bq'], 'L0_attn_b_Wk': _L0_attn_b_in['Wk'], 'L0_attn_b_bk': _L0_attn_b_in['bk'], 'L0_attn_b_Wv': _L0_attn_b_in['Wv'], 'L0_attn_b_bv': _L0_attn_b_in['bv'], 'L0_attn_b_Wo': _L0_attn_b_in['Wo'], 'L0_attn_b_bo': _L0_attn_b_in['bo'], 'L0_attn_b_temp': _L0_attn_b_in['temp'], 'L0_ffn_alpha': _L0_ffn_in['alpha'], 'L0_ffn_w_gate': _L0_ffn_in['w_gate'], 'L0_ffn_b_gate': _L0_ffn_in['b_gate'], 'L0_ffn_W1m': _L0_ffn_in['W1m'], 'L0_ffn_b1m': _L0_ffn_in['b1m'], 'L0_ffn_W2m': _L0_ffn_in['W2m'], 'L0_ffn_b2m': _L0_ffn_in['b2m'], 'L0_ffn_W1e': _L0_ffn_in['W1e'], 'L0_ffn_b1e': _L0_ffn_in['b1e'], 'L0_ffn_W2e': _L0_ffn_in['W2e'], 'L0_ffn_b2e': _L0_ffn_in['b2e']}
    _x0 = _d['L0_attn_a_x']
    _d['L0_attn_a_x'] = jax.random.normal(jax.random.fold_in(jax.random.key(seed), 1), (4, 1024, 128), dtype=_x0.dtype)
    del _x0
    return _d

def reference(L0_attn_a_x, L0_attn_a_ln_g, L0_attn_a_ln_b, L0_attn_a_w1_w, L0_attn_a_w1_b, L0_attn_a_v1_w, L0_attn_a_v1_b, L0_attn_a_w2_w, L0_attn_a_w2_b, L0_attn_a_conv_w, L0_attn_a_A_log, L0_attn_a_D_skip, L0_attn_a_W_dt, L0_attn_a_b_dt, L0_attn_a_W_B, L0_attn_a_W_C, L0_attn_b_Wsq, L0_attn_b_bsq, L0_attn_b_Wsk, L0_attn_b_bsk, L0_attn_b_Wsv, L0_attn_b_bsv, L0_attn_b_Wg, L0_attn_b_bg, L0_attn_b_Wq, L0_attn_b_bq, L0_attn_b_Wk, L0_attn_b_bk, L0_attn_b_Wv, L0_attn_b_bv, L0_attn_b_Wo, L0_attn_b_bo, L0_attn_b_temp, L0_ffn_alpha, L0_ffn_w_gate, L0_ffn_b_gate, L0_ffn_W1m, L0_ffn_b1m, L0_ffn_W2m, L0_ffn_b2m, L0_ffn_W1e, L0_ffn_b1e, L0_ffn_W2e, L0_ffn_b2e):

    def _L0_attn_a_ref(x, ln_g, ln_b, w1_w, w1_b, v1_w, v1_b, w2_w, w2_b, conv_w, A_log, D_skip, W_dt, b_dt, W_B, W_C):
        import jax, jax.numpy as jnp
        import numpy as np
        B, L, D, N = (4, 256, 128, 16)

        def _layernorm(x, g, b, eps=1e-05):
            mu = jnp.mean(x, axis=-1, keepdims=True)
            var = jnp.mean(jnp.square(x - mu), axis=-1, keepdims=True)
            return (x - mu) * jax.lax.rsqrt(var + eps) * g + b

        def _silu(x):
            return x * jax.nn.sigmoid(x)

        def _depthwise_conv(x, w):
            xc = x.transpose(0, 2, 1)
            y = jax.lax.conv_general_dilated(xc, w, window_strides=(1,), padding=[(1, 1)], feature_group_count=xc.shape[1], dimension_numbers=('NCH', 'OIH', 'NCH'))
            return y.transpose(0, 2, 1)

        def _selective_scan(u, A_log, D_skip, W_dt, b_dt, W_B, W_C):
            A = -jnp.exp(A_log)
            dt = jax.nn.softplus(u @ W_dt + b_dt)
            Bt = u @ W_B
            Ct = u @ W_C

            def step(h, inp):
                dt_t, B_t, C_t, u_t = inp
                dA = jnp.exp(dt_t[..., None] * A)
                h = dA * h + (dt_t * u_t)[..., None] * B_t[:, None, :]
                y = jnp.einsum('bdn,bn->bd', h, C_t)
                return (h, y)
            h0 = jnp.zeros((u.shape[0], u.shape[2], A.shape[1]), u.dtype)
            xs = (dt.transpose(1, 0, 2), Bt.transpose(1, 0, 2), Ct.transpose(1, 0, 2), u.transpose(1, 0, 2))
            _, ys = jax.lax.scan(step, h0, xs)
            return ys.transpose(1, 0, 2) + u * D_skip
        x_norm = _layernorm(x, ln_g, ln_b)
        x1 = x_norm @ w1_w + w1_b
        x_conv = _silu(_depthwise_conv(x1, conv_w))
        x_ssm = _selective_scan(x_conv, A_log, D_skip, W_dt, b_dt, W_B, W_C)
        v = _silu(x_norm @ v1_w + v1_b)
        return x_ssm * v @ w2_w + w2_b

    def _L0_attn_b_ref(x, Wsq, bsq, Wsk, bsk, Wsv, bsv, Wg, bg, Wq, bq, Wk, bk, Wv, bv, Wo, bo, temp):
        import jax, jax.numpy as jnp
        import numpy as np
        B, T, DIM, H = (4, 128, 128, 16)
        D = DIM // H

        def _lin(x, Wt, bias):
            return x @ Wt.T + bias

        def _l2norm(x, eps=1e-12):
            n = jnp.sqrt(jnp.sum(x * x, axis=-1, keepdims=True))
            return x / jnp.maximum(n, eps)
        Bx, Tx, C = x.shape
        nh, hd = (H, C // H)
        sq = _lin(x, Wsq, bsq).reshape(Bx, Tx, nh, hd)
        sk = _lin(x, Wsk, bsk).reshape(Bx, Tx, nh, hd)
        sv = _lin(x, Wsv, bsv).reshape(Bx, Tx, nh, hd)
        g = jnp.exp(-jax.nn.softplus(_lin(x, Wg, bg)))

        def step(M, inp):
            g_t, k_t, v_t, q_t = inp
            M = g_t[..., None, None] * M + k_t[..., None] * v_t[..., None, :]
            h = jnp.einsum('bhd,bhde->bhe', q_t, M)
            return (M, h)
        xs = (g.transpose(1, 0, 2), sk.transpose(1, 0, 2, 3), sv.transpose(1, 0, 2, 3), sq.transpose(1, 0, 2, 3))
        M0 = jnp.zeros((Bx, nh, hd, hd), x.dtype)
        _, hs = jax.lax.scan(step, M0, xs)
        Hseq = hs.transpose(1, 0, 2, 3).reshape(Bx, Tx, C)
        Q = _lin(Hseq, Wq, bq).reshape(Bx, Tx, nh, hd).transpose(0, 2, 1, 3)
        K = _lin(Hseq, Wk, bk).reshape(Bx, Tx, nh, hd).transpose(0, 2, 1, 3)
        V = _lin(x, Wv, bv).reshape(Bx, Tx, nh, hd).transpose(0, 2, 1, 3)
        Q = _l2norm(Q)
        K = _l2norm(K)
        scores = jnp.einsum('bhqd,bhkd->bhqk', Q, K) * jax.nn.softplus(temp)
        attn = jax.nn.softmax(scores, axis=-1)
        out = jnp.einsum('bhqk,bhkd->bhqd', attn, V).transpose(0, 2, 1, 3).reshape(Bx, Tx, C)
        return _lin(out, Wo, bo)

    def _L0_ffn_ref(x, alpha, w_gate, b_gate, W1m, b1m, W2m, b2m, W1e, b1e, W2e, b2e):
        import jax, jax.numpy as jnp
        import numpy as np
        from jax import lax
        B, N, D, H, E, K = (16, 128, 128, 512, 8, 2)
        main = jax.nn.gelu(x @ W1m + b1m) @ W2m + b2m
        logits = jnp.mean(x, axis=1) @ w_gate + b_gate
        probs = jax.nn.softmax(logits, axis=-1)
        top_vals, top_idx = lax.top_k(probs, K)
        gate_w = top_vals / jnp.sum(top_vals, axis=-1, keepdims=True)
        W1g = W1e[top_idx]
        b1g = b1e[top_idx]
        W2g = W2e[top_idx]
        b2g = b2e[top_idx]
        h = jax.nn.gelu(jnp.einsum('bnd,bkdh->bknh', x, W1g) + b1g[:, :, None, :])
        eo = jnp.einsum('bknh,bkhd->bknd', h, W2g) + b2g[:, :, None, :]
        expert_out = jnp.einsum('bk,bknd->bnd', gate_w, eo)
        a = jnp.clip(alpha, 0.1, 1.0)
        return a * main + (1.0 - a) * expert_out
    x = L0_attn_a_x
    x = x + _L0_attn_a_ref(_layernorm(x, axis=-1), L0_attn_a_ln_g, L0_attn_a_ln_b, L0_attn_a_w1_w, L0_attn_a_w1_b, L0_attn_a_v1_w, L0_attn_a_v1_b, L0_attn_a_w2_w, L0_attn_a_w2_b, L0_attn_a_conv_w, L0_attn_a_A_log, L0_attn_a_D_skip, L0_attn_a_W_dt, L0_attn_a_b_dt, L0_attn_a_W_B, L0_attn_a_W_C)
    x = x + _L0_ffn_ref(_layernorm(x, axis=-1), L0_ffn_alpha, L0_ffn_w_gate, L0_ffn_b_gate, L0_ffn_W1m, L0_ffn_b1m, L0_ffn_W2m, L0_ffn_b2m, L0_ffn_W1e, L0_ffn_b1e, L0_ffn_W2e, L0_ffn_b2e)
    x = x + _L0_attn_b_ref(_layernorm(x, axis=-1), L0_attn_b_Wsq, L0_attn_b_bsq, L0_attn_b_Wsk, L0_attn_b_bsk, L0_attn_b_Wsv, L0_attn_b_bsv, L0_attn_b_Wg, L0_attn_b_bg, L0_attn_b_Wq, L0_attn_b_bq, L0_attn_b_Wk, L0_attn_b_bk, L0_attn_b_Wv, L0_attn_b_bv, L0_attn_b_Wo, L0_attn_b_bo, L0_attn_b_temp)
    x = x + _L0_ffn_ref(_layernorm(x, axis=-1), L0_ffn_alpha, L0_ffn_w_gate, L0_ffn_b_gate, L0_ffn_W1m, L0_ffn_b1m, L0_ffn_W2m, L0_ffn_b2m, L0_ffn_W1e, L0_ffn_b1e, L0_ffn_W2e, L0_ffn_b2e)
    return x

_drawn_inputs = setup_inputs


def setup_inputs(seed=0):
    import zlib

    import numpy as np

    out = dict(_drawn_inputs(seed))
    spreads = {'L0_attn_a_ln_g': (1.0, 0.2),
     'L0_attn_a_ln_b': (0.0, 0.1),
     'L0_attn_a_w1_b': (0.0, 0.1),
     'L0_attn_a_v1_b': (0.0, 0.1),
     'L0_attn_a_w2_b': (0.0, 0.1),
     'L0_attn_a_D_skip': (1.0, 0.2),
     'L0_attn_a_b_dt': (-4.0, 0.6),
     'L0_attn_b_temp': (1.0, 0.6),
     'L0_ffn_b_gate': (0.0, 0.722),
     'L0_ffn_b1m': (0.0, 0.1),
     'L0_ffn_b2m': (0.0, 0.1),
     'L0_ffn_b1e': (0.0, 0.8),
     'L0_ffn_b2e': (0.0, 0.618)}
    factors = {'L0_attn_a_W_dt': 8.0,
     'L0_attn_b_Wsq': 8.0,
     'L0_attn_b_bsq': 63.588,
     'L0_attn_b_Wsk': 8.0,
     'L0_attn_b_bsk': 55.246,
     'L0_attn_b_Wsv': 8.0,
     'L0_attn_b_bsv': 50.139,
     'L0_attn_b_Wg': 8.0,
     'L0_attn_b_bg': 64.0,
     'L0_attn_b_Wq': 8.0,
     'L0_attn_b_bq': 64.0,
     'L0_attn_b_Wk': 8.0,
     'L0_attn_b_bk': 64.0,
     'L0_attn_b_Wv': 8.0,
     'L0_attn_b_bv': 8.0,
     'L0_attn_b_Wo': 8.0,
     'L0_attn_b_bo': 3.005,
     'L0_ffn_w_gate': 7.654,
     'L0_ffn_W1e': 8.0,
     'L0_ffn_W2e': 8.0}
    for name, (base, spread) in spreads.items():
        noise = np.random.default_rng([zlib.crc32(name.encode()), seed]).standard_normal(out[name].shape)
        drawn = base * np.exp(spread * noise) if base else spread * noise
        out[name] = jnp.asarray(drawn.astype(out[name].dtype))
    for name, factor in factors.items():
        out[name] = (out[name] * factor).astype(out[name].dtype)
    return out
```

```python
from contextlib import ExitStack

import numpy as np

import concourse.bass as bass
from concourse import mybir

ALU = mybir.AluOpType
ACT = mybir.ActivationFunctionType
AX = mybir.AxisListType
F32 = mybir.dt.float32
F16 = mybir.dt.float16
BF16 = mybir.dt.bfloat16
U32 = mybir.dt.uint32

P = 128
B, T = 4, 1024
HALF = 512
HALVES = (slice(0, HALF), slice(HALF, T))
NT = HALF // P
TT = T // P
NS = 16
H, HD = 16, 8
E, F = 8, 512
FC = F // P
G = 4
GH = H // G
KC = T // P
EPS = 1e-5
BC3 = 3 * 2 * NS

VEC_SIZES = (("ln_g", 1), ("ln_b", 1), ("w1_b", 1), ("v1_b", 1), ("w2_b", 1), ("conv", 3), ("d_skip", 1),
             ("b_dt", 1), ("a_log", NS), ("bsk", 1), ("bsq", 1), ("bg", 1), ("bsv", HD), ("bv", 1), ("bo", 1),
             ("alpha", 1), ("b1m", FC), ("b2m", 1), ("temp", H), ("head_mask", GH))
VEC = {}
NV = 0
for _name, _n in VEC_SIZES:
    VEC[_name] = NV
    NV += _n

SSM_MATS = ("w1", "v1", "w2", "wdt")
RET_MATS = ("wsk", "wsq", "wg", "wv")
ATT_MATS = ("wq", "wk")


class Count:
    def __init__(self, sem, per=1, start=0):
        self.sem, self.per, self.start = sem, per, start

    def at(self, i, n=0):
        return i * self.per + (self.start + n + 1)

    def before(self, i, n, k):
        assert self.start >= k
        return i * self.per + (self.start + n + 1 - k)


class Stage:

    def __init__(self, nc, name):
        self.nc, self.name, self.ctx = nc, name, ExitStack()

    def __enter__(self):
        return self

    def __exit__(self, *a):
        return self.ctx.__exit__(*a)

    def sb(self, name, shape, dt=F32):
        return self.ctx.enter_context(self.nc.sbuf_tensor(f"{self.name}_{name}", shape, dt))

    def ps(self, name, shape, dt=F32):
        return self.ctx.enter_context(self.nc.psum_tensor(f"{self.name}_{name}", shape, dt))

    def sem(self, name):
        return self.ctx.enter_context(self.nc.semaphore(f"{self.name}_{name}"))

    def count(self, name, per=1, start=0):
        return Count(self.sem(name), per, start)


class Layer:

    def __init__(self, nc, dram):
        self.nc, self.dram = nc, dram

    def col(self, name, k=0, n=1):
        return self.vec[:, VEC[name] + k:VEC[name] + k + n]


def load_constants(t, whole):
    nc, d = t.nc, t.dram
    t.x_t = whole.sb("x_t", [P, B, T])
    t.z_sum = whole.sb("z_sum", [P, B, 2])
    t.vec = whole.sb("vec", [P, NV])
    t.ident = whole.sb("ident", [P, P])
    t.minus_half = whole.sb("minus_half", [P, P])
    t.eps = whole.sb("eps", [P, NT])
    t.blend = whole.sb("blend", [P, 2])
    t.w_gate = whole.sb("w_gate", [P, E])
    t.b_gate = whole.sb("b_gate", [1, E])
    t.ones_row = whole.sb("ones_row", [1, P])
    with Stage(nc, "load") as s:
        loaded, clipped = s.sem("loaded"), s.sem("clipped")
        with nc.Block() as block:

            @block.sync
            def _(sp):
                for dst, src in ((t.vec, d["vecs"]), (t.ident, d["ident"]), (t.w_gate, d["w_gate"]),
                                 (t.b_gate, d["b_gate"])):
                    sp.dma_start(dst[:, :], src).then_inc(loaded, 16)
                sp.wait_ge(loaded, 16 * 4)

            @block.vector
            def _(dve):
                dve.memset(t.minus_half[:, :], -0.5)
                dve.memset(t.eps[:, :], EPS)
                dve.memset(t.ones_row[:, :], 1.0)
                dve.wait_ge(loaded, 16 * 4)
                dve.tensor_scalar(t.blend[:, 0:1], t.col("alpha"), 0.1, 1.0, ALU.max, ALU.min).then_inc(clipped, 1)
                dve.wait_ge(clipped, 1)
                dve.tensor_scalar(t.blend[:, 1:2], t.blend[:, 0:1], -1.0, 1.0, ALU.mult, ALU.add)


def layernorm(t, name, first=False):
    nc, d = t.nc, t.dram
    with Stage(nc, name) as s:
        x_half = s.sb("x_half", [P, 2, HALF])
        x_tok = s.sb("x_tok", [P, 2, NT, P])
        stats = s.sb("stats", [P, 2, NT, 6])
        mv = s.sb("mv", [P, 2, NT, 2])
        rstd = s.sb("rstd", [P, 2, NT])
        rtmp = s.sb("rtmp", [P, 2, 5, NT])
        z_tok = s.sb("z_tok", [P, 2, NT, P])
        tok_ps = [s.ps(f"tok_ps{k}", [P, NT, P]) for k in range(2)]
        z_ps = [s.ps(f"z_ps{k}", [P, HALF]) for k in range(2)]
        x_loaded = [s.sem(f"x_loaded{k}") for k in range(2)]
        RS = 7 if first else 2
        x_staged = s.count("x_staged", 2)
        turned = s.count("turned", 2, 2)
        kept = s.count("kept", 2, 2)
        got_mv = s.count("got_mv", 2 * NT)
        rstd_steps = s.count("rstd_steps", 2 * RS)
        normed = s.count("normed", 2 * NT, 2 * NT)
        z_turned = s.count("z_turned", 2, 2)
        z_copied = s.count("z_copied", 2, 2)
        with nc.Block() as block:

            if first:
                @block.sync
                def _(sp):
                    with sp.Fori(0, B) as b:
                        for k in range(2):
                            sp.wait_ge(z_turned.sem, z_turned.before(b, k, 2))
                            sp.dma_start(x_tok[:, k, :, :], d["x"][b, k]).then_inc(x_loaded[k], 16)

            @block.tensor
            def _(pe):
                pe.sem_inc(turned.sem, turned.start)
                pe.sem_inc(z_turned.sem, z_turned.start)
                with pe.Fori(0, B) as b:
                    for k in range(2):
                        if first:
                            pe.wait_ge(x_loaded[k], b * 16 + 16)
                            pe.wait_ge(kept.sem, kept.before(b, k, 2))
                        else:
                            pe.wait_ge(x_staged.sem, x_staged.at(b, k))
                            pe.wait_ge(normed.sem, normed.before(b, k * NT + NT - 1, 2 * NT))
                        for j in range(NT):
                            src = x_tok[:, k, j, :] if first else x_half[:, k, j * P:(j + 1) * P]
                            last = pe.transpose(tok_ps[k][:, j, :], src, t.ident[:, :])
                        last.then_inc(turned.sem, 1)
                    for k in range(2):
                        pe.wait_ge(normed.sem, normed.at(b, k * NT + NT - 1))
                        pe.wait_ge(z_copied.sem, z_copied.before(b, k, 2))
                        for j in range(NT):
                            last = pe.transpose(z_ps[k][:, j * P:(j + 1) * P], z_tok[:, k, j, :], t.ident[:, :])
                        last.then_inc(z_turned.sem, 1)

            @block.vector
            def _(dve):
                dve.sem_inc(normed.sem, normed.start)
                with dve.Fori(0, B) as b:
                    for k in range(2):
                        if first:
                            dve.wait_ge(x_loaded[k], b * 16 + 16)
                        else:
                            dve.wait_ge(turned.sem, turned.at(b, k))
                        dve.wait_ge(normed.sem, normed.before(b, k * NT + NT - 1, 2 * NT))
                        for j in range(NT):
                            src = x_tok[:, k, j, :] if first else tok_ps[k][:, j, :]
                            dve.bn_stats(stats[:, k, j, :], src)
                        dve.drain()
                        for j in range(NT):
                            dve.bn_aggr(mv[:, k, j, :], stats[:, k, j, :]).then_inc(got_mv.sem, 1)
                    for k in range(2):
                        dve.wait_ge(rstd_steps.sem, rstd_steps.at(b, k * RS + RS - 1))
                        dve.wait_ge(z_turned.sem, z_turned.before(b, k, 2))
                        for j in range(NT):
                            src = x_tok[:, k, j, :] if first else tok_ps[k][:, j, :]
                            dve.tensor_scalar(z_tok[:, k, j, :], src, mv[:, k, j, 0:1], rstd[:, k, j:j + 1],
                                              ALU.subtract, ALU.mult).then_inc(normed.sem, 1)

            @block.gpsimd
            def _(pool):
                half, eps = t.minus_half[:, 0:NT], t.eps[:, :]
                with pool.Fori(0, B) as b:
                    for k in range(2):
                        var = mv[:, k, :, 1]
                        veps, r1, v1, v2, v3 = (rtmp[:, k, i, :] for i in range(5))
                        pool.wait_ge(got_mv.sem, got_mv.at(b, k * NT + NT - 1))
                        pool.wait_ge(normed.sem, normed.before(b, k * NT + NT - 1, 2 * NT))
                        pool.tensor_tensor(veps, var, eps, ALU.add).then_inc(rstd_steps.sem, 1)
                        pool.wait_ge(rstd_steps.sem, rstd_steps.at(b, k * RS))
                        if not first:
                            pool.tensor_tensor(rstd[:, k, :], veps, half, ALU.pow).then_inc(rstd_steps.sem, 1)
                            continue
                        pool.tensor_tensor(r1, veps, half, ALU.pow).then_inc(rstd_steps.sem, 1)
                        pool.wait_ge(rstd_steps.sem, rstd_steps.at(b, k * RS + 1))
                        pool.tensor_tensor(v1, var, r1, ALU.mult).then_inc(rstd_steps.sem, 1)
                        pool.wait_ge(rstd_steps.sem, rstd_steps.at(b, k * RS + 2))
                        pool.tensor_tensor(v2, v1, r1, ALU.mult).then_inc(rstd_steps.sem, 1)
                        pool.wait_ge(rstd_steps.sem, rstd_steps.at(b, k * RS + 3))
                        pool.tensor_tensor(v3, v2, eps, ALU.add).then_inc(rstd_steps.sem, 1)
                        pool.wait_ge(rstd_steps.sem, rstd_steps.at(b, k * RS + 4))
                        pool.tensor_tensor(v1, v3, half, ALU.pow).then_inc(rstd_steps.sem, 1)
                        pool.wait_ge(rstd_steps.sem, rstd_steps.at(b, k * RS + 5))
                        pool.tensor_tensor(rstd[:, k, :], v1, r1, ALU.mult).then_inc(rstd_steps.sem, 1)

            @block.scalar
            def _(act):
                act.sem_inc(kept.sem, kept.start)
                act.sem_inc(z_copied.sem, z_copied.start)
                with act.Fori(0, B) as b:
                    for k in range(2):
                        if first:
                            act.wait_ge(turned.sem, turned.at(b, k))
                            act.activation(t.x_t[:, b, HALVES[k]], tok_ps[k][:, :, :].rearrange("p a c -> p (a c)"),
                                           ACT.Copy).then_inc(kept.sem, 1)
                        else:
                            act.wait_ge(turned.sem, turned.before(b, k, 2))
                            act.activation(x_half[:, k, :], t.x_t[:, b, HALVES[k]],
                                           ACT.Copy).then_inc(x_staged.sem, 1)
                    for k in range(2):
                        act.wait_ge(z_turned.sem, z_turned.at(b, k))
                        if first:
                            act.activation(t.z_t[:, b, HALVES[k]], z_ps[k][:, :], ACT.Identity, bias=t.col("ln_b"),
                                           scale=t.col("ln_g")).then_inc(z_copied.sem, 1)
                        else:
                            act.activation(t.z_t[:, b, HALVES[k]], z_ps[k][:, :], ACT.Copy,
                                           accum_out=t.z_sum[:, b, k:k + 1]).then_inc(z_copied.sem, 1)


def product(pe, out, w, rhs, start=True, stop=True):
    for h in HALVES:
        last = pe.matmul(out[:, h], w, rhs[:, h], start=start, stop=stop)
    return last


def scan_buffers(t, s):
    t.ssm_mats = s.sb("mats", [P, len(SSM_MATS), P])
    t.ssm_w = {n: t.ssm_mats[:, i, :] for i, n in enumerate(SSM_MATS)}
    t.u_t, t.v_t, t.dt_t, t.du_t = (s.sb(n, [P, B, T]) for n in ("u_t", "v_t", "dt_t", "du_t"))
    t.bc = s.sb("bc", [BC3, B, T], BF16)
    t.sel = s.sb("sel", [BC3, 2 * NS, P], BF16)


def scan_inputs(t, big):
    nc, d = t.nc, t.dram
    mats = t.ssm_mats
    wbc = big.sb("wbc", [P, BC3])
    pick = big.sb("pick", [BC3, 2 * NS])
    x1 = big.sb("x1", [P, T + 2])
    y0, y1, y2 = (big.sb(n, [P, T]) for n in ("y0", "y1", "y2"))
    w_ready, wbc_ready = big.sem("w_ready"), big.sem("wbc_ready")
    with Stage(nc, "conv") as q:
        x1_ps, v_ps = q.ps("x1_ps", [P, T]), q.ps("v_ps", [P, T])
        padded = q.sem("padded")
        x1_made, v_made = q.count("x1_made"), q.count("v_made")
        x1_copied, v_silu = q.count("x1_copied", 1, 1), q.count("v_silu", 1, 1)
        conv_steps = q.count("conv_steps", 3, 3)
        u_made = q.count("u_made", 1, 1)
        with nc.Block() as block:

            @block.sync
            def _(sp):
                sp.dma_start(mats[:, :, :], d["ssm_mats"]).then_inc(w_ready, 16)
                sp.dma_start(wbc[:, :], d["wbc"]).then_inc(wbc_ready, 16)
                sp.dma_start(pick[:, :], d["pick"]).then_inc(wbc_ready, 16)
                sp.wait_ge(w_ready, 16)
                sp.wait_ge(wbc_ready, 32)

            @block.tensor
            def _(pe):
                pe.wait_ge(w_ready, 16)
                with pe.Fori(0, B) as b:
                    pe.wait_ge(x1_copied.sem, x1_copied.before(b, 0, 1))
                    product(pe, x1_ps, t.ssm_w["w1"], t.z_t[:, b, :]).then_inc(x1_made.sem, 1)
                    pe.wait_ge(v_silu.sem, v_silu.before(b, 0, 1))
                    product(pe, v_ps, t.ssm_w["v1"], t.z_t[:, b, :]).then_inc(v_made.sem, 1)

            @block.scalar
            def _(act):
                act.sem_inc(x1_copied.sem, 1)
                act.sem_inc(v_silu.sem, 1)
                act.sem_inc(u_made.sem, 1)
                with act.Fori(0, B) as b:
                    act.wait_ge(x1_made.sem, x1_made.at(b))
                    act.wait_ge(conv_steps.sem, conv_steps.before(b, 2, 3))
                    act.activation(x1[:, 1:T + 1], x1_ps[:, :], ACT.Identity,
                                   bias=t.col("w1_b")).then_inc(x1_copied.sem, 1)
                    act.wait_ge(v_made.sem, v_made.at(b))
                    act.activation(t.v_t[:, b, :], v_ps[:, :], ACT.Silu, bias=t.col("v1_b")).then_inc(v_silu.sem, 1)
                    act.wait_ge(conv_steps.sem, conv_steps.at(b, 2))
                    act.activation(t.u_t[:, b, :], y2[:, :], ACT.Silu).then_inc(u_made.sem, 1)

            @block.vector
            def _(dve):
                dve.sem_inc(conv_steps.sem, 3)
                dve.memset(x1[:, 0:1], 0.0)
                dve.memset(x1[:, T + 1:T + 2], 0.0).then_inc(padded, 1)
                dve.wait_ge(padded, 1)
                with dve.Fori(0, B) as b:
                    dve.wait_ge(x1_copied.sem, x1_copied.at(b))
                    dve.tensor_scalar(y0[:, :], x1[:, 0:T], t.col("conv", 0), None,
                                      ALU.mult).then_inc(conv_steps.sem, 1)
                    dve.wait_ge(conv_steps.sem, conv_steps.at(b, 0))
                    dve.scalar_tensor_tensor(y1[:, :], x1[:, 1:T + 1], t.col("conv", 1), y0[:, :], ALU.mult,
                                             ALU.add).then_inc(conv_steps.sem, 1)
                    dve.wait_ge(conv_steps.sem, conv_steps.at(b, 1))
                    dve.wait_ge(u_made.sem, u_made.before(b, 0, 1))
                    dve.scalar_tensor_tensor(y2[:, :], x1[:, 2:T + 2], t.col("conv", 2), y1[:, :], ALU.mult,
                                             ALU.add).then_inc(conv_steps.sem, 1)
                dve.wait_ge(wbc_ready, 32)
                dve.tensor_copy(t.sel[:, :, :],
                                pick[:, :].rearrange("p (n o) -> p n o", o=1).broadcast_to([BC3, 2 * NS, P]))

    with Stage(nc, "dt") as q:
        dt_ps, bc_ps = q.ps("dt_ps", [P, T]), q.ps("bc_ps", [P, T])
        hi, mid = q.sb("hi", [BC3, T], BF16), q.sb("mid", [BC3, T], BF16)
        rest = q.sb("rest", [BC3, T])
        dt_made, bc_made = q.count("dt_made"), q.count("bc_made")
        soft_steps = q.count("soft_steps", 4, 4)
        dt_done = q.count("dt_done", 1, 1)
        split_steps = q.count("split_steps", 6, 6)
        with nc.Block() as block:

            @block.tensor
            def _(pe):
                with pe.Fori(0, B) as b:
                    pe.wait_ge(soft_steps.sem, soft_steps.before(b, 0, 4))
                    product(pe, dt_ps, t.ssm_w["wdt"], t.u_t[:, b, :]).then_inc(dt_made.sem, 1)
                    pe.wait_ge(split_steps.sem, split_steps.before(b, 5, 6))
                    product(pe, bc_ps[0:BC3, :], wbc[:, :], t.u_t[:, b, :]).then_inc(bc_made.sem, 1)

            @block.scalar
            def _(act):
                act.sem_inc(soft_steps.sem, soft_steps.start)
                with act.Fori(0, B) as b:
                    act.wait_ge(dt_made.sem, dt_made.at(b))
                    act.wait_ge(dt_done.sem, dt_done.before(b, 0, 1))
                    act.activation(x1[:, 0:T], dt_ps[:, :], ACT.Identity,
                                   bias=t.col("b_dt")).then_inc(soft_steps.sem, 1)
                    act.wait_ge(soft_steps.sem, soft_steps.at(b, 0))
                    act.activation(y0[:, :], x1[:, 0:T], ACT.Abs).then_inc(soft_steps.sem, 1)
                    act.wait_ge(soft_steps.sem, soft_steps.at(b, 1))
                    act.activation(y1[:, :], y0[:, :], ACT.Exp, scale=-1.0).then_inc(soft_steps.sem, 1)
                    act.wait_ge(soft_steps.sem, soft_steps.at(b, 2))
                    act.activation(y2[:, :], y1[:, :], ACT.Ln, bias=1.0).then_inc(soft_steps.sem, 1)

            @block.vector
            def _(dve):
                dve.sem_inc(dt_done.sem, 1)
                dve.sem_inc(split_steps.sem, 6)
                with dve.Fori(0, B) as b:
                    dve.wait_ge(bc_made.sem, bc_made.at(b))
                    dve.tensor_copy(hi[:, :], bc_ps[0:BC3, :]).then_inc(split_steps.sem, 1)
                    dve.wait_ge(split_steps.sem, split_steps.at(b, 0))
                    dve.tensor_tensor(rest[:, :], bc_ps[0:BC3, :], hi[:, :], ALU.subtract).then_inc(split_steps.sem, 1)
                    dve.wait_ge(split_steps.sem, split_steps.at(b, 1))
                    dve.tensor_copy(mid[:, :], rest[:, :]).then_inc(split_steps.sem, 1)
                    dve.wait_ge(split_steps.sem, split_steps.at(b, 2))
                    dve.tensor_tensor(t.bc[:, b, :], rest[:, :], mid[:, :], ALU.subtract).then_inc(split_steps.sem, 1)
                    dve.wait_ge(split_steps.sem, split_steps.at(b, 3))
                    dve.tensor_scalar(t.bc[0:32, b, :], hi[0:32, :], 1.0, None, ALU.mult).then_inc(split_steps.sem, 1)
                    dve.tensor_scalar(t.bc[32:64, b, :], mid[32:64, :], 1.0, None, ALU.mult).then_inc(split_steps.sem, 1)
                    dve.wait_ge(split_steps.sem, split_steps.at(b, 5))
                    dve.wait_ge(soft_steps.sem, soft_steps.at(b, 3))
                    dve.scalar_tensor_tensor(t.dt_t[:, b, :], x1[:, 0:T], 0.0, y2[:, :], ALU.max,
                                             ALU.add).then_inc(dt_done.sem, 1)

            @block.gpsimd
            def _(pool):
                with pool.Fori(0, B) as b:
                    pool.wait_ge(dt_done.sem, dt_done.at(b))
                    pool.tensor_tensor(t.du_t[:, b, :], t.dt_t[:, b, :], t.u_t[:, b, :], ALU.mult)


def selective_scan(t):
    nc = t.nc
    LAG = 3
    TAIL = NS + LAG + 1
    with Stage(nc, "scan") as s:
        a_neg = s.sb("a_neg", [P, NS])
        dt_b = s.sb("dt_b", [P, T])
        decay = s.sb("decay", [P, 2, T])
        drive = s.sb("drive", [P, 2, T])
        state = s.sb("state", [P, 2, T])
        c_rep = s.sb("c_rep", [P, 2, T])
        hc = s.sb("hc", [P, 4, T])
        y_sb = s.sb("y_sb", [P, T])
        yv = s.sb("yv", [P, T])
        b_ps = [s.ps(f"b_ps{k}", [P, T]) for k in range(2)]
        c_ps, y_ps = (s.ps(n, [P, T]) for n in ("c_ps", "y_ps"))
        a_steps = s.sem("a_steps")
        b_spread = s.count("b_spread", NS)
        c_spread = s.count("c_spread", NS)
        summed = s.count("summed", NS, 4)
        dt_staged = s.count("dt_staged")
        decayed = s.count("decayed", NS, 1)
        c_copied = s.count("c_copied", NS, 1)
        driven = s.count("driven", NS, 2)
        scanned = s.count("scanned", NS, 2)
        weighed = s.count("weighed", NS, 2)
        y_steps = s.count("y_steps", 2, 2)
        projected = s.count("projected", 1, 1)
        added = s.count("added", 1, 1)

        def batches(eng, body):
            first, end = TAIL + 2 - NS, TAIL + 2
            for n in range(first):
                body(0, n)
            with eng.Fori(0, B - 1) as b:
                for n in range(first, end):
                    body(b, n)
            for n in range(first, end):
                body(B - 1, n)

        def there(b, n):
            return n < NS or not isinstance(b, int) or b < B - 1

        with nc.Block() as block:

            @block.tensor
            def _(pe):
                pe.sem_inc(summed.sem, summed.start)
                pe.sem_inc(projected.sem, projected.start)

                def body(b, n):
                    if there(b, n):
                        at, m = b + n // NS, n % NS
                        pe.wait_ge(driven.sem, driven.before(b, n, 2))
                        if n == TAIL + 1:
                            pe.wait_ge(added.sem, added.at(b))
                        product(pe, b_ps[n % 2], t.sel[:, m, :], t.bc[:, at, :]).then_inc(b_spread.sem, 1)
                        pe.wait_ge(c_copied.sem, c_copied.before(b, n, 1))
                        product(pe, c_ps, t.sel[:, NS + m, :], t.bc[:, at, :]).then_inc(c_spread.sem, 1)
                    k = n - LAG
                    if k >= 0 and there(b, k):
                        pe.wait_ge(weighed.sem, weighed.at(b, k))
                        if k % NS == 0:
                            pe.wait_ge(y_steps.sem, y_steps.before(b, 2 * (k // NS), 2))
                        product(pe, y_ps, t.ident[:, :], hc[:, k % 4, :], start=k % NS == 0,
                                stop=k % NS == NS - 1).then_inc(summed.sem, 1)
                    if n == TAIL:
                        pe.wait_ge(y_steps.sem, y_steps.at(b, 1))
                        if there(b, n):
                            pe.wait_ge(driven.sem, driven.at(b, n - 1))
                        product(pe, b_ps[(TAIL + 1) % 2], t.ssm_w["w2"], yv[:, :]).then_inc(projected.sem, 1)

                batches(pe, body)

            @block.scalar
            def _(act):
                act.sem_inc(c_copied.sem, c_copied.start)
                act.activation(a_neg[:, :], t.col("a_log", 0, NS), ACT.Exp).then_inc(a_steps, 1)
                act.wait_ge(a_steps, 1)
                act.mul(a_neg[:, :], a_neg[:, :], -1.0).then_inc(a_steps, 1)
                act.wait_ge(a_steps, 2)
                act.sem_inc(decayed.sem, decayed.start)
                with act.Fori(0, B) as b:
                    act.wait_ge(decayed.sem, decayed.before(b, 0, 1))
                    act.activation(dt_b[:, :], t.dt_t[:, b, :], ACT.Copy).then_inc(dt_staged.sem, 1)
                    act.wait_ge(dt_staged.sem, dt_staged.at(b))
                    for n in range(NS):
                        act.wait_ge(scanned.sem, scanned.before(b, n, 2))
                        act.activation(decay[:, n % 2, :], dt_b[:, :], ACT.Exp,
                                       scale=a_neg[:, n:n + 1]).then_inc(decayed.sem, 1)
                        act.wait_ge(c_spread.sem, c_spread.at(b, n))
                        act.wait_ge(weighed.sem, weighed.before(b, n, 2))
                        act.activation(c_rep[:, n % 2, :], c_ps[:, :], ACT.Copy).then_inc(c_copied.sem, 1)

            @block.vector
            def _(dve):
                dve.sem_inc(driven.sem, driven.start)
                dve.sem_inc(scanned.sem, scanned.start)
                dve.sem_inc(y_steps.sem, y_steps.start)
                dve.sem_inc(added.sem, added.start)

                def body(b, n):
                    if there(b, n):
                        dve.wait_ge(b_spread.sem, b_spread.at(b, n))
                        dve.wait_ge(scanned.sem, scanned.before(b, n, 2))
                        dve.tensor_tensor(drive[:, n % 2, :], b_ps[n % 2][:, :], t.du_t[:, b + n // NS, :],
                                          ALU.mult).then_inc(driven.sem, 1)
                    k = n - 1
                    if k >= 0 and there(b, k):
                        dve.wait_ge(driven.sem, driven.at(b, k))
                        dve.wait_ge(decayed.sem, decayed.at(b, k))
                        dve.wait_ge(weighed.sem, weighed.before(b, k, 2))
                        dve.tensor_tensor_scan(state[:, k % 2, :], decay[:, k % 2, :], drive[:, k % 2, :], 0.0,
                                               ALU.mult, ALU.add).then_inc(scanned.sem, 1)
                    if n == TAIL - 1:
                        dve.wait_ge(summed.sem, summed.at(b, NS - 1))
                        dve.scalar_tensor_tensor(y_sb[:, :], t.u_t[:, b, :], t.col("d_skip"), y_ps[:, :], ALU.mult,
                                                 ALU.add).then_inc(y_steps.sem, 1)
                        dve.wait_ge(y_steps.sem, y_steps.at(b, 0))
                        dve.wait_ge(projected.sem, projected.before(b, 0, 1))
                        dve.tensor_tensor(yv[:, :], y_sb[:, :], t.v_t[:, b, :], ALU.mult).then_inc(y_steps.sem, 1)
                    if n == TAIL:
                        dve.wait_ge(projected.sem, projected.at(b))
                        dve.scalar_tensor_tensor(t.x_t[:, b, :], b_ps[(TAIL + 1) % 2][:, :], t.col("w2_b"),
                                                 t.x_t[:, b, :], ALU.add, ALU.add).then_inc(added.sem, 1)

                batches(dve, body)

            @block.gpsimd
            def _(pool):
                pool.sem_inc(weighed.sem, weighed.start)
                with pool.Fori(0, B) as b:
                    for n in range(NS):
                        pool.wait_ge(scanned.sem, scanned.at(b, n))
                        pool.wait_ge(c_copied.sem, c_copied.at(b, n))
                        pool.wait_ge(summed.sem, summed.before(b, n, 4))
                        pool.tensor_tensor(hc[:, n % 4, :], state[:, n % 2, :], c_rep[:, n % 2, :],
                                           ALU.mult).then_inc(weighed.sem, 1)


def ffn(t, name):
    nc, d = t.nc, t.dram
    with Stage(nc, name) as s:
        w1m = s.sb("w1m", [P, F])
        w2m = s.sb("w2m", [P, FC, P])
        logits = s.sb("logits", [1, B, E])
        best = s.sb("best", [1, B, 8])
        which = s.sb("which", [1, B, 8], U32)
        gap = s.sb("gap", [1, B])
        th = s.sb("th", [1, B])
        share_row = s.sb("share_row", [1, B, 2])
        share = s.sb("share", [P, B, 2])
        m_loaded, m_scaled = s.sem("m_loaded"), s.sem("m_scaled")
        with Stage(nc, name + "_gate") as q:
            gate_ps = q.ps("gate_ps", [1, B, E])
            share_ps = q.ps("share_ps", [P, 2 * B])
            scored, picked, spread = q.sem("scored"), q.sem("picked"), q.sem("spread")
            tanh_done = q.sem("tanh_done")
            with nc.Block() as block:

                @block.sync
                def _(sp):
                    sp.dma_start(w1m[:, :], d["w1m"]).then_inc(m_loaded, 16)
                    sp.dma_start(w2m[:, :, :], d["w2m"]).then_inc(m_loaded, 16)
                    sp.wait_ge(m_loaded, 32)

                @block.tensor
                def _(pe):
                    for b in range(B):
                        for k in range(2):
                            last = pe.matmul(gate_ps[:, b, :], t.z_sum[:, b, k:k + 1], t.w_gate[:, :], start=k == 0,
                                             stop=k == 1)
                    last.then_inc(scored, 1)
                    pe.wait_ge(picked, 3 * B + 3)
                    pe.matmul(share_ps[:, :], t.ones_row[:, :], share_row[:, :, :].rearrange("p b k -> p (b k)"),
                              start=True, stop=True).then_inc(spread, 1)

                @block.vector
                def _(dve):
                    dve.wait_ge(scored, 1)
                    for b in range(B):
                        dve.scalar_tensor_tensor(logits[:, b, :], gate_ps[:, b, :], 1.0 / T, t.b_gate[:, :], ALU.mult,
                                                 ALU.add).then_inc(picked, 1)
                    dve.wait_ge(picked, B)
                    for b in range(B):
                        dve.max(best[:, b, :], logits[:, b, :]).then_inc(picked, 1)
                    dve.wait_ge(picked, 2 * B)
                    for b in range(B):
                        dve.max_index(which[:, b, :], best[:, b, :], logits[:, b, :]).then_inc(picked, 1)
                    dve.tensor_tensor(gap[:, :], best[:, :, 0], best[:, :, 1], ALU.subtract).then_inc(picked, 1)
                    dve.wait_ge(tanh_done, 1)
                    dve.tensor_scalar(share_row[:, :, 0], th[:, :], 0.5, 0.5, ALU.mult, ALU.add).then_inc(picked, 1)
                    dve.tensor_scalar(share_row[:, :, 1], th[:, :], -0.5, 0.5, ALU.mult, ALU.add).then_inc(picked, 1)
                    dve.wait_ge(spread, 1)
                    dve.tensor_scalar(share[:, :, :].rearrange("p b k -> p (b k)"), share_ps[:, :],
                                      t.blend[:, 1:2], None, ALU.mult)
                    dve.wait_ge(m_loaded, 32)
                    dve.tensor_scalar(w2m[:, :, :], w2m[:, :, :], t.blend[:, 0:1], None, ALU.mult)

                @block.scalar
                def _(act):
                    act.wait_ge(picked, 3 * B + 1)
                    act.activation(th[:, :], gap[:, :], ACT.Tanh, scale=0.5).then_inc(tanh_done, 1)

        w1e = [s.sb(f"w1e{k}", [P, F]) for k in range(2)]
        w2e = [s.sb(f"w2e{k}", [P, FC, P]) for k in range(2)]
        w2x = [s.sb(f"w2x{k}", [P, FC, P]) for k in range(2)]
        be = [s.sb(f"be{k}", [P, FC + 1]) for k in range(2)]
        bias = s.sb("bias", [P, 3])
        hid = s.sb("hid", [P, 2, T])
        h_ps = [s.ps(f"h_ps{k}", [P, T]) for k in range(2)]
        o_ps = s.ps("o_ps", [P, T])
        M = 3 * FC
        e_loaded = [s.sem(f"e_loaded{k}") for k in range(2)]
        upped = s.count("upped", M, M)
        gelued = s.count("gelued", M, 2)
        downed = s.count("downed", M, M)
        weighed = s.count("weighed", 2, 2)
        biased = s.count("biased", 3, 3)
        added = s.count("added", 1, 1)
        with nc.Block() as block:

            @block.sync
            def _(sp):
                with sp.Fori(0, B) as b:
                    for k in range(2):
                        if k == 0:
                            sp.wait_ge(added.sem, added.before(b, 0, 1))
                        e = sp.value_load(which[0:1, b, k:k + 1], min_val=0, max_val=E - 1)
                        sp.dma_start(w1e[k][:, :], d["w1e"][e]).then_inc(e_loaded[k], 16)
                        sp.dma_start(w2e[k][:, :, :], d["w2e"][e]).then_inc(e_loaded[k], 16)
                        sp.dma_start(be[k][:, :], d["be"][e]).then_inc(e_loaded[k], 16)

            def path(m):
                s_, c = divmod(m, FC)
                return s_, c

            @block.tensor
            def _(pe):
                pe.sem_inc(upped.sem, upped.start)
                pe.sem_inc(downed.sem, downed.start)
                with pe.Fori(0, B) as b:
                    for m in range(M + 1):
                        if m < M:
                            k, c = path(m)
                            if k and c == 0:
                                pe.wait_ge(e_loaded[k - 1], b * 48 + 48)
                            pe.wait_ge(gelued.sem, gelued.before(b, m, 2))
                            w = (w1m if k == 0 else w1e[k - 1])[:, c * P:(c + 1) * P]
                            product(pe, h_ps[m % 2], w, t.z_t[:, b, :]).then_inc(upped.sem, 1)
                        if m >= 1:
                            k, c = path(m - 1)
                            if k and c == 0:
                                pe.wait_ge(weighed.sem, weighed.at(b, k - 1))
                            if m == 1:
                                pe.wait_ge(added.sem, added.before(b, 0, 1))
                            pe.wait_ge(gelued.sem, gelued.at(b, m - 1))
                            w = (w2m if k == 0 else w2x[k - 1])[:, c, :]
                            product(pe, o_ps, w, hid[:, (m - 1) % 2, :], start=m == 1,
                                    stop=m == M).then_inc(downed.sem, 1)

            @block.scalar
            def _(act):
                act.sem_inc(gelued.sem, gelued.start)
                with act.Fori(0, B) as b:
                    for m in range(M):
                        k, c = path(m)
                        act.wait_ge(upped.sem, upped.at(b, m))
                        act.wait_ge(downed.sem, downed.before(b, m, 2))
                        if k and c == 0:
                            act.wait_ge(e_loaded[k - 1], b * 48 + 48)
                        b1 = t.col("b1m", c) if k == 0 else be[k - 1][:, c:c + 1]
                        act.activation(hid[:, m % 2, :], h_ps[m % 2][:, :], ACT.Gelu_apprx_tanh,
                                       bias=b1).then_inc(gelued.sem, 1)

            @block.vector
            def _(dve):
                dve.sem_inc(weighed.sem, weighed.start)
                dve.sem_inc(biased.sem, biased.start)
                dve.sem_inc(added.sem, added.start)
                with dve.Fori(0, B) as b:
                    dve.wait_ge(added.sem, added.before(b, 0, 1))
                    dve.tensor_scalar(bias[:, 0:1], t.col("b2m"), t.blend[:, 0:1], None,
                                      ALU.mult).then_inc(biased.sem, 1)
                    for k in range(2):
                        dve.wait_ge(e_loaded[k], b * 48 + 48)
                        dve.wait_ge(downed.sem, downed.before(b, (k + 2) * FC - 1, M))
                        dve.wait_ge(weighed.sem, weighed.before(b, k, 2))
                        dve.tensor_scalar(w2x[k][:, :, :], w2e[k][:, :, :], share[:, b, k:k + 1], None,
                                          ALU.mult).then_inc(weighed.sem, 1)
                        dve.wait_ge(biased.sem, biased.at(b, k))
                        dve.scalar_tensor_tensor(bias[:, k + 1:k + 2], be[k][:, FC:FC + 1], share[:, b, k:k + 1],
                                                 bias[:, k:k + 1], ALU.mult, ALU.add).then_inc(biased.sem, 1)
                    dve.wait_ge(biased.sem, biased.at(b, 2))
                    dve.wait_ge(downed.sem, downed.at(b, M - 1))
                    dve.scalar_tensor_tensor(t.x_t[:, b, :], o_ps[:, :], bias[:, 2:3], t.x_t[:, b, :], ALU.add,
                                             ALU.add).then_inc(added.sem, 1)


def retention(t):
    nc, d = t.nc, t.dram
    with Stage(nc, "ret") as q:
        mats = q.sb("mats", [P, len(RET_MATS), P])
        w = {n: mats[:, i, :] for i, n in enumerate(RET_MATS)}
        wsv = q.sb("wsv", [P, HD, P])
        head_sum = q.sb("head_sum", [P, HD, P])
        bg_neg = q.sb("bg_neg", [P, 1])
        z_b = q.sb("z_b", [P, T])
        k_sb, q_sb, g_sb = (q.sb(n, [P, T]) for n in ("k_sb", "q_sb", "g_sb"))
        kv = q.sb("kv", [P, 2, T])
        mem = q.sb("mem", [P, 2, T])
        qm = q.sb("qm", [P, 2, T])
        a_ps = q.ps("a_ps", [P, T])
        v_ps = [q.ps(f"v_ps{k}", [P, T]) for k in range(2)]
        h_ps = q.ps("h_ps", [P, T])
        w_loaded, bg_done = q.sem("w_loaded"), q.sem("bg_done")
        z_staged = q.count("z_staged", 1)
        made = q.count("made", 4, 4)
        copied = q.count("copied", 4, 4)
        v_made = q.count("v_made", HD)
        kv_done = q.count("kv_done", HD, 2)
        scanned = q.count("scanned", HD, HD)
        weighed = q.count("weighed", HD, HD)
        summed = q.count("summed", HD, HD)
        h_copied = q.count("h_copied", 1, 1)
        with nc.Block() as block:

            @block.sync
            def _(sp):
                sp.dma_start(mats[:, :, :], d["ret_mats"]).then_inc(w_loaded, 16)
                sp.dma_start(wsv[:, :, :], d["wsv"]).then_inc(w_loaded, 16)
                sp.dma_start(head_sum[:, :, :], d["head_sum"]).then_inc(w_loaded, 16)
                sp.wait_ge(w_loaded, 48)

            @block.tensor
            def _(pe):
                pe.sem_inc(made.sem, made.start)
                pe.sem_inc(summed.sem, summed.start)
                pe.wait_ge(w_loaded, 48)

                def add_column(b, e):
                    pe.wait_ge(weighed.sem, weighed.at(b, e))
                    if e == 0:
                        pe.wait_ge(h_copied.sem, h_copied.before(b, 0, 1))
                    product(pe, h_ps, head_sum[:, e, :], qm[:, e % 2, :], start=e == 0,
                            stop=e == HD - 1).then_inc(summed.sem, 1)

                def value(b, e):
                    pe.wait_ge(kv_done.sem, kv_done.before(b, e, 2))
                    product(pe, v_ps[e % 2], wsv[:, e, :], t.z_t[:, b, :]).then_inc(v_made.sem, 1)

                with pe.Fori(0, B) as b:
                    for i, n in enumerate(("wsk", "wg", "wsq")):
                        pe.wait_ge(copied.sem, copied.before(b, i, 1))
                        product(pe, a_ps, w[n], t.z_t[:, b, :]).then_inc(made.sem, 1)
                        if i < 2:
                            value(b, i)
                    pe.wait_ge(z_staged.sem, z_staged.at(b))
                    pe.wait_ge(copied.sem, copied.before(b, 3, 1))
                    for j in range(TT):
                        last = pe.matmul(a_ps[:, j * P:(j + 1) * P], z_b[:, j * P:(j + 1) * P], w["wv"], start=True,
                                         stop=True)
                    last.then_inc(made.sem, 1)
                    for e in range(2, HD):
                        value(b, e)
                        add_column(b, e - 2)
                    add_column(b, HD - 2)
                    add_column(b, HD - 1)

            @block.scalar
            def _(act):
                act.sem_inc(copied.sem, copied.start)
                act.sem_inc(h_copied.sem, h_copied.start)
                act.wait_ge(bg_done, 1)
                with act.Fori(0, B) as b:
                    act.wait_ge(made.sem, made.before(b, 3, 4))
                    act.activation(z_b[:, :], t.z_t[:, b, :], ACT.Copy).then_inc(z_staged.sem, 1)
                    act.wait_ge(made.sem, made.at(b, 0))
                    act.wait_ge(scanned.sem, scanned.before(b, HD - 1, HD))
                    act.activation(k_sb[:, :], a_ps[:, :], ACT.Identity, bias=t.col("bsk")).then_inc(copied.sem, 1)
                    act.wait_ge(made.sem, made.at(b, 1))
                    act.activation(g_sb[:, :], a_ps[:, :], ACT.Sigmoid, bias=bg_neg[:, 0:1],
                                   scale=-1.0).then_inc(copied.sem, 1)
                    act.wait_ge(made.sem, made.at(b, 2))
                    act.wait_ge(weighed.sem, weighed.before(b, HD - 1, HD))
                    act.activation(q_sb[:, :], a_ps[:, :], ACT.Identity, bias=t.col("bsq")).then_inc(copied.sem, 1)
                    act.wait_ge(made.sem, made.at(b, 3))
                    act.activation(t.v_tok[:, b, :, :].rearrange("p a c -> p (a c)"), a_ps[:, :],
                                   ACT.Copy).then_inc(copied.sem, 1)
                    act.wait_ge(summed.sem, summed.at(b, HD - 1))
                    act.activation(t.h_seq[:, b, :], h_ps[:, :], ACT.Copy).then_inc(h_copied.sem, 1)

            @block.vector
            def _(dve):
                dve.sem_inc(kv_done.sem, kv_done.start)
                dve.sem_inc(scanned.sem, scanned.start)
                dve.tensor_scalar(bg_neg[:, :], t.col("bg"), -1.0, None, ALU.mult).then_inc(bg_done, 1)

                def outer(b, e):
                    dve.wait_ge(v_made.sem, v_made.at(b, e))
                    dve.wait_ge(scanned.sem, scanned.before(b, e, 2))
                    dve.scalar_tensor_tensor(kv[:, e % 2, :], v_ps[e % 2][:, :], t.col("bsv", e), k_sb[:, :],
                                             ALU.add, ALU.mult).then_inc(kv_done.sem, 1)

                with dve.Fori(0, B) as b:
                    dve.wait_ge(copied.sem, copied.at(b, 0))
                    outer(b, 0)
                    dve.wait_ge(copied.sem, copied.at(b, 1))
                    for e in range(HD):
                        if e + 1 < HD:
                            outer(b, e + 1)
                        dve.wait_ge(kv_done.sem, kv_done.at(b, e))
                        dve.wait_ge(weighed.sem, weighed.before(b, e, 2))
                        dve.tensor_tensor_scan(mem[:, e % 2, :], g_sb[:, :], kv[:, e % 2, :], 0.0, ALU.mult,
                                               ALU.add).then_inc(scanned.sem, 1)

            @block.gpsimd
            def _(pool):
                pool.sem_inc(weighed.sem, weighed.start)
                with pool.Fori(0, B) as b:
                    pool.wait_ge(copied.sem, copied.at(b, 2))
                    for e in range(HD):
                        pool.wait_ge(scanned.sem, scanned.at(b, e))
                        pool.wait_ge(summed.sem, summed.before(b, e, 2))
                        pool.tensor_tensor(qm[:, e % 2, :], mem[:, e % 2, :], q_sb[:, :],
                                           ALU.mult).then_inc(weighed.sem, 1)


def queries_and_keys(t, s):
    nc, d = t.nc, t.dram
    t.q_st = s.sb("q_st", [P, G, B, T], F16)
    t.k_st = s.sb("k_st", [P, G, B, T], F16)
    with Stage(nc, "qk") as q:
        mats = q.sb("mats", [P, 2, P])
        rows = q.sb("rows", [P, 2, P])
        temp = q.sb("temp", [P, 4, H])
        h_b = q.sb("h_b", [P, T])
        raw = q.sb("raw", [P, 2, TT, P])
        sq = q.sb("sq", [P, 2, TT, P])
        ss = q.sb("ss", [P, 2, 2, TT * H])
        rn = q.sb("rn", [P, 2, 2, TT * H])
        rt = q.sb("rt", [P, TT * H])
        unit = q.sb("unit", [P, 2, TT, P])
        part = q.sb("part", [P, 2, 2, T], F16)
        tok_ps = [q.ps(f"tok_ps{x}", [P, TT, P]) for x in range(2)]
        u_ps = [q.ps(f"u_ps{x}", [P, T]) for x in range(2)]
        w_loaded, temp_steps = q.sem("w_loaded"), q.sem("temp_steps")
        h_staged = q.count("h_staged", 1)
        made = q.count("made", 2, 2)
        raw_done = q.count("raw_done", 2, 2)
        squared = q.count("squared", 2, 2)
        sums = q.count("sums", 2 * 2, 4)
        rooted = q.count("rooted", 2, 2)
        inverted = q.count("inverted", 2, 2)
        scaled = q.count("scaled", 1, 1)
        unit_done = q.count("unit_done", 2, 2)
        turned = q.count("turned", 2, 2)
        hi_done = q.count("hi_done", 2, 2)
        lo_done = q.count("lo_done", 2, 2)
        sending = q.sem("sending")
        stacked = q.sem("stacked")
        part_free = q.count("part_free", 1, 1)
        MOVES = 2 * 4 * G * 16
        with nc.Block() as block:

            @block.sync
            def _(sp):
                sp.dma_start(mats[:, :, :], d["att_mats"]).then_inc(w_loaded, 16)
                sp.dma_start(rows[:, :, :], d["bqk"]).then_inc(w_loaded, 16)
                sp.sem_inc(part_free.sem, part_free.start)
                with sp.Fori(0, B) as b:
                    for x, stack in enumerate((t.q_st, t.k_st)):
                        sp.wait_ge(lo_done.sem, lo_done.at(b, x))
                        sp.sem_inc(sending, 1)
                        for r in range(4):
                            half = (r % 2, r // 2)[x]
                            for g in range(G):
                                sp.dma_start(stack[32 * r:32 * r + 32, g, b, :], part[32 * g:32 * g + 32, x, half, :]).then_inc(stacked, 16)
                    sp.wait_ge(stacked, (b + 1) * MOVES)
                    sp.sem_inc(part_free.sem, 1)

            @block.tensor
            def _(pe):
                pe.sem_inc(made.sem, made.start)
                pe.sem_inc(turned.sem, turned.start)
                pe.wait_ge(w_loaded, 32)
                with pe.Fori(0, B) as b:
                    pe.wait_ge(h_staged.sem, h_staged.at(b))
                    for x in range(2):
                        pe.wait_ge(raw_done.sem, raw_done.before(b, x, 2))
                        for j in range(TT):
                            last = pe.matmul(tok_ps[x][:, j, :], h_b[:, j * P:(j + 1) * P], mats[:, x, :], start=True,
                                             stop=True)
                        last.then_inc(made.sem, 1)
                    for x in range(2):
                        pe.wait_ge(unit_done.sem, unit_done.at(b, x))
                        pe.wait_ge(lo_done.sem, lo_done.before(b, x, 2))
                        for j in range(TT):
                            last = pe.transpose(u_ps[x][:, j * P:(j + 1) * P], unit[:, x, j, :], t.ident[:, :])
                        last.then_inc(turned.sem, 1)

            @block.scalar
            def _(act):
                act.sem_inc(squared.sem, squared.start)
                act.sem_inc(rooted.sem, rooted.start)
                act.sem_inc(hi_done.sem, hi_done.start)
                act.activation(temp[:, 0, :], t.col("temp", 0, H), ACT.Abs).then_inc(temp_steps, 1)
                act.wait_ge(temp_steps, 1)
                act.activation(temp[:, 1, :], temp[:, 0, :], ACT.Exp, scale=-1.0).then_inc(temp_steps, 1)
                act.wait_ge(temp_steps, 2)
                act.activation(temp[:, 2, :], temp[:, 1, :], ACT.Ln, bias=1.0).then_inc(temp_steps, 1)
                with act.Fori(0, B) as b:
                    act.wait_ge(made.sem, made.before(b, 1, 2))
                    act.activation(h_b[:, :], t.h_seq[:, b, :], ACT.Copy).then_inc(h_staged.sem, 1)
                    for x in range(2):
                        act.wait_ge(raw_done.sem, raw_done.at(b, x))
                        act.wait_ge(sums.sem, sums.before(b, 2 * x, 4))
                        act.activation(sq[:, x, :, :], raw[:, x, :, :], ACT.Square).then_inc(squared.sem, 1)
                    for x in range(2):
                        act.wait_ge(sums.sem, sums.at(b, 2 * x + 1))
                        act.wait_ge(inverted.sem, inverted.before(b, x, 2))
                        act.activation(rn[:, x, 1, :], ss[:, x, 1, :], ACT.Sqrt).then_inc(rooted.sem, 1)
                    for x in range(2):
                        act.wait_ge(turned.sem, turned.at(b, x))
                        act.wait_ge(part_free.sem, part_free.before(b, 0, 1))
                        act.activation(part[:, x, 0, :], u_ps[x][:, :], ACT.Copy).then_inc(hi_done.sem, 1)

            @block.vector
            def _(dve):
                for c in (raw_done, sums, inverted, scaled, unit_done, lo_done):
                    dve.sem_inc(c.sem, c.start)
                dve.wait_ge(temp_steps, 3)
                dve.scalar_tensor_tensor(temp[:, 3, :], t.col("temp", 0, H), 0.0, temp[:, 2, :], ALU.max,
                                         ALU.add).then_inc(temp_steps, 1)
                dve.wait_ge(temp_steps, 4)
                dve.wait_ge(w_loaded, 32)
                heat = temp[:, 3, :].rearrange("p (o h) -> p o h", o=1).broadcast_to([P, TT, H])
                with dve.Fori(0, B) as b:
                    for x in range(2):
                        dve.wait_ge(made.sem, made.at(b, x))
                        dve.wait_ge(squared.sem, squared.before(b, x, 2))
                        dve.wait_ge(unit_done.sem, unit_done.before(b, x, 2))
                        bias = rows[:, x, :].rearrange("p (o c) -> p o c", o=1).broadcast_to([P, TT, P])
                        dve.tensor_tensor(raw[:, x, :, :], tok_ps[x][:, :, :], bias,
                                          ALU.add).then_inc(raw_done.sem, 1)
                    for x in range(2):
                        dve.wait_ge(squared.sem, squared.at(b, x))
                        dve.tensor_reduce(ss[:, x, 0, :],
                                          sq[:, x, :, :].rearrange("p a (h c) -> p (a h) c", c=HD), AX.X,
                                          ALU.add).then_inc(sums.sem, 1)
                        dve.wait_ge(sums.sem, sums.at(b, 2 * x))
                        dve.wait_ge(rooted.sem, rooted.before(b, x, 2))
                        dve.tensor_scalar(ss[:, x, 1, :], ss[:, x, 0, :], 1e-24, None,
                                          ALU.max).then_inc(sums.sem, 1)
                    for x in range(2):
                        dve.wait_ge(rooted.sem, rooted.at(b, x))
                        dve.wait_ge(unit_done.sem, unit_done.before(b, x, 2))
                        dve.reciprocal(rn[:, x, 0, :], rn[:, x, 1, :]).then_inc(inverted.sem, 1)
                    dve.wait_ge(inverted.sem, inverted.at(b, 0))
                    dve.tensor_tensor(rt[:, :].rearrange("p (a h) -> p a h", h=H),
                                      rn[:, 0, 0, :].rearrange("p (a h) -> p a h", h=H), heat,
                                      ALU.mult).then_inc(scaled.sem, 1)
                    dve.wait_ge(scaled.sem, scaled.at(b))
                    for x in range(2):
                        dve.wait_ge(inverted.sem, inverted.at(b, x))
                        dve.wait_ge(turned.sem, turned.before(b, x, 2))
                        factor = (rt[:, :], rn[:, 1, 0, :])[x].rearrange("p (n o) -> p n o", o=1).broadcast_to([P, TT * H, HD])
                        dve.tensor_tensor(unit[:, x, :, :].rearrange("p a (h c) -> p (a h) c", c=HD),
                                          raw[:, x, :, :].rearrange("p a (h c) -> p (a h) c", c=HD), factor,
                                          ALU.mult).then_inc(unit_done.sem, 1)
                    for x in range(2):
                        dve.wait_ge(hi_done.sem, hi_done.at(b, x))
                        dve.tensor_tensor(part[:, x, 1, :], u_ps[x][:, :], part[:, x, 0, :],
                                          ALU.subtract).then_inc(lo_done.sem, 1)


def attention(t, s):
    nc = t.nc
    t.att = t.h_seq
    RING = 4
    with Stage(nc, "att") as q:
        km = q.sb("km", [P, 2, GH, T], F16)
        va = q.sb("va", [P, 2, KC, GH, 32])
        prob = q.sb("prob", [P, RING, GH, HALF])
        o_sb = q.sb("o_sb", [P, T])
        num = q.sb("num", [P, T])
        den = q.sb("den", [P, T])
        rec = q.sb("rec", [P, T])
        s_ps = [q.ps(f"s_ps{k}", [P, 2, HALF]) for k in range(3)]
        o_ps = [q.ps(f"o_ps{k}", [P, HALF]) for k in range(2)]
        U = 2 * KC
        blank = q.sem("blank")
        keyed = q.count("keyed", G, 2)
        scored = q.count("scored", G * U * 2)
        exped = q.count("exped", G * U * 2, 3)
        used = q.count("used", G * U, 2 * U)
        out_done = q.count("out_done", G * 2, 2)
        moved = q.sem("moved")
        recips = q.count("recips", G)
        normed = q.count("normed", G, 1)
        MOVES = 2 * GH * 16
        with nc.Block() as block:

            @block.gpsimd
            def _(pool):
                pool.sem_inc(keyed.sem, keyed.start)
                pool.memset(va[:, :, :, :, HD:32], 1.0).then_inc(blank, 1)
                pool.wait_ge(blank, 1)
                with pool.Fori(0, B) as b:
                    for g in range(G):
                        pool.wait_ge(used.sem, used.before(b, g * U + U - 1, 2 * U))
                        pool.tensor_copy(
                            va[:, g % 2, :, :, 0:HD],
                            t.v_tok[:, b, :, :].rearrange("p k (g j c) -> p g k j c", g=G, c=HD)[:, g, :, :, :])
                        for j in range(GH):
                            last = pool.tensor_tensor(km[:, g % 2, j, :], t.k_st[:, g, b, :],
                                                      t.col("head_mask", j).broadcast_to([P, T]), ALU.mult)
                        last.then_inc(keyed.sem, 1)

            @block.tensor
            def _(pe):
                pe.sem_inc(used.sem, used.start)
                with pe.Fori(0, B) as b:

                    def scores(g, u, pair):
                        half, kc = divmod(u, KC)
                        n = (g * U + u) * 2 + pair
                        pe.wait_ge(exped.sem, exped.before(b, n, 3 if n >= 2 else 2))
                        for i in range(2):
                            j = 2 * pair + i
                            last = pe.matmul(s_ps[n % 3][:, i, :], km[:, g % 2, j, kc * P:(kc + 1) * P],
                                             t.q_st[:, g, b, HALVES[half]], start=True, stop=True)
                        last.then_inc(scored.sem, 1)

                    def values(g, u, pair):
                        half, kc = divmod(u, KC)
                        if kc == 0 and pair == 0:
                            pe.wait_ge(out_done.sem, out_done.before(b, g * 2 + half, 2))
                        pe.wait_ge(exped.sem, exped.at(b, (g * U + u) * 2 + pair))
                        for j in (2 * pair, 2 * pair + 1):
                            last = pe.matmul(o_ps[half][32 * j:32 * j + 32, :], va[:, g % 2, kc, j, :],
                                             prob[:, u % RING, j, :], start=kc == 0, stop=kc == KC - 1)
                        if pair == 1:
                            last.then_inc(used.sem, 1)

                    for g in range(G):
                        pe.wait_ge(keyed.sem, keyed.at(b, g))
                        for u in range(U):
                            for pair in range(2):
                                scores(g, u, pair)
                                if (g, u) >= (0, 2):
                                    values(*divmod(g * U + u - 2, U), pair)
                    for u in (U - 2, U - 1):
                        for pair in range(2):
                            values(G - 1, u, pair)

            @block.scalar
            def _(act):
                act.sem_inc(exped.sem, exped.start)
                with act.Fori(0, B) as b:
                    for g in range(G):
                        for u in range(U):
                            for pair in range(2):
                                n = (g * U + u) * 2 + pair
                                act.wait_ge(scored.sem, scored.at(b, n))
                                if pair == 0:
                                    act.wait_ge(used.sem, used.before(b, g * U + u, RING))
                                act.activation(prob[:, u % RING, 2 * pair:2 * pair + 2, :], s_ps[n % 3][:, :, :],
                                               ACT.Exp).then_inc(exped.sem, 1)

            @block.vector
            def _(dve):
                dve.sem_inc(out_done.sem, out_done.start)
                dve.sem_inc(normed.sem, normed.start)
                with dve.Fori(0, B) as b:
                    for g in range(G):
                        for half in range(2):
                            dve.wait_ge(used.sem, used.at(b, g * U + half * KC + KC - 1))
                            dve.tensor_copy(o_sb[:, HALVES[half]], o_ps[half][:, :]).then_inc(out_done.sem, 1)
                        dve.wait_ge(moved, (b * G + g + 1) * MOVES)
                        mine = slice(32 * g, 32 * g + 32)
                        dve.reciprocal(rec[mine, :], den[mine, :]).then_inc(recips.sem, 1)
                        dve.wait_ge(recips.sem, recips.at(b, g))
                        dve.tensor_tensor(t.att[mine, b, :], num[mine, :], rec[mine, :],
                                          ALU.mult).then_inc(normed.sem, 1)

            @block.sync
            def _(sp):
                with sp.Fori(0, B) as b:
                    for g in range(G):
                        sp.wait_ge(out_done.sem, out_done.at(b, 2 * g + 1))
                        for j in range(GH):
                            for i, to in enumerate((num, den)):
                                at, frm = HD * (GH * g + j), 32 * j + HD * i
                                sp.dma_start(to[at:at + HD, :], o_sb[frm:frm + HD, :]).then_inc(moved, 16)


def attention_output(t):
    nc, d = t.nc, t.dram
    with Stage(nc, "out") as s:
        wo = s.sb("wo", [P, P])
        bias = s.sb("bias", [P, 1])
        b_ps = s.ps("b_ps", [P, 1])
        o_ps = [s.ps(f"o_ps{k}", [P, HALF]) for k in range(2)]
        w_loaded, b_made, b_done = s.sem("w_loaded"), s.sem("b_made"), s.sem("b_done")
        made = s.count("made", 2)
        added = s.count("added", 2, 2)
        with nc.Block() as block:

            @block.sync
            def _(sp):
                sp.dma_start(wo[:, :], d["wo"]).then_inc(w_loaded, 16)

            @block.tensor
            def _(pe):
                pe.wait_ge(w_loaded, 16)
                pe.matmul(b_ps[:, :], wo[:, :], t.col("bv"), start=True, stop=True).then_inc(b_made, 1)
                with pe.Fori(0, B) as b:
                    for k in range(2):
                        pe.wait_ge(added.sem, added.before(b, k, 2))
                        pe.matmul(o_ps[k][:, :], wo[:, :], t.att[:, b, HALVES[k]], start=True,
                                  stop=True).then_inc(made.sem, 1)

            @block.vector
            def _(dve):
                dve.sem_inc(added.sem, added.start)
                dve.wait_ge(b_made, 1)
                dve.tensor_tensor(bias[:, :], b_ps[:, :], t.col("bo"), ALU.add).then_inc(b_done, 1)
                dve.wait_ge(b_done, 1)
                with dve.Fori(0, B) as b:
                    for k in range(2):
                        dve.wait_ge(made.sem, made.at(b, k))
                        dve.scalar_tensor_tensor(t.x_t[:, b, HALVES[k]], o_ps[k][:, :], bias[:, 0:1],
                                                 t.x_t[:, b, HALVES[k]], ALU.add, ALU.add).then_inc(added.sem, 1)


def store(t):
    nc, d = t.nc, t.dram
    with Stage(nc, "store") as s:
        x_half = s.sb("x_half", [P, 2, HALF])
        out = s.sb("out", [P, B, 2, NT, P])
        ps = [s.ps(f"ps{k}", [P, NT, P]) for k in range(2)]
        staged = s.count("staged", 2)
        turned = s.count("turned", 2, 2)
        copied = s.count("copied", 2, 2)
        stored = s.sem("stored")
        with nc.Block() as block:

            @block.scalar
            def _(act):
                with act.Fori(0, B) as b:
                    for k in range(2):
                        act.wait_ge(turned.sem, turned.before(b, k, 2))
                        act.activation(x_half[:, k, :], t.x_t[:, b, HALVES[k]], ACT.Copy).then_inc(staged.sem, 1)

            @block.tensor
            def _(pe):
                pe.sem_inc(turned.sem, turned.start)
                with pe.Fori(0, B) as b:
                    for k in range(2):
                        pe.wait_ge(staged.sem, staged.at(b, k))
                        pe.wait_ge(copied.sem, copied.before(b, k, 2))
                        for j in range(NT):
                            last = pe.transpose(ps[k][:, j, :], x_half[:, k, j * P:(j + 1) * P], t.ident[:, :])
                        last.then_inc(turned.sem, 1)

            @block.vector
            def _(dve):
                dve.sem_inc(copied.sem, copied.start)
                with dve.Fori(0, B) as b:
                    for k in range(2):
                        dve.wait_ge(turned.sem, turned.at(b, k))
                        dve.tensor_copy(out[:, b, k, :, :], ps[k][:, :, :]).then_inc(copied.sem, 1)

            @block.sync
            def _(sp):
                with sp.Fori(0, B) as b:
                    for k in range(2):
                        sp.wait_ge(copied.sem, copied.at(b, k))
                        sp.dma_start(d["out"][b, k], out[:, b, k, :, :]).then_inc(stored, 16)
                sp.wait_ge(stored, 16 * B * 2)


def hybrid_layer(nc, dram):
    t = Layer(nc, dram)
    with Stage(nc, "all") as whole:
        load_constants(t, whole)
        with Stage(nc, "z1") as z:
            with Stage(nc, "ssm") as s:
                scan_buffers(t, s)
                with Stage(nc, "pre") as big:
                    t.z_t = big.sb("z_t", [P, B, T])
                    layernorm(t, "ln1", first=True)
                    scan_inputs(t, big)
                selective_scan(t)
            t.z_t = z.sb("z_t", [P, B, T])
            layernorm(t, "ln2")
            ffn(t, "ffn1")
        with Stage(nc, "attn") as s:
            with Stage(nc, "hv") as hv:
                t.h_seq = hv.sb("h_seq", [P, B, T])
                t.v_tok = hv.sb("v_tok", [P, B, TT, P])
                with Stage(nc, "z3") as z:
                    t.z_t = z.sb("z_t", [P, B, T])
                    layernorm(t, "ln3")
                    retention(t)
                queries_and_keys(t, hv)
                attention(t, hv)
                attention_output(t)
        with Stage(nc, "z4") as z:
            t.z_t = z.sb("z_t", [P, B, T])
            layernorm(t, "ln4")
            ffn(t, "ffn2")
        store(t)


def pack(i):
    a = {k: np.asarray(v) for k, v in i.items()}
    A = lambda n: a["L0_attn_a_" + n]
    R = lambda n: a["L0_attn_b_" + n]
    M = lambda n: a["L0_ffn_" + n]
    cols = {
        "ln_g": A("ln_g"), "ln_b": A("ln_b"), "w1_b": A("w1_b"), "v1_b": A("v1_b"), "w2_b": A("w2_b"),
        "conv": A("conv_w")[:, 0, :], "d_skip": A("D_skip"), "b_dt": A("b_dt"), "a_log": A("A_log"),
        "bsk": R("bsk"), "bsq": R("bsq"), "bg": np.repeat(R("bg"), HD),
        "bsv": np.repeat(R("bsv").reshape(H, HD), HD, axis=0), "bv": R("bv"), "bo": R("bo"),
        "alpha": np.full((P,), M("alpha")), "b1m": M("b1m").reshape(FC, P).T, "b2m": M("b2m"),
        "temp": np.tile(R("temp").reshape(1, H), (P, 1)),
        "head_mask": np.tile(np.repeat(np.eye(GH, dtype=np.float32), HD, axis=0), (P // (GH * HD), 1)),
    }
    vecs = np.concatenate([cols[n].reshape(P, k) for n, k in VEC_SIZES], axis=1)
    bc = np.concatenate([A("W_B"), A("W_C")], axis=1)
    wsv = R("Wsv").T.reshape(P, H, HD)
    head_sum = np.zeros((H, HD, HD, H, HD), np.float32)
    for h in range(H):
        for e in range(HD):
            head_sum[h, :, e, h, e] = 1
    return {
        "x": A("x").reshape(B, 2, NT, P, P).transpose(0, 1, 3, 2, 4),
        "vecs": vecs,
        "ident": np.eye(P, dtype=np.float32),
        "w_gate": M("w_gate"),
        "b_gate": M("b_gate").reshape(1, E),
        "w1m": M("W1m"),
        "w2m": M("W2m").reshape(FC, P, P).transpose(1, 0, 2),
        "ssm_mats": np.stack([A("w1_w"), A("v1_w"), A("w2_w"), A("W_dt")], axis=1),
        "wbc": np.tile(bc, (1, 3)),
        "pick": np.tile(np.eye(2 * NS, dtype=np.float32), (3, 1)),
        "ret_mats": np.stack([R("Wsk").T, R("Wsq").T, np.repeat(R("Wg").T, HD, axis=1), R("Wv").T], axis=1),
        "wsv": np.repeat(wsv.transpose(0, 2, 1)[:, :, :, None], HD, axis=3).reshape(P, HD, P),
        "head_sum": head_sum.reshape(P, HD, P),
        "att_mats": np.stack([R("Wq").T, R("Wk").T], axis=1),
        "bqk": np.tile(np.stack([R("bq"), R("bk")])[None], (P, 1, 1)),
        "wo": R("Wo").T,
        "w1e": M("W1e"),
        "w2e": M("W2e").reshape(E, FC, P, P).transpose(0, 2, 1, 3),
        "be": np.concatenate([M("b1e").reshape(E, FC, P).transpose(0, 2, 1), M("b2e").reshape(E, P, 1)], axis=2),
    }


def program(nc, arrays):
    dram = {n: nc.dram_tensor("in_" + n, a.shape, F32, kind="ExternalInput").ap() for n, a in arrays.items()}
    out = nc.dram_tensor("out", (B, 2, NT, P, P), F32, kind="ExternalOutput").ap()
    dram["out"] = out.rearrange("b k j p c -> b k p j c")
    hybrid_layer(nc, dram)


def kernel(**inputs):
    import concourse.bacc as bacc
    from concourse.bass_utils import run_bass_kernel_spmd

    arrays = {n: np.ascontiguousarray(a) for n, a in pack(inputs).items()}
    nc = bacc.Bacc("TRN2", target_bir_lowering=False, num_devices=1)
    program(nc, arrays)
    r = run_bass_kernel_spmd(nc, [{"in_" + n: a for n, a in arrays.items()}], core_ids=[0])
    return r.results[0]["out"].reshape(B, T, P)
```

```python
from contextlib import ExitStack

import numpy as np

import concourse.bass as bass
from concourse import mybir

ALU = mybir.AluOpType
ACT = mybir.ActivationFunctionType
AX = mybir.AxisListType
F32 = mybir.dt.float32
F16 = mybir.dt.float16
BF16 = mybir.dt.bfloat16
U32 = mybir.dt.uint32

P = 128
B, T = 4, 1024
HALF = 512
HALVES = (slice(0, HALF), slice(HALF, T))
NT = HALF // P
TT = T // P
NS = 16
H, HD = 16, 8
E, F = 8, 512
FC = F // P
G = 4
GH = H // G
KC = T // P
EPS = 1e-5
COLUMNS = (0, 2, 4, 6, 1, 3, 5, 7)
WS = 64.0
BC3 = 3 * 2 * NS

VEC_SIZES = (("ln_g", 1), ("ln_b", 1), ("w1_b", 1), ("v1_b", 1), ("w2_b", 1), ("conv", 3), ("d_skip", 1),
             ("b_dt", 1), ("a_log", NS), ("bsk", 1), ("bsq", 1), ("bg", 1), ("bsv", HD), ("bv", 1), ("bo", 1),
             ("alpha", 1), ("b1m", FC), ("b2m", 1), ("temp", H), ("head_mask", GH))
VEC = {}
NV = 0
for _name, _n in VEC_SIZES:
    VEC[_name] = NV
    NV += _n

SSM_MATS = ("w1", "v1", "w2", "wdt")
RET_MATS = ("wsk", "wsq", "wg", "wv")
ATT_MATS = ("wq", "wk")


class Count:
    def __init__(self, sem, per=1, start=0):
        self.sem, self.per, self.start = sem, per, start

    def at(self, i, n=0):
        return i * self.per + (self.start + n + 1)

    def before(self, i, n, k):
        assert self.start >= k
        return i * self.per + (self.start + n + 1 - k)


class Stage:

    def __init__(self, nc, name):
        self.nc, self.name, self.ctx = nc, name, ExitStack()

    def __enter__(self):
        return self

    def __exit__(self, *a):
        return self.ctx.__exit__(*a)

    def sb(self, name, shape, dt=F32):
        return self.ctx.enter_context(self.nc.sbuf_tensor(f"{self.name}_{name}", shape, dt))

    def ps(self, name, shape, dt=F32):
        return self.ctx.enter_context(self.nc.psum_tensor(f"{self.name}_{name}", shape, dt))

    def sem(self, name):
        return self.ctx.enter_context(self.nc.semaphore(f"{self.name}_{name}"))

    def count(self, name, per=1, start=0):
        return Count(self.sem(name), per, start)


class Layer:

    def __init__(self, nc, dram):
        self.nc, self.dram = nc, dram

    def col(self, name, k=0, n=1):
        return self.vec[:, VEC[name] + k:VEC[name] + k + n]


def load_constants(t, whole):
    nc, d = t.nc, t.dram
    t.x_t = whole.sb("x_t", [P, B, T])
    t.z_sum = whole.sb("z_sum", [P, B, 2])
    t.vec = whole.sb("vec", [P, NV])
    t.ident = whole.sb("ident", [P, P])
    t.minus_half = whole.sb("minus_half", [P, P])
    t.eps = whole.sb("eps", [P, NT])
    t.blend = whole.sb("blend", [P, 3])
    t.w_gate = whole.sb("w_gate", [P, E])
    t.b_gate = whole.sb("b_gate", [1, E])
    t.ones_row = whole.sb("ones_row", [1, P])
    with Stage(nc, "load") as s:
        loaded, clipped = s.sem("loaded"), s.sem("clipped")
        with nc.Block() as block:

            @block.sync
            def _(sp):
                for dst, src in ((t.vec, d["vecs"]), (t.ident, d["ident"]), (t.w_gate, d["w_gate"]),
                                 (t.b_gate, d["b_gate"])):
                    sp.dma_start(dst[:, :], src).then_inc(loaded, 16)
                sp.wait_ge(loaded, 16 * 4)

            @block.vector
            def _(dve):
                dve.memset(t.minus_half[:, :], -0.5)
                dve.memset(t.eps[:, :], EPS)
                dve.memset(t.ones_row[:, :], 1.0)
                dve.wait_ge(loaded, 16 * 4)
                dve.tensor_scalar(t.blend[:, 0:1], t.col("alpha"), 0.1, 1.0, ALU.max, ALU.min).then_inc(clipped, 1)
                dve.wait_ge(clipped, 1)
                dve.tensor_scalar(t.blend[:, 1:2], t.blend[:, 0:1], -1.0, 1.0, ALU.mult, ALU.add)
                dve.tensor_scalar(t.blend[:, 2:3], t.blend[:, 0:1], WS, None, ALU.mult)


def layernorm(t, name, first=False, split=False):
    nc, d = t.nc, t.dram
    with Stage(nc, name) as s:
        x_half = s.sb("x_half", [P, 2, HALF])
        x_in = s.sb("x_in", [P, 2, HALF])
        stats = s.sb("stats", [P, 2, NT, 6])
        mv = s.sb("mv", [P, 2, NT, 2])
        rstd = s.sb("rstd", [P, 2, NT])
        rtmp = s.sb("rtmp", [P, 2, 5, NT])
        z_tok = s.sb("z_tok", [P, 2, NT, P])
        tok_ps = [s.ps(f"tok_ps{k}", [P, NT, P]) for k in range(2)]
        z_ps = [s.ps(f"z_ps{k}", [P, HALF]) for k in range(2)]
        x_loaded = [s.sem(f"x_loaded{k}") for k in range(2)] if first else None
        RS = 7 if first else 2
        x_staged = s.count("x_staged", 2, 2)
        turned = s.count("turned", 2, 2)
        kept = s.count("kept", 2, 2) if first else None
        got_mv = s.count("got_mv", 2 * NT)
        rstd_steps = s.count("rstd_steps", 2 * RS)
        normed = s.count("normed", 2 * NT, 2 * NT)
        z_turned = s.count("z_turned", 2, 2)
        z_copied = s.count("z_copied", 2, 2)
        z_rest = s.count("z_rest", 2, 2) if split else None
        with nc.Block() as block:

            if first:
                @block.sync
                def _(sp):
                    with sp.Fori(0, B) as b:
                        for k in range(2):
                            sp.wait_ge(x_staged.sem, x_staged.before(b, k, 2))
                            sp.dma_start(x_in[:, k, :], d["x"][b, k]).then_inc(x_loaded[k], 16)

            @block.tensor
            def _(pe):
                pe.sem_inc(turned.sem, turned.start)
                pe.sem_inc(z_turned.sem, z_turned.start)
                def body(b, n):
                    k = n % 2
                    if there(b, n, 2):
                        pe.wait_ge(x_staged.sem, x_staged.at(b, n))
                        if first:
                            pe.wait_ge(kept.sem, kept.before(b, n, 2))
                        pe.wait_ge(normed.sem, normed.before(b, n * NT + NT - 1, 2 * NT))
                        for j in range(NT):
                            last = pe.transpose(tok_ps[k][:, j, :], x_half[:, k, j * P:(j + 1) * P], t.ident[:, :])
                        last.then_inc(turned.sem, 1)
                    if n >= 2:
                        pe.wait_ge(normed.sem, normed.at(b, k * NT + NT - 1))
                        z_read = z_rest if split else z_copied
                        pe.wait_ge(z_read.sem, z_read.before(b, k, 2))
                        for j in range(NT):
                            last = pe.transpose(z_ps[k][:, j * P:(j + 1) * P], z_tok[:, k, j, :], t.ident[:, :])
                        last.then_inc(z_turned.sem, 1)

                pipelined(pe, 2, 2, body)

            @block.vector
            def _(dve):
                dve.sem_inc(normed.sem, normed.start)
                if split:
                    dve.sem_inc(z_rest.sem, z_rest.start)

                def statistics(b):
                    for k in range(2):
                        if first:
                            dve.wait_ge(x_staged.sem, x_staged.at(b, k))
                        else:
                            dve.wait_ge(turned.sem, turned.at(b, k))
                        dve.wait_ge(normed.sem, normed.before(b, k * NT + NT - 1, 2 * NT))
                        for j in range(NT):
                            src = x_half[:, k, j * P:(j + 1) * P] if first else tok_ps[k][:, j, :]
                            dve.bn_stats(stats[:, k, j, :], src)
                        dve.drain()
                        for j in range(NT):
                            dve.bn_aggr(mv[:, k, j, :], stats[:, k, j, :]).then_inc(got_mv.sem, 1)

                def normalise(b):
                    for k in range(2):
                        dve.wait_ge(rstd_steps.sem, rstd_steps.at(b, k * RS + RS - 1))
                        dve.wait_ge(z_turned.sem, z_turned.before(b, k, 2))
                        for j in range(NT):
                            src = x_half[:, k, j * P:(j + 1) * P] if first else tok_ps[k][:, j, :]
                            dve.tensor_scalar(z_tok[:, k, j, :], src, mv[:, k, j, 0:1], rstd[:, k, j:j + 1],
                                              ALU.subtract, ALU.mult).then_inc(normed.sem, 1)

                def low_part(b):
                    for k in range(2 if split else 0):
                        dve.wait_ge(z_copied.sem, z_copied.at(b, k))
                        dve.tensor_tensor(t.z_lo[:, b, HALVES[k]], z_ps[k][:, :], t.z_hi[:, b, HALVES[k]],
                                          ALU.subtract).then_inc(z_rest.sem, 1)

                statistics(0)
                normalise(0)
                with dve.Fori(0, B - 1) as b:
                    statistics(b + 1)
                    low_part(b)
                    normalise(b + 1)
                low_part(B - 1)

            @block.gpsimd
            def _(pool):
                half, eps = t.minus_half[:, 0:NT], t.eps[:, :]
                with pool.Fori(0, B) as b:
                    for k in range(2):
                        var = mv[:, k, :, 1]
                        veps, r1, v1, v2, v3 = (rtmp[:, k, i, :] for i in range(5))
                        pool.wait_ge(got_mv.sem, got_mv.at(b, k * NT + NT - 1))
                        pool.wait_ge(normed.sem, normed.before(b, k * NT + NT - 1, 2 * NT))
                        pool.tensor_tensor(veps, var, eps, ALU.add).then_inc(rstd_steps.sem, 1)
                        pool.wait_ge(rstd_steps.sem, rstd_steps.at(b, k * RS))
                        if not first:
                            pool.tensor_tensor(rstd[:, k, :], veps, half, ALU.pow).then_inc(rstd_steps.sem, 1)
                            continue
                        pool.tensor_tensor(r1, veps, half, ALU.pow).then_inc(rstd_steps.sem, 1)
                        pool.wait_ge(rstd_steps.sem, rstd_steps.at(b, k * RS + 1))
                        pool.tensor_tensor(v1, var, r1, ALU.mult).then_inc(rstd_steps.sem, 1)
                        pool.wait_ge(rstd_steps.sem, rstd_steps.at(b, k * RS + 2))
                        pool.tensor_tensor(v2, v1, r1, ALU.mult).then_inc(rstd_steps.sem, 1)
                        pool.wait_ge(rstd_steps.sem, rstd_steps.at(b, k * RS + 3))
                        pool.tensor_tensor(v3, v2, eps, ALU.add).then_inc(rstd_steps.sem, 1)
                        pool.wait_ge(rstd_steps.sem, rstd_steps.at(b, k * RS + 4))
                        pool.tensor_tensor(v1, v3, half, ALU.pow).then_inc(rstd_steps.sem, 1)
                        pool.wait_ge(rstd_steps.sem, rstd_steps.at(b, k * RS + 5))
                        pool.tensor_tensor(rstd[:, k, :], v1, r1, ALU.mult).then_inc(rstd_steps.sem, 1)

            @block.scalar
            def _(act):
                if first:
                    act.sem_inc(kept.sem, kept.start)
                act.sem_inc(z_copied.sem, z_copied.start)
                act.sem_inc(x_staged.sem, x_staged.start)

                def body(b, n):
                    k, at = n % 2, b + n // 2
                    if there(b, n, 2):
                        act.wait_ge(turned.sem, turned.before(b, n, 2))
                        if first:
                            act.wait_ge(normed.sem, normed.before(b, n * NT + NT - 1, 2 * NT))
                            act.wait_ge(x_loaded[k], at * 16 + 16)
                        act.activation(x_half[:, k, :], x_in[:, k, :] if first else t.x_t[:, at, HALVES[k]],
                                       ACT.Copy).then_inc(x_staged.sem, 1)
                        if first:
                            act.wait_ge(turned.sem, turned.at(b, n))
                            act.activation(t.x_t[:, at, HALVES[k]], tok_ps[k][:, :, :].rearrange("p a c -> p (a c)"),
                                           ACT.Copy).then_inc(kept.sem, 1)
                    if n >= 2:
                        act.wait_ge(z_turned.sem, z_turned.at(b, k))
                        if first:
                            act.activation(t.z_t[:, b, HALVES[k]], z_ps[k][:, :], ACT.Identity, bias=t.col("ln_b"),
                                           scale=t.col("ln_g")).then_inc(z_copied.sem, 1)
                        elif split:
                            act.activation(t.z_hi[:, b, HALVES[k]], z_ps[k][:, :], ACT.Copy,
                                           accum_out=t.z_sum[:, b, k:k + 1]).then_inc(z_copied.sem, 1)
                        else:
                            act.activation(t.z_t[:, b, HALVES[k]], z_ps[k][:, :],
                                           ACT.Copy).then_inc(z_copied.sem, 1)

                pipelined(act, 2, 2, body)


def product(pe, out, w, rhs, start=True, stop=True):
    for h in HALVES:
        last = pe.matmul(out[:, h], w, rhs[:, h], start=start, stop=stop)
    return last


def product_of_parts(pe, out, w_hi, w_lo, x_hi, x_lo, start=True, stop=True):
    parts = ((w_hi, x_hi), (w_hi, x_lo), (w_lo, x_hi))
    for i, (w, x) in enumerate(parts):
        for h in HALVES:
            last = pe.matmul(out[:, h], w, x[:, h], start=start and i == 0, stop=stop and i == len(parts) - 1)
    return last


def scan_buffers(t, s):
    t.ssm_mats = s.sb("mats", [P, len(SSM_MATS), P])
    t.ssm_w = {n: t.ssm_mats[:, i, :] for i, n in enumerate(SSM_MATS)}
    t.u_t, t.v_t, t.dt_t, t.du_t = (s.sb(n, [P, B, T]) for n in ("u_t", "v_t", "dt_t", "du_t"))
    t.bc = s.sb("bc", [BC3, B, T], BF16)
    t.sel = s.sb("sel", [BC3, 2 * NS, P], BF16)


def scan_inputs(t, big):
    nc, d = t.nc, t.dram
    mats = t.ssm_mats
    wbc = big.sb("wbc", [P, BC3])
    pick = big.sb("pick", [BC3, 2 * NS])
    x1 = big.sb("x1", [P, T + 2])
    y0, y1, y2 = (big.sb(n, [P, T]) for n in ("y0", "y1", "y2"))
    w_ready, wbc_ready = big.sem("w_ready"), big.sem("wbc_ready")
    with Stage(nc, "conv") as q:
        x1_ps, v_ps = q.ps("x1_ps", [P, T]), q.ps("v_ps", [P, T])
        padded = q.sem("padded")
        x1_made, v_made = q.count("x1_made"), q.count("v_made")
        x1_copied, v_silu = q.count("x1_copied", 1, 1), q.count("v_silu", 1, 1)
        conv_steps = q.count("conv_steps", 3, 3)
        u_made = q.count("u_made", 1, 1)
        with nc.Block() as block:

            @block.sync
            def _(sp):
                sp.dma_start(mats[:, :, :], d["ssm_mats"]).then_inc(w_ready, 16)
                sp.dma_start(wbc[:, :], d["wbc"]).then_inc(wbc_ready, 16)
                sp.dma_start(pick[:, :], d["pick"]).then_inc(wbc_ready, 16)
                sp.wait_ge(w_ready, 16)
                sp.wait_ge(wbc_ready, 32)

            @block.tensor
            def _(pe):
                pe.wait_ge(w_ready, 16)
                with pe.Fori(0, B) as b:
                    pe.wait_ge(x1_copied.sem, x1_copied.before(b, 0, 1))
                    product(pe, x1_ps, t.ssm_w["w1"], t.z_t[:, b, :]).then_inc(x1_made.sem, 1)
                    pe.wait_ge(v_silu.sem, v_silu.before(b, 0, 1))
                    product(pe, v_ps, t.ssm_w["v1"], t.z_t[:, b, :]).then_inc(v_made.sem, 1)

            @block.scalar
            def _(act):
                act.sem_inc(x1_copied.sem, 1)
                act.sem_inc(v_silu.sem, 1)
                act.sem_inc(u_made.sem, 1)
                with act.Fori(0, B) as b:
                    act.wait_ge(x1_made.sem, x1_made.at(b))
                    act.wait_ge(conv_steps.sem, conv_steps.before(b, 2, 3))
                    act.activation(x1[:, 1:T + 1], x1_ps[:, :], ACT.Identity,
                                   bias=t.col("w1_b")).then_inc(x1_copied.sem, 1)
                    act.wait_ge(v_made.sem, v_made.at(b))
                    act.activation(t.v_t[:, b, :], v_ps[:, :], ACT.Silu, bias=t.col("v1_b")).then_inc(v_silu.sem, 1)
                    act.wait_ge(conv_steps.sem, conv_steps.at(b, 2))
                    act.activation(t.u_t[:, b, :], y2[:, :], ACT.Silu).then_inc(u_made.sem, 1)

            @block.vector
            def _(dve):
                dve.sem_inc(conv_steps.sem, 3)
                dve.memset(x1[:, 0:1], 0.0)
                dve.memset(x1[:, T + 1:T + 2], 0.0).then_inc(padded, 1)
                dve.wait_ge(padded, 1)
                with dve.Fori(0, B) as b:
                    dve.wait_ge(x1_copied.sem, x1_copied.at(b))
                    dve.tensor_scalar(y0[:, :], x1[:, 0:T], t.col("conv", 0), None,
                                      ALU.mult).then_inc(conv_steps.sem, 1)
                    dve.wait_ge(conv_steps.sem, conv_steps.at(b, 0))
                    dve.scalar_tensor_tensor(y1[:, :], x1[:, 1:T + 1], t.col("conv", 1), y0[:, :], ALU.mult,
                                             ALU.add).then_inc(conv_steps.sem, 1)
                    dve.wait_ge(conv_steps.sem, conv_steps.at(b, 1))
                    dve.wait_ge(u_made.sem, u_made.before(b, 0, 1))
                    dve.scalar_tensor_tensor(y2[:, :], x1[:, 2:T + 2], t.col("conv", 2), y1[:, :], ALU.mult,
                                             ALU.add).then_inc(conv_steps.sem, 1)
                dve.wait_ge(wbc_ready, 32)
                dve.tensor_copy(t.sel[:, :, :],
                                pick[:, :].rearrange("p (n o) -> p n o", o=1).broadcast_to([BC3, 2 * NS, P]))

    with Stage(nc, "dt") as q:
        dt_ps, bc_ps = q.ps("dt_ps", [P, T]), q.ps("bc_ps", [P, T])
        hi, mid = q.sb("hi", [BC3, T], BF16), q.sb("mid", [BC3, T], BF16)
        rest = q.sb("rest", [BC3, T])
        dt_made, bc_made = q.count("dt_made"), q.count("bc_made")
        soft_steps = q.count("soft_steps", 4, 4)
        dt_done = q.count("dt_done", 1, 1)
        split_steps = q.count("split_steps", 6, 6)
        with nc.Block() as block:

            @block.tensor
            def _(pe):
                with pe.Fori(0, B) as b:
                    pe.wait_ge(soft_steps.sem, soft_steps.before(b, 0, 4))
                    product(pe, dt_ps, t.ssm_w["wdt"], t.u_t[:, b, :]).then_inc(dt_made.sem, 1)
                    pe.wait_ge(split_steps.sem, split_steps.before(b, 5, 6))
                    product(pe, bc_ps[0:BC3, :], wbc[:, :], t.u_t[:, b, :]).then_inc(bc_made.sem, 1)

            @block.scalar
            def _(act):
                act.sem_inc(soft_steps.sem, soft_steps.start)
                with act.Fori(0, B) as b:
                    act.wait_ge(dt_made.sem, dt_made.at(b))
                    act.wait_ge(dt_done.sem, dt_done.before(b, 0, 1))
                    act.activation(x1[:, 0:T], dt_ps[:, :], ACT.Identity,
                                   bias=t.col("b_dt")).then_inc(soft_steps.sem, 1)
                    act.wait_ge(soft_steps.sem, soft_steps.at(b, 0))
                    act.activation(y0[:, :], x1[:, 0:T], ACT.Abs).then_inc(soft_steps.sem, 1)
                    act.wait_ge(soft_steps.sem, soft_steps.at(b, 1))
                    act.activation(y1[:, :], y0[:, :], ACT.Exp, scale=-1.0).then_inc(soft_steps.sem, 1)
                    act.wait_ge(soft_steps.sem, soft_steps.at(b, 2))
                    act.activation(y2[:, :], y1[:, :], ACT.Ln, bias=1.0).then_inc(soft_steps.sem, 1)

            @block.vector
            def _(dve):
                dve.sem_inc(dt_done.sem, 1)
                dve.sem_inc(split_steps.sem, 6)
                with dve.Fori(0, B) as b:
                    dve.wait_ge(bc_made.sem, bc_made.at(b))
                    dve.tensor_copy(hi[:, :], bc_ps[0:BC3, :]).then_inc(split_steps.sem, 1)
                    dve.wait_ge(split_steps.sem, split_steps.at(b, 0))
                    dve.tensor_tensor(rest[:, :], bc_ps[0:BC3, :], hi[:, :], ALU.subtract).then_inc(split_steps.sem, 1)
                    dve.wait_ge(split_steps.sem, split_steps.at(b, 1))
                    dve.tensor_copy(mid[:, :], rest[:, :]).then_inc(split_steps.sem, 1)
                    dve.wait_ge(split_steps.sem, split_steps.at(b, 2))
                    dve.tensor_tensor(t.bc[:, b, :], rest[:, :], mid[:, :], ALU.subtract).then_inc(split_steps.sem, 1)
                    dve.wait_ge(split_steps.sem, split_steps.at(b, 3))
                    dve.tensor_scalar(t.bc[0:32, b, :], hi[0:32, :], 1.0, None, ALU.mult).then_inc(split_steps.sem, 1)
                    dve.tensor_scalar(t.bc[32:64, b, :], mid[32:64, :], 1.0, None, ALU.mult).then_inc(split_steps.sem, 1)
                    dve.wait_ge(split_steps.sem, split_steps.at(b, 5))
                    dve.wait_ge(soft_steps.sem, soft_steps.at(b, 3))
                    dve.scalar_tensor_tensor(t.dt_t[:, b, :], x1[:, 0:T], 0.0, y2[:, :], ALU.max,
                                             ALU.add).then_inc(dt_done.sem, 1)

            @block.gpsimd
            def _(pool):
                with pool.Fori(0, B) as b:
                    pool.wait_ge(dt_done.sem, dt_done.at(b))
                    pool.tensor_tensor(t.du_t[:, b, :], t.dt_t[:, b, :], t.u_t[:, b, :], ALU.mult)


def pipelined(eng, first, per, body):
    for n in range(first):
        body(0, n)
    with eng.Fori(0, B - 1) as b:
        for n in range(first, first + per):
            body(b, n)
    for n in range(first, first + per):
        body(B - 1, n)


def there(b, n, per):
    return n < per or not isinstance(b, int) or b < B - 1


def selective_scan(t):
    nc = t.nc
    LAG = 3
    TAIL = NS + LAG + 1
    with Stage(nc, "scan") as s:
        a_neg = s.sb("a_neg", [P, NS])
        dt_b = s.sb("dt_b", [P, T])
        decay = s.sb("decay", [P, 2, T])
        drive = s.sb("drive", [P, 2, T])
        state = s.sb("state", [P, 2, T])
        c_rep = s.sb("c_rep", [P, 2, T])
        hc = s.sb("hc", [P, 4, T])
        y_sb = s.sb("y_sb", [P, T])
        yv = s.sb("yv", [P, T])
        b_ps = [s.ps(f"b_ps{k}", [P, T]) for k in range(2)]
        c_ps, y_ps = (s.ps(n, [P, T]) for n in ("c_ps", "y_ps"))
        a_steps = s.sem("a_steps")
        b_spread = s.count("b_spread", NS)
        c_spread = s.count("c_spread", NS)
        summed = s.count("summed", NS, 4)
        dt_staged = s.count("dt_staged")
        decayed = s.count("decayed", NS, 1)
        c_copied = s.count("c_copied", NS, 1)
        driven = s.count("driven", NS, 2)
        scanned = s.count("scanned", NS, 2)
        weighed = s.count("weighed", NS, 2)
        y_steps = s.count("y_steps", 2, 2)
        projected = s.count("projected", 1, 1)
        added = s.count("added", 1, 1)
        with nc.Block() as block:

            @block.tensor
            def _(pe):
                pe.sem_inc(summed.sem, summed.start)
                pe.sem_inc(projected.sem, projected.start)

                def body(b, n):
                    if there(b, n, NS):
                        at, m = b + n // NS, n % NS
                        pe.wait_ge(driven.sem, driven.before(b, n, 2))
                        if n == TAIL + 1:
                            pe.wait_ge(added.sem, added.at(b))
                        product(pe, b_ps[n % 2], t.sel[:, m, :], t.bc[:, at, :]).then_inc(b_spread.sem, 1)
                        pe.wait_ge(c_copied.sem, c_copied.before(b, n, 1))
                        product(pe, c_ps, t.sel[:, NS + m, :], t.bc[:, at, :]).then_inc(c_spread.sem, 1)
                    k = n - LAG
                    if k >= 0 and there(b, k, NS):
                        pe.wait_ge(weighed.sem, weighed.at(b, k))
                        if k % NS == 0:
                            pe.wait_ge(y_steps.sem, y_steps.before(b, 2 * (k // NS), 2))
                        product(pe, y_ps, t.ident[:, :], hc[:, k % 4, :], start=k % NS == 0,
                                stop=k % NS == NS - 1).then_inc(summed.sem, 1)
                    if n == TAIL:
                        pe.wait_ge(y_steps.sem, y_steps.at(b, 1))
                        if there(b, n, NS):
                            pe.wait_ge(driven.sem, driven.at(b, n - 1))
                        product(pe, b_ps[(TAIL + 1) % 2], t.ssm_w["w2"], yv[:, :]).then_inc(projected.sem, 1)

                pipelined(pe, TAIL + 2 - NS, NS, body)

            @block.scalar
            def _(act):
                act.sem_inc(c_copied.sem, c_copied.start)
                act.activation(a_neg[:, :], t.col("a_log", 0, NS), ACT.Exp).then_inc(a_steps, 1)
                act.wait_ge(a_steps, 1)
                act.mul(a_neg[:, :], a_neg[:, :], -1.0).then_inc(a_steps, 1)
                act.wait_ge(a_steps, 2)
                act.sem_inc(decayed.sem, decayed.start)
                with act.Fori(0, B) as b:
                    act.wait_ge(decayed.sem, decayed.before(b, 0, 1))
                    act.activation(dt_b[:, :], t.dt_t[:, b, :], ACT.Copy).then_inc(dt_staged.sem, 1)
                    act.wait_ge(dt_staged.sem, dt_staged.at(b))
                    for n in range(NS):
                        act.wait_ge(scanned.sem, scanned.before(b, n, 2))
                        act.activation(decay[:, n % 2, :], dt_b[:, :], ACT.Exp,
                                       scale=a_neg[:, n:n + 1]).then_inc(decayed.sem, 1)
                        act.wait_ge(c_spread.sem, c_spread.at(b, n))
                        act.wait_ge(weighed.sem, weighed.before(b, n, 2))
                        act.activation(c_rep[:, n % 2, :], c_ps[:, :], ACT.Copy).then_inc(c_copied.sem, 1)

            @block.vector
            def _(dve):
                dve.sem_inc(driven.sem, driven.start)
                dve.sem_inc(scanned.sem, scanned.start)
                dve.sem_inc(y_steps.sem, y_steps.start)
                dve.sem_inc(added.sem, added.start)

                def body(b, n):
                    if there(b, n, NS):
                        dve.wait_ge(b_spread.sem, b_spread.at(b, n))
                        dve.wait_ge(scanned.sem, scanned.before(b, n, 2))
                        dve.tensor_tensor(drive[:, n % 2, :], b_ps[n % 2][:, :], t.du_t[:, b + n // NS, :],
                                          ALU.mult).then_inc(driven.sem, 1)
                    k = n - 1
                    if k >= 0 and there(b, k, NS):
                        dve.wait_ge(driven.sem, driven.at(b, k))
                        dve.wait_ge(decayed.sem, decayed.at(b, k))
                        dve.wait_ge(weighed.sem, weighed.before(b, k, 2))
                        dve.tensor_tensor_scan(state[:, k % 2, :], decay[:, k % 2, :], drive[:, k % 2, :], 0.0,
                                               ALU.mult, ALU.add).then_inc(scanned.sem, 1)
                    if n == TAIL - 1:
                        dve.wait_ge(summed.sem, summed.at(b, NS - 1))
                        dve.scalar_tensor_tensor(y_sb[:, :], t.u_t[:, b, :], t.col("d_skip"), y_ps[:, :], ALU.mult,
                                                 ALU.add).then_inc(y_steps.sem, 1)
                        dve.wait_ge(y_steps.sem, y_steps.at(b, 0))
                        dve.wait_ge(projected.sem, projected.before(b, 0, 1))
                        dve.tensor_tensor(yv[:, :], y_sb[:, :], t.v_t[:, b, :], ALU.mult).then_inc(y_steps.sem, 1)
                    if n == TAIL:
                        dve.wait_ge(projected.sem, projected.at(b))
                        dve.scalar_tensor_tensor(t.x_t[:, b, :], b_ps[(TAIL + 1) % 2][:, :], t.col("w2_b"),
                                                 t.x_t[:, b, :], ALU.add, ALU.add).then_inc(added.sem, 1)

                pipelined(dve, TAIL + 2 - NS, NS, body)

            @block.gpsimd
            def _(pool):
                pool.sem_inc(weighed.sem, weighed.start)
                with pool.Fori(0, B) as b:
                    for n in range(NS):
                        pool.wait_ge(scanned.sem, scanned.at(b, n))
                        pool.wait_ge(c_copied.sem, c_copied.at(b, n))
                        pool.wait_ge(summed.sem, summed.before(b, n, 4))
                        pool.tensor_tensor(hc[:, n % 4, :], state[:, n % 2, :], c_rep[:, n % 2, :],
                                           ALU.mult).then_inc(weighed.sem, 1)


def ffn(t, name):
    nc, d = t.nc, t.dram
    with Stage(nc, name) as s:
        w1m = s.sb("w1m", [P, F])
        w2m = s.sb("w2m", [P, FC * P])
        w1p = [[s.sb(f"w1p{k}{i}", [P, F], F16) for i in range(2)] for k in range(3)]
        w2p = [[s.sb(f"w2p{k}{i}", [P, FC * P], F16) for i in range(2)] for k in range(3)]
        logits = s.sb("logits", [1, B, E])
        best = s.sb("best", [1, B, 8])
        which = s.sb("which", [1, B, 8], U32)
        gap = s.sb("gap", [1, B])
        th = s.sb("th", [1, B])
        share_row = s.sb("share_row", [1, B, 2])
        share = s.sb("share", [P, B, 2])
        m_loaded, m_steps = s.sem("m_loaded"), s.sem("m_steps")
        with Stage(nc, name + "_gate") as q:
            gate_ps = q.ps("gate_ps", [1, B, E])
            share_ps = q.ps("share_ps", [P, 2 * B])
            scored, picked, spread = q.sem("scored"), q.sem("picked"), q.sem("spread")
            tanh_done = q.sem("tanh_done")
            with nc.Block() as block:

                @block.sync
                def _(sp):
                    sp.dma_start(w1m[:, :], d["w1m"]).then_inc(m_loaded, 16)
                    sp.dma_start(w2m[:, :], d["w2m"]).then_inc(m_loaded, 16)
                    sp.wait_ge(m_loaded, 32)

                @block.tensor
                def _(pe):
                    for b in range(B):
                        for k in range(2):
                            last = pe.matmul(gate_ps[:, b, :], t.z_sum[:, b, k:k + 1], t.w_gate[:, :], start=k == 0,
                                             stop=k == 1)
                    last.then_inc(scored, 1)
                    pe.wait_ge(picked, 3 * B + 3)
                    pe.matmul(share_ps[:, :], t.ones_row[:, :], share_row[:, :, :].rearrange("p b k -> p (b k)"),
                              start=True, stop=True).then_inc(spread, 1)

                @block.vector
                def _(dve):
                    dve.wait_ge(scored, 1)
                    for b in range(B):
                        dve.scalar_tensor_tensor(logits[:, b, :], gate_ps[:, b, :], 1.0 / T, t.b_gate[:, :], ALU.mult,
                                                 ALU.add).then_inc(picked, 1)
                    dve.wait_ge(picked, B)
                    for b in range(B):
                        dve.max(best[:, b, :], logits[:, b, :]).then_inc(picked, 1)
                    dve.wait_ge(picked, 2 * B)
                    for b in range(B):
                        dve.max_index(which[:, b, :], best[:, b, :], logits[:, b, :]).then_inc(picked, 1)
                    dve.tensor_tensor(gap[:, :], best[:, :, 0], best[:, :, 1], ALU.subtract).then_inc(picked, 1)
                    dve.wait_ge(tanh_done, 1)
                    dve.tensor_scalar(share_row[:, :, 0], th[:, :], WS / 2, WS / 2, ALU.mult, ALU.add).then_inc(picked, 1)
                    dve.tensor_scalar(share_row[:, :, 1], th[:, :], -WS / 2, WS / 2, ALU.mult, ALU.add).then_inc(picked, 1)
                    dve.wait_ge(spread, 1)
                    dve.tensor_scalar(share[:, :, :].rearrange("p b k -> p (b k)"), share_ps[:, :],
                                      t.blend[:, 1:2], None, ALU.mult)
                    dve.wait_ge(m_loaded, 32)
                    dve.tensor_scalar(w1m[:, :], w1m[:, :], WS, None, ALU.mult).then_inc(m_steps, 1)
                    dve.tensor_scalar(w2m[:, :], w2m[:, :], t.blend[:, 2:3], None, ALU.mult).then_inc(m_steps, 1)
                    dve.wait_ge(m_steps, 2)
                    for w, (hi, lo) in ((w1m, w1p[0]), (w2m, w2p[0])):
                        dve.tensor_scalar(hi[:, :], w[:, :], 1.0, None, ALU.mult).then_inc(m_steps, 1)
                    dve.wait_ge(m_steps, 4)
                    for w, (hi, lo) in ((w1m, w1p[0]), (w2m, w2p[0])):
                        dve.tensor_tensor(lo[:, :], w[:, :], hi[:, :], ALU.subtract)

                @block.scalar
                def _(act):
                    act.wait_ge(picked, 3 * B + 1)
                    act.activation(th[:, :], gap[:, :], ACT.Tanh, scale=0.5).then_inc(tanh_done, 1)

        w1e = [s.sb(f"w1e{k}", [P, F]) for k in range(2)]
        w2e = [s.sb(f"w2e{k}", [P, FC * P]) for k in range(2)]
        w1x = [s.sb(f"w1x{k}", [P, F]) for k in range(2)]
        w2x = [s.sb(f"w2x{k}", [P, FC * P]) for k in range(2)]
        be = [s.sb(f"be{k}", [P, FC + 1]) for k in range(2)]
        bias = s.sb("bias", [P, 3])
        hid = s.sb("hid", [P, 2, T])
        hid_hi, hid_lo = s.sb("hid_hi", [P, 3, T], F16), s.sb("hid_lo", [P, 3, T], F16)
        y = s.sb("y", [P, T])
        h_ps = [s.ps(f"h_ps{k}", [P, T]) for k in range(2)]
        o_ps = s.ps("o_ps", [P, T])
        M = 3 * FC
        LAG = 2
        e_loaded = [s.sem(f"e_loaded{k}") for k in range(2)]
        loading, splitting = s.sem("loading"), s.sem("splitting")
        be_loaded = [s.sem(f"be_loaded{k}") for k in range(2)]
        upped = s.count("upped", M, M)
        gelued = s.count("gelued", M, 2)
        hid_split = s.count("hid_split", 2 * M, 4)
        downed = s.count("downed", M, M)
        weighed = s.count("weighed", 2, 2)
        biased = s.count("biased", 3, 3)
        w_split = s.count("w_split", 2 * 5, 10)
        y_made = s.count("y_made", 1, 1)
        added = s.count("added", 1, 1)
        with nc.Block() as block:

            @block.sync
            def _(sp):
                with sp.Fori(0, B) as b:
                    for k in range(2):
                        sp.wait_ge(w_split.sem, w_split.before(b, 5 * k + 3, 10))
                        e = sp.value_load(which[0:1, b, k:k + 1], min_val=0, max_val=E - 1)
                        sp.dma_start(w1e[k][:, :], d["w1e"][e]).then_inc(e_loaded[k], 16)
                        sp.dma_start(w2e[k][:, :], d["w2e"][e]).then_inc(e_loaded[k], 16)
                    sp.wait_ge(added.sem, added.before(b, 0, 1))
                    sp.sem_inc(loading, 1)
                    for k in range(2):
                        e = sp.value_load(which[0:1, b, k:k + 1], min_val=0, max_val=E - 1)
                        sp.dma_start(be[k][:, :], d["be"][e]).then_inc(be_loaded[k], 16)

            @block.gpsimd
            def _(pool):
                pool.sem_inc(w_split.sem, w_split.start)
                with pool.Fori(0, B) as b:
                    for k in range(2):
                        (w1_hi, w1_lo), (w2_hi, w2_lo) = w1p[k + 1], w2p[k + 1]
                        pool.wait_ge(e_loaded[k], b * 32 + 32)
                        pool.wait_ge(w_split.sem, w_split.before(b, 5 * k + 2, 10))
                        pool.sem_inc(splitting, 1)
                        pool.tensor_scalar(w1x[k][:, :], w1e[k][:, :], WS, None, ALU.mult).then_inc(w_split.sem, 1)
                        pool.wait_ge(downed.sem, downed.before(b, (k + 2) * FC - 1, M))
                        pool.wait_ge(w_split.sem, w_split.at(b, 5 * k))
                        pool.sem_inc(splitting, 1)
                        pool.tensor_scalar(w1_hi[:, :], w1x[k][:, :], 1.0, None, ALU.mult).then_inc(w_split.sem, 1)
                        pool.wait_ge(w_split.sem, w_split.at(b, 5 * k + 1))
                        pool.tensor_tensor(w1_lo[:, :], w1x[k][:, :], w1_hi[:, :],
                                           ALU.subtract).then_inc(w_split.sem, 1)
                        pool.wait_ge(weighed.sem, weighed.at(b, k))
                        pool.sem_inc(splitting, 1)
                        pool.tensor_scalar(w2_hi[:, :], w2x[k][:, :], 1.0, None, ALU.mult).then_inc(w_split.sem, 1)
                        pool.wait_ge(w_split.sem, w_split.at(b, 5 * k + 3))
                        pool.tensor_tensor(w2_lo[:, :], w2x[k][:, :], w2_hi[:, :],
                                           ALU.subtract).then_inc(w_split.sem, 1)

            @block.tensor
            def _(pe):
                pe.sem_inc(upped.sem, upped.start)
                pe.sem_inc(downed.sem, downed.start)
                def body(b, m):
                    if there(b, m, M):
                        k, c = divmod(m % M, FC)
                        if k and c == 0:
                            pe.wait_ge(w_split.sem, w_split.at(b, 5 * k - 3))
                        pe.wait_ge(gelued.sem, gelued.before(b, m, 2))
                        w_hi, w_lo = (w[:, c * P:(c + 1) * P] for w in w1p[k])
                        product_of_parts(pe, h_ps[m % 2], w_hi, w_lo, t.z_hi[:, b + m // M, :],
                                         t.z_lo[:, b + m // M, :]).then_inc(upped.sem, 1)
                    n = m - LAG
                    if n >= 0:
                        k, c = divmod(n, FC)
                        if k and c == 0:
                            pe.wait_ge(w_split.sem, w_split.at(b, 5 * k - 1))
                        if n == 0:
                            pe.wait_ge(y_made.sem, y_made.before(b, 0, 1))
                        pe.wait_ge(hid_split.sem, hid_split.at(b, 2 * n + 1))
                        w_hi, w_lo = (w[:, c * P:(c + 1) * P] for w in w2p[k])
                        product_of_parts(pe, o_ps, w_hi, w_lo, hid_hi[:, n % 3, :], hid_lo[:, n % 3, :],
                                         start=n == 0, stop=n == M - 1).then_inc(downed.sem, 1)

                pipelined(pe, LAG, M, body)

            @block.scalar
            def _(act):
                act.sem_inc(gelued.sem, gelued.start)
                with act.Fori(0, B) as b:
                    for m in range(M):
                        k, c = divmod(m, FC)
                        act.wait_ge(upped.sem, upped.at(b, m))
                        act.wait_ge(hid_split.sem, hid_split.before(b, 2 * m + 1, 4))
                        if k and c == 0:
                            act.wait_ge(be_loaded[k - 1], b * 16 + 16)
                        b1 = t.col("b1m", c) if k == 0 else be[k - 1][:, c:c + 1]
                        act.activation(hid[:, m % 2, :], h_ps[m % 2][:, :], ACT.Gelu_apprx_tanh,
                                       bias=b1, scale=1.0 / WS).then_inc(gelued.sem, 1)

            @block.vector
            def _(dve):
                dve.sem_inc(weighed.sem, weighed.start)
                dve.sem_inc(biased.sem, biased.start)
                dve.sem_inc(hid_split.sem, hid_split.start)
                dve.sem_inc(y_made.sem, y_made.start)
                dve.sem_inc(added.sem, added.start)
                def body(b, m):
                    if m == 2:
                        dve.wait_ge(added.sem, added.before(b, 0, 1))
                        dve.tensor_scalar(bias[:, 0:1], t.col("b2m"), t.blend[:, 2:3], None,
                                          ALU.mult).then_inc(biased.sem, 1)
                    if m in (2, 5):
                        k = m // 4
                        dve.wait_ge(e_loaded[k], b * 32 + 32)
                        dve.wait_ge(w_split.sem, w_split.before(b, 5 * k + 4, 10))
                        dve.tensor_scalar(w2x[k][:, :], w2e[k][:, :], share[:, b, k:k + 1], None,
                                          ALU.mult).then_inc(weighed.sem, 1)
                    if m in (7, 8):
                        k = m - 7
                        dve.wait_ge(be_loaded[k], b * 16 + 16)
                        dve.wait_ge(biased.sem, biased.at(b, k))
                        dve.scalar_tensor_tensor(bias[:, k + 1:k + 2], be[k][:, FC:FC + 1], share[:, b, k:k + 1],
                                                 bias[:, k:k + 1], ALU.mult, ALU.add).then_inc(biased.sem, 1)
                    if there(b, m, M):
                        dve.wait_ge(gelued.sem, gelued.at(b, m))
                        dve.wait_ge(downed.sem, downed.before(b, m, 3))
                        dve.tensor_copy(hid_hi[:, m % 3, :], hid[:, m % 2, :]).then_inc(hid_split.sem, 1)
                        dve.wait_ge(hid_split.sem, hid_split.at(b, 2 * m))
                        dve.tensor_tensor(hid_lo[:, m % 3, :], hid[:, m % 2, :], hid_hi[:, m % 3, :],
                                          ALU.subtract).then_inc(hid_split.sem, 1)
                    if m == M + LAG - 1:
                        dve.wait_ge(biased.sem, biased.at(b, 2))
                        dve.wait_ge(downed.sem, downed.at(b, M - 1))
                        dve.tensor_scalar(y[:, :], o_ps[:, :], bias[:, 2:3], 1.0 / WS, ALU.add,
                                          ALU.mult).then_inc(y_made.sem, 1)
                        dve.wait_ge(y_made.sem, y_made.at(b))
                        dve.tensor_tensor(t.x_t[:, b, :], t.x_t[:, b, :], y[:, :], ALU.add).then_inc(added.sem, 1)

                pipelined(dve, LAG, M, body)


def retention(t):
    nc, d = t.nc, t.dram
    SUM_AT = 6
    with Stage(nc, "ret") as q:
        mats = q.sb("mats", [P, len(RET_MATS), P])
        w = {n: mats[:, i, :] for i, n in enumerate(RET_MATS)}
        wsv = q.sb("wsv", [P, HD, P])
        head_sum = q.sb("head_sum", [P, 2, 2 * H])
        bg_neg = q.sb("bg_neg", [P, 1])
        z_b = q.sb("z_b", [P, T])
        k_sb, q_sb, g_sb = (q.sb(n, [P, T]) for n in ("k_sb", "q_sb", "g_sb"))
        kv = q.sb("kv", [P, 2, T])
        mem = q.sb("mem", [P, 2, T])
        qm = q.sb("qm", [P, HD, T])
        a_ps = q.ps("a_ps", [P, T])
        v_ps = [q.ps(f"v_ps{k}", [P, T]) for k in range(2)]
        h_ps = q.ps("h_ps", [P, T])
        w_loaded, bg_done = q.sem("w_loaded"), q.sem("bg_done")
        z_staged = q.count("z_staged", 1)
        made = q.count("made", 4, 4)
        copied = q.count("copied", 4, 4)
        v_made = q.count("v_made", HD)
        kv_done = q.count("kv_done", HD, 2)
        scanned = q.count("scanned", HD, HD)
        weighed = q.count("weighed", HD, HD)
        summed = q.count("summed", 2, 2)
        h_copied = q.count("h_copied", 1, 1)
        with nc.Block() as block:

            @block.sync
            def _(sp):
                sp.dma_start(mats[:, :, :], d["ret_mats"]).then_inc(w_loaded, 16)
                sp.dma_start(wsv[:, :, :], d["wsv"]).then_inc(w_loaded, 16)
                sp.dma_start(head_sum[:, :, :], d["head_sum"]).then_inc(w_loaded, 16)
                sp.wait_ge(w_loaded, 48)

            @block.tensor
            def _(pe):
                pe.sem_inc(made.sem, made.start)
                pe.sem_inc(summed.sem, summed.start)
                pe.wait_ge(w_loaded, 48)

                def whole_batch(b, i, name):
                    pe.wait_ge(copied.sem, copied.before(b, i, 1))
                    product(pe, a_ps, w[name], t.z_t[:, b, :]).then_inc(made.sem, 1)

                def v_by_tokens(b):
                    pe.wait_ge(z_staged.sem, z_staged.at(b))
                    pe.wait_ge(copied.sem, copied.before(b, 3, 1))
                    for j in range(TT):
                        last = pe.matmul(a_ps[:, j * P:(j + 1) * P], z_b[:, j * P:(j + 1) * P], w["wv"], start=True,
                                         stop=True)
                    last.then_inc(made.sem, 1)

                def body(b, n):
                    if there(b, n, HD):
                        at, m = b + n // HD, n % HD
                        if m == 0:
                            whole_batch(at, 0, "wsk")
                        pe.wait_ge(kv_done.sem, kv_done.before(b, n, 2))
                        product(pe, v_ps[n % 2], wsv[:, m, :], t.z_t[:, at, :]).then_inc(v_made.sem, 1)
                        if m == 0:
                            whole_batch(at, 1, "wg")
                        if m == 1:
                            whole_batch(at, 2, "wsq")
                        if m == 2:
                            v_by_tokens(at)
                    if n in (SUM_AT, SUM_AT + 4):
                        odd = n // (SUM_AT + 4)
                        pe.wait_ge(weighed.sem, weighed.at(b, 4 * odd + 3))
                        if not odd:
                            pe.wait_ge(h_copied.sem, h_copied.before(b, 0, 1))
                        for h in HALVES:
                            for c in range(4):
                                last = pe.matmul(h_ps[32 * c:32 * c + 32, h], head_sum[:, odd, :],
                                                 qm[:, 4 * odd + c, h], start=not odd, stop=bool(odd))
                        last.then_inc(summed.sem, 1)

                pipelined(pe, SUM_AT + 5 - HD, HD, body)

            @block.scalar
            def _(act):
                act.sem_inc(copied.sem, copied.start)
                act.sem_inc(h_copied.sem, h_copied.start)
                act.wait_ge(bg_done, 1)

                def inputs(b):
                    act.wait_ge(made.sem, made.before(b, 3, 4))
                    act.activation(z_b[:, :], t.z_t[:, b, :], ACT.Copy).then_inc(z_staged.sem, 1)
                    act.wait_ge(made.sem, made.at(b, 0))
                    act.wait_ge(kv_done.sem, kv_done.before(b, 1, 2))
                    act.activation(k_sb[:, :], a_ps[:, :], ACT.Identity, bias=t.col("bsk")).then_inc(copied.sem, 1)
                    act.wait_ge(made.sem, made.at(b, 1))
                    act.wait_ge(scanned.sem, scanned.before(b, HD - 1, HD))
                    act.activation(g_sb[:, :], a_ps[:, :], ACT.Sigmoid, bias=bg_neg[:, 0:1],
                                   scale=-1.0).then_inc(copied.sem, 1)
                    act.wait_ge(made.sem, made.at(b, 2))
                    act.wait_ge(weighed.sem, weighed.before(b, HD - 1, HD))
                    act.activation(q_sb[:, :], a_ps[:, :], ACT.Identity, bias=t.col("bsq")).then_inc(copied.sem, 1)
                    act.wait_ge(made.sem, made.at(b, 3))
                    act.activation(t.v_tok[:, b, :, :].rearrange("p a c -> p (a c)"), a_ps[:, :],
                                   ACT.Copy).then_inc(copied.sem, 1)

                def output(b):
                    act.wait_ge(summed.sem, summed.at(b, 1))
                    act.activation(t.h_seq[:, b, :], h_ps[:, :], ACT.Copy).then_inc(h_copied.sem, 1)

                inputs(0)
                with act.Fori(0, B - 1) as b:
                    inputs(b + 1)
                    output(b)
                output(B - 1)

            @block.vector
            def _(dve):
                dve.sem_inc(kv_done.sem, kv_done.start)
                dve.sem_inc(scanned.sem, scanned.start)
                dve.tensor_scalar(bg_neg[:, :], t.col("bg"), -1.0, None, ALU.mult).then_inc(bg_done, 1)

                def body(b, n):
                    if there(b, n, HD):
                        if n % HD == 0:
                            dve.wait_ge(copied.sem, copied.at(b + n // HD, 0))
                        dve.wait_ge(v_made.sem, v_made.at(b, n))
                        dve.wait_ge(scanned.sem, scanned.before(b, n, 2))
                        dve.scalar_tensor_tensor(kv[:, n % 2, :], v_ps[n % 2][:, :], t.col("bsv", n % HD),
                                                 k_sb[:, :], ALU.add, ALU.mult).then_inc(kv_done.sem, 1)
                    m = n - 1
                    if m >= 0:
                        if m % HD == 0:
                            dve.wait_ge(copied.sem, copied.at(b + m // HD, 1))
                        dve.wait_ge(kv_done.sem, kv_done.at(b, m))
                        dve.wait_ge(weighed.sem, weighed.before(b, m, 2))
                        dve.tensor_tensor_scan(mem[:, m % 2, :], g_sb[:, :], kv[:, m % 2, :], 0.0, ALU.mult,
                                               ALU.add).then_inc(scanned.sem, 1)

                pipelined(dve, 1, HD, body)

            @block.gpsimd
            def _(pool):
                pool.sem_inc(weighed.sem, weighed.start)
                with pool.Fori(0, B) as b:
                    pool.wait_ge(copied.sem, copied.at(b, 2))
                    for n in range(HD):
                        pool.wait_ge(scanned.sem, scanned.at(b, n))
                        pool.wait_ge(summed.sem, summed.before(b, n // 4, 2))
                        pool.tensor_tensor(qm[:, n, :], mem[:, n % 2, :], q_sb[:, :],
                                           ALU.mult).then_inc(weighed.sem, 1)


STACK_MOVES = 4 * G * 16


def stack(t, eng, x, b):
    to = (t.q_st, t.k_st)[x]
    for r in range(4):
        half = (r % 2, r // 2)[x]
        for g in range(G):
            eng.dma_start(to[32 * r:32 * r + 32, g, b, :],
                          t.part[32 * g:32 * g + 32, x, half, :]).then_inc(t.stacked[x], 16)


def queries_and_keys(t, s):
    nc, d = t.nc, t.dram
    t.q_st = s.sb("q_st", [P, G, B, T], F16)
    t.k_st = s.sb("k_st", [P, G, B, T], F16)
    t.part = part = s.sb("part", [P, 2, 2, T], F16)
    t.stacked = [s.sem(f"stacked{x}") for x in range(2)]
    with Stage(nc, "qk") as q:
        mats = q.sb("mats", [P, 2, P])
        rows = q.sb("rows", [P, 2, P])
        temp = q.sb("temp", [P, 4, H])
        h_b = q.sb("h_b", [P, T])
        raw = q.sb("raw", [P, 2, TT, P])
        sq = q.sb("sq", [P, 2, TT, P])
        ss = q.sb("ss", [P, 2, 2, TT * H])
        rn = q.sb("rn", [P, 2, 2, TT * H])
        rt = q.sb("rt", [P, TT * H])
        unit = q.sb("unit", [P, 2, TT, P])
        tok_ps = [q.ps(f"tok_ps{x}", [P, TT, P]) for x in range(2)]
        u_ps = [q.ps(f"u_ps{x}", [P, T]) for x in range(2)]
        w_loaded, temp_steps = q.sem("w_loaded"), q.sem("temp_steps")
        h_staged = q.count("h_staged", 1)
        made = q.count("made", 2, 2)
        raw_done = q.count("raw_done", 2, 2)
        squared = q.count("squared", 2, 2)
        sums = q.count("sums", 2 * 2, 4)
        rooted = q.count("rooted", 2, 2)
        inverted = q.count("inverted", 2, 2)
        scaled = q.count("scaled", 1, 1)
        unit_done = q.count("unit_done", 2, 2)
        turned = q.count("turned", 2, 2)
        hi_done = q.count("hi_done", 2, 2)
        lo_done = q.count("lo_done", 2, 2)
        sending = [q.sem(f"sending{x}") for x in range(2)]
        part_free = [q.count(f"part_free{x}", 1, 1) for x in range(2)]

        def stack_batches(eng, x):
            eng.sem_inc(part_free[x].sem, part_free[x].start)
            with eng.Fori(0, B - 1) as b:
                eng.wait_ge(lo_done.sem, lo_done.at(b, x))
                eng.sem_inc(sending[x], 1)
                stack(t, eng, x, b)
                eng.wait_ge(t.stacked[x], (b + 1) * STACK_MOVES)
                eng.sem_inc(part_free[x].sem, 1)

        with nc.Block() as block:

            @block.sync
            def _(sp):
                sp.dma_start(mats[:, :, :], d["att_mats"]).then_inc(w_loaded, 16)
                sp.dma_start(rows[:, :, :], d["bqk"]).then_inc(w_loaded, 16)
                stack_batches(sp, 0)

            @block.gpsimd
            def _(pool):
                stack_batches(pool, 1)

            @block.tensor
            def _(pe):
                pe.sem_inc(made.sem, made.start)
                pe.sem_inc(turned.sem, turned.start)
                pe.wait_ge(w_loaded, 32)
                with pe.Fori(0, B) as b:
                    pe.wait_ge(h_staged.sem, h_staged.at(b))
                    for x in range(2):
                        pe.wait_ge(raw_done.sem, raw_done.before(b, x, 2))
                        for j in range(TT):
                            last = pe.matmul(tok_ps[x][:, j, :], h_b[:, j * P:(j + 1) * P], mats[:, x, :], start=True,
                                             stop=True)
                        last.then_inc(made.sem, 1)
                    for x in range(2):
                        pe.wait_ge(unit_done.sem, unit_done.at(b, x))
                        pe.wait_ge(lo_done.sem, lo_done.before(b, x, 2))
                        for j in range(TT):
                            last = pe.transpose(u_ps[x][:, j * P:(j + 1) * P], unit[:, x, j, :], t.ident[:, :])
                        last.then_inc(turned.sem, 1)

            @block.scalar
            def _(act):
                act.sem_inc(squared.sem, squared.start)
                act.sem_inc(rooted.sem, rooted.start)
                act.sem_inc(hi_done.sem, hi_done.start)
                act.activation(temp[:, 0, :], t.col("temp", 0, H), ACT.Abs).then_inc(temp_steps, 1)
                act.wait_ge(temp_steps, 1)
                act.activation(temp[:, 1, :], temp[:, 0, :], ACT.Exp, scale=-1.0).then_inc(temp_steps, 1)
                act.wait_ge(temp_steps, 2)
                act.activation(temp[:, 2, :], temp[:, 1, :], ACT.Ln, bias=1.0).then_inc(temp_steps, 1)
                with act.Fori(0, B) as b:
                    act.wait_ge(made.sem, made.before(b, 1, 2))
                    act.activation(h_b[:, :], t.h_seq[:, b, :], ACT.Copy).then_inc(h_staged.sem, 1)
                    for x in range(2):
                        act.wait_ge(raw_done.sem, raw_done.at(b, x))
                        act.wait_ge(sums.sem, sums.before(b, 2 * x, 4))
                        act.activation(sq[:, x, :, :], raw[:, x, :, :], ACT.Square).then_inc(squared.sem, 1)
                    for x in range(2):
                        act.wait_ge(sums.sem, sums.at(b, 2 * x + 1))
                        act.wait_ge(inverted.sem, inverted.before(b, x, 2))
                        act.activation(rn[:, x, 1, :], ss[:, x, 1, :], ACT.Sqrt).then_inc(rooted.sem, 1)
                    for x in range(2):
                        act.wait_ge(turned.sem, turned.at(b, x))
                        act.wait_ge(part_free[x].sem, part_free[x].before(b, 0, 1))
                        act.activation(part[:, x, 0, :], u_ps[x][:, :], ACT.Copy).then_inc(hi_done.sem, 1)

            @block.vector
            def _(dve):
                for c in (raw_done, sums, inverted, scaled, unit_done, lo_done):
                    dve.sem_inc(c.sem, c.start)
                dve.wait_ge(temp_steps, 3)
                dve.scalar_tensor_tensor(temp[:, 3, :], t.col("temp", 0, H), 0.0, temp[:, 2, :], ALU.max,
                                         ALU.add).then_inc(temp_steps, 1)
                dve.wait_ge(temp_steps, 4)
                dve.wait_ge(w_loaded, 32)
                heat = temp[:, 3, :].rearrange("p (o h) -> p o h", o=1).broadcast_to([P, TT, H])
                with dve.Fori(0, B) as b:
                    for x in range(2):
                        dve.wait_ge(made.sem, made.at(b, x))
                        dve.wait_ge(squared.sem, squared.before(b, x, 2))
                        dve.wait_ge(unit_done.sem, unit_done.before(b, x, 2))
                        bias = rows[:, x, :].rearrange("p (o c) -> p o c", o=1).broadcast_to([P, TT, P])
                        dve.tensor_tensor(raw[:, x, :, :], tok_ps[x][:, :, :], bias,
                                          ALU.add).then_inc(raw_done.sem, 1)
                    for x in range(2):
                        dve.wait_ge(squared.sem, squared.at(b, x))
                        dve.tensor_reduce(ss[:, x, 0, :],
                                          sq[:, x, :, :].rearrange("p a (h c) -> p (a h) c", c=HD), AX.X,
                                          ALU.add).then_inc(sums.sem, 1)
                        dve.wait_ge(sums.sem, sums.at(b, 2 * x))
                        dve.wait_ge(rooted.sem, rooted.before(b, x, 2))
                        dve.tensor_scalar(ss[:, x, 1, :], ss[:, x, 0, :], 1e-24, None,
                                          ALU.max).then_inc(sums.sem, 1)
                    for x in range(2):
                        dve.wait_ge(rooted.sem, rooted.at(b, x))
                        dve.wait_ge(unit_done.sem, unit_done.before(b, x, 2))
                        dve.reciprocal(rn[:, x, 0, :], rn[:, x, 1, :]).then_inc(inverted.sem, 1)
                    dve.wait_ge(inverted.sem, inverted.at(b, 0))
                    dve.tensor_tensor(rt[:, :].rearrange("p (a h) -> p a h", h=H),
                                      rn[:, 0, 0, :].rearrange("p (a h) -> p a h", h=H), heat,
                                      ALU.mult).then_inc(scaled.sem, 1)
                    dve.wait_ge(scaled.sem, scaled.at(b))
                    for x in range(2):
                        dve.wait_ge(inverted.sem, inverted.at(b, x))
                        dve.wait_ge(turned.sem, turned.before(b, x, 2))
                        factor = (rt[:, :], rn[:, 1, 0, :])[x].rearrange("p (n o) -> p n o", o=1).broadcast_to([P, TT * H, HD])
                        dve.tensor_tensor(unit[:, x, :, :].rearrange("p a (h c) -> p (a h) c", c=HD),
                                          raw[:, x, :, :].rearrange("p a (h c) -> p (a h) c", c=HD), factor,
                                          ALU.mult).then_inc(unit_done.sem, 1)
                    for x in range(2):
                        dve.wait_ge(hi_done.sem, hi_done.at(b, x))
                        dve.tensor_tensor(part[:, x, 1, :], u_ps[x][:, :], part[:, x, 0, :],
                                          ALU.subtract).then_inc(lo_done.sem, 1)


def attention(t):
    nc, d = t.nc, t.dram
    RING = 4
    OUT_AT = 12
    with Stage(nc, "att") as q:
        km = q.sb("km", [P, 2, GH, T], F16)
        va = q.sb("va", [P, 2, KC, GH, 32])
        prob = q.sb("prob", [P, RING, GH, HALF])
        o_sb, num, den, att = (t.h_seq[:, i, :] for i in range(B))
        wo = q.sb("wo", [P, P])
        bias = q.sb("bias", [P, 1])
        s_ps = [q.ps(f"s_ps{k}", [P, 2, HALF]) for k in range(3)]
        o_ps = [q.ps(f"o_ps{k}", [P, HALF]) for k in range(2)]
        U = 2 * KC
        w_loaded, bias_steps = q.sem("w_loaded"), q.sem("bias_steps")
        blank = q.sem("blank")
        keyed = q.count("keyed", G)
        scored = q.count("scored", G * U * 2)
        exped = q.count("exped", G * U * 2, 3)
        used = q.count("used", G * U, RING)
        out_done = q.count("out_done", G * 2, 2)
        moved = q.sem("moved")
        recips = q.count("recips", G)
        normed = q.count("normed", G, G)
        projected = q.count("projected", 1, 1)
        added = q.count("added", 1, 1)
        MOVES = 2 * GH * 16
        with nc.Block() as block:

            @block.gpsimd
            def _(pool):
                pool.memset(va[:, :, :, :, HD:32], 1.0).then_inc(blank, 1)
                stack(t, pool, 1, B - 1)

            @block.tensor
            def _(pe):
                pe.sem_inc(used.sem, used.start)
                pe.wait_ge(w_loaded, 16)
                pe.matmul(s_ps[0][:, 0, 0:1], wo[:, :], t.col("bv"), start=True, stop=True).then_inc(bias_steps, 1)
                pe.wait_ge(bias_steps, 2)

                def project(b, k):
                    pe.wait_ge(normed.sem, normed.before(b, G - 1, G))
                    for h in range(2):
                        last = pe.matmul(s_ps[k][:, h, :], wo[:, :], att[:, HALVES[h]], start=True, stop=True)
                    last.then_inc(projected.sem, 1)

                with pe.Fori(0, B) as b:

                    def scores(g, u, pair):
                        half, kc = divmod(u, KC)
                        n = (g * U + u) * 2 + pair
                        pe.wait_ge(exped.sem, exped.before(b, n, 3 if n >= 2 else 2))
                        if n == 2 * OUT_AT:
                            project(b, n % 3)
                            pe.wait_ge(added.sem, added.before(b, 0, 1))
                        for i in range(2):
                            j = 2 * pair + i
                            last = pe.matmul(s_ps[n % 3][:, i, :], km[:, g % 2, j, kc * P:(kc + 1) * P],
                                             t.q_st[:, g, b, HALVES[half]], start=True, stop=True)
                        last.then_inc(scored.sem, 1)

                    def values(g, u, pair):
                        half, kc = divmod(u, KC)
                        if kc == 0 and pair == 0:
                            pe.wait_ge(out_done.sem, out_done.before(b, g * 2 + half, 2))
                        pe.wait_ge(exped.sem, exped.at(b, (g * U + u) * 2 + pair))
                        for j in (2 * pair, 2 * pair + 1):
                            last = pe.matmul(o_ps[half][32 * j:32 * j + 32, :], va[:, g % 2, kc, j, :],
                                             prob[:, u % RING, j, :], start=kc == 0, stop=kc == KC - 1)
                        if pair == 1:
                            last.then_inc(used.sem, 1)

                    pe.wait_ge(t.stacked[0], (b + 1) * STACK_MOVES)
                    for g in range(G):
                        pe.wait_ge(keyed.sem, keyed.at(b, g))
                        for u in range(U):
                            for pair in range(2):
                                scores(g, u, pair)
                                if (g, u) >= (0, 2):
                                    values(*divmod(g * U + u - 2, U), pair)
                    for u in (U - 2, U - 1):
                        for pair in range(2):
                            values(G - 1, u, pair)
                pe.wait_ge(exped.sem, exped.at(B - 1, G * U * 2 - 1))
                project(B, 0)

            @block.scalar
            def _(act):
                act.sem_inc(exped.sem, exped.start)
                with act.Fori(0, B) as b:
                    for g in range(G):
                        for u in range(U):
                            for pair in range(2):
                                n = (g * U + u) * 2 + pair
                                act.wait_ge(scored.sem, scored.at(b, n))
                                if pair == 0:
                                    act.wait_ge(used.sem, used.before(b, g * U + u, RING))
                                act.activation(prob[:, u % RING, 2 * pair:2 * pair + 2, :], s_ps[n % 3][:, :, :],
                                               ACT.Exp).then_inc(exped.sem, 1)

            @block.vector
            def _(dve):
                dve.memset(att, 0.0).then_inc(normed.sem, G)
                dve.sem_inc(out_done.sem, out_done.start)
                dve.sem_inc(projected.sem, projected.start)
                dve.sem_inc(added.sem, added.start)
                dve.wait_ge(bias_steps, 1)
                dve.tensor_tensor(bias[:, :], s_ps[0][:, 0, 0:1], t.col("bo"), ALU.add).then_inc(bias_steps, 1)
                dve.wait_ge(blank, 1)

                def keys_and_values(b, g):
                    if g % G == 0:
                        dve.wait_ge(t.stacked[1], (b + g // G + 1) * STACK_MOVES)
                    b, g = b + g // G, g % G
                    dve.tensor_copy(
                        va[:, g % 2, :, :, 0:HD],
                        t.v_tok[:, b, :, :].rearrange("p k (g j c) -> p g k j c", g=G, c=HD)[:, g, :, :, :])
                    for j in range(GH):
                        last = dve.tensor_scalar(km[:, g % 2, j, :], t.k_st[:, g, b, :], t.col("head_mask", j), None,
                                                 ALU.mult)
                    last.then_inc(keyed.sem, 1)

                def body(b, n):
                    g = n - 2
                    if g >= 0:
                        for half in range(2):
                            dve.wait_ge(used.sem, used.at(b, g * U + half * KC + KC - 1))
                            dve.tensor_copy(o_sb[:, HALVES[half]], o_ps[half][:, :]).then_inc(out_done.sem, 1)
                    if there(b, n, G):
                        keys_and_values(b, n)
                    if g >= 0:
                        dve.wait_ge(moved, (b * G + g + 1) * MOVES)
                        mine = slice(32 * g, 32 * g + 32)
                        dve.reciprocal(den[mine, :], den[mine, :]).then_inc(recips.sem, 1)
                        dve.wait_ge(recips.sem, recips.at(b, g))
                        if g == 0:
                            dve.wait_ge(projected.sem, projected.at(b))
                        dve.tensor_tensor(att[mine, :], num[mine, :], den[mine, :], ALU.mult).then_inc(normed.sem, 1)
                    if g == G - 1:
                        dve.wait_ge(projected.sem, projected.at(b + 1))
                        k = 0 if isinstance(b, int) and b == B - 1 else 2 * OUT_AT % 3
                        dve.scalar_tensor_tensor(t.x_t[:, b, :], s_ps[k][:, :, :].rearrange("p h c -> p (h c)"),
                                                 bias[:, 0:1], t.x_t[:, b, :], ALU.add, ALU.add).then_inc(added.sem, 1)

                pipelined(dve, 2, G, body)

            @block.sync
            def _(sp):
                sp.dma_start(wo[:, :], d["wo"]).then_inc(w_loaded, 16)
                stack(t, sp, 0, B - 1)
                with sp.Fori(0, B) as b:
                    for g in range(G):
                        sp.wait_ge(out_done.sem, out_done.at(b, 2 * g + 1))
                        for j in range(GH):
                            for i, to in enumerate((num, den)):
                                at, frm = HD * (GH * g + j), 32 * j + HD * i
                                sp.dma_start(to[at:at + HD, :], o_sb[frm:frm + HD, :]).then_inc(moved, 16)


def store(t):
    nc, d = t.nc, t.dram
    with Stage(nc, "store") as s:
        x_half = s.sb("x_half", [P, 2, HALF])
        out = s.sb("out", [P, B, 2, NT, P])
        ps = [s.ps(f"ps{k}", [P, NT, P]) for k in range(2)]
        staged = s.count("staged", 2)
        turned = s.count("turned", 2, 2)
        copied = s.count("copied", 2, 2)
        stored = s.sem("stored")
        with nc.Block() as block:

            @block.scalar
            def _(act):
                with act.Fori(0, B) as b:
                    for k in range(2):
                        act.wait_ge(turned.sem, turned.before(b, k, 2))
                        act.activation(x_half[:, k, :], t.x_t[:, b, HALVES[k]], ACT.Copy).then_inc(staged.sem, 1)

            @block.tensor
            def _(pe):
                pe.sem_inc(turned.sem, turned.start)
                with pe.Fori(0, B) as b:
                    for k in range(2):
                        pe.wait_ge(staged.sem, staged.at(b, k))
                        pe.wait_ge(copied.sem, copied.before(b, k, 2))
                        for j in range(NT):
                            last = pe.transpose(ps[k][:, j, :], x_half[:, k, j * P:(j + 1) * P], t.ident[:, :])
                        last.then_inc(turned.sem, 1)

            @block.vector
            def _(dve):
                dve.sem_inc(copied.sem, copied.start)
                with dve.Fori(0, B) as b:
                    for k in range(2):
                        dve.wait_ge(turned.sem, turned.at(b, k))
                        dve.tensor_copy(out[:, b, k, :, :], ps[k][:, :, :]).then_inc(copied.sem, 1)

            @block.sync
            def _(sp):
                with sp.Fori(0, B) as b:
                    for k in range(2):
                        sp.wait_ge(copied.sem, copied.at(b, k))
                        sp.dma_start(d["out"][b, k], out[:, b, k, :, :]).then_inc(stored, 16)
                sp.wait_ge(stored, 16 * B * 2)


def hybrid_layer(nc, dram):
    t = Layer(nc, dram)
    with Stage(nc, "all") as whole:
        load_constants(t, whole)
        with Stage(nc, "z1") as z:
            with Stage(nc, "ssm") as s:
                scan_buffers(t, s)
                with Stage(nc, "pre") as big:
                    t.z_t = big.sb("z_t", [P, B, T])
                    layernorm(t, "ln1", first=True)
                    scan_inputs(t, big)
                selective_scan(t)
            t.z_hi, t.z_lo = (z.sb(n, [P, B, T], F16) for n in ("z_hi", "z_lo"))
            layernorm(t, "ln2", split=True)
            ffn(t, "ffn1")
        with Stage(nc, "attn") as s:
            with Stage(nc, "hv") as hv:
                t.h_seq = hv.sb("h_seq", [P, B, T])
                t.v_tok = hv.sb("v_tok", [P, B, TT, P])
                with Stage(nc, "z3") as z:
                    t.z_t = z.sb("z_t", [P, B, T])
                    layernorm(t, "ln3")
                    retention(t)
                queries_and_keys(t, hv)
                attention(t)
        with Stage(nc, "z4") as z:
            t.z_hi, t.z_lo = (z.sb(n, [P, B, T], F16) for n in ("z_hi", "z_lo"))
            layernorm(t, "ln4", split=True)
            ffn(t, "ffn2")
        store(t)


def pack(i):
    a = {k: np.asarray(v) for k, v in i.items()}
    A = lambda n: a["L0_attn_a_" + n]
    R = lambda n: a["L0_attn_b_" + n]
    M = lambda n: a["L0_ffn_" + n]
    cols = {
        "ln_g": A("ln_g"), "ln_b": A("ln_b"), "w1_b": A("w1_b"), "v1_b": A("v1_b"), "w2_b": A("w2_b"),
        "conv": A("conv_w")[:, 0, :], "d_skip": A("D_skip"), "b_dt": A("b_dt"), "a_log": A("A_log"),
        "bsk": R("bsk"), "bsq": R("bsq"), "bg": np.repeat(R("bg"), HD),
        "bsv": np.repeat(R("bsv").reshape(H, HD)[:, COLUMNS], HD, axis=0), "bv": R("bv"), "bo": R("bo"),
        "alpha": np.full((P,), M("alpha")), "b1m": M("b1m").reshape(FC, P).T, "b2m": M("b2m"),
        "temp": np.tile(R("temp").reshape(1, H), (P, 1)),
        "head_mask": np.tile(np.repeat(np.eye(GH, dtype=np.float32), HD, axis=0), (P // (GH * HD), 1)),
    }
    vecs = np.concatenate([cols[n].reshape(P, k) for n, k in VEC_SIZES], axis=1)
    bc = np.concatenate([A("W_B"), A("W_C")], axis=1)
    wsv = R("Wsv").T.reshape(P, H, HD)[:, :, COLUMNS]
    head_sum = np.zeros((H, HD, 2, 2, H), np.float32)
    for h in range(H):
        for e in range(2):
            head_sum[h, :, e, e, h] = 1
    by_column = lambda w: w.T.reshape(H, HD, P).transpose(1, 0, 2).reshape(P, P)
    return {
        "x": A("x").reshape(B, 2, NT, P, P).transpose(0, 1, 3, 2, 4),
        "vecs": vecs,
        "ident": np.eye(P, dtype=np.float32),
        "w_gate": M("w_gate"),
        "b_gate": M("b_gate").reshape(1, E),
        "w1m": M("W1m"),
        "w2m": M("W2m").reshape(FC, P, P).transpose(1, 0, 2).reshape(P, FC * P),
        "ssm_mats": np.stack([A("w1_w"), A("v1_w"), A("w2_w"), A("W_dt")], axis=1),
        "wbc": np.tile(bc, (1, 3)),
        "pick": np.tile(np.eye(2 * NS, dtype=np.float32), (3, 1)),
        "ret_mats": np.stack([R("Wsk").T, R("Wsq").T, np.repeat(R("Wg").T, HD, axis=1), R("Wv").T], axis=1),
        "wsv": np.repeat(wsv.transpose(0, 2, 1)[:, :, :, None], HD, axis=3).reshape(P, HD, P),
        "head_sum": head_sum.reshape(P, 2, 2 * H),
        "att_mats": np.stack([by_column(R("Wq")), by_column(R("Wk"))], axis=1),
        "bqk": np.tile(np.stack([R("bq"), R("bk")])[None], (P, 1, 1)),
        "wo": R("Wo").T,
        "w1e": M("W1e"),
        "w2e": M("W2e").reshape(E, FC, P, P).transpose(0, 2, 1, 3).reshape(E, P, FC * P),
        "be": np.concatenate([M("b1e").reshape(E, FC, P).transpose(0, 2, 1), M("b2e").reshape(E, P, 1)], axis=2),
    }


def program(nc, arrays):
    dram = {n: nc.dram_tensor("in_" + n, a.shape, F32, kind="ExternalInput").ap() for n, a in arrays.items()}
    out = nc.dram_tensor("out", (B, 2, NT, P, P), F32, kind="ExternalOutput").ap()
    dram["x"] = dram["x"].rearrange("b k p j c -> b k p (j c)")
    dram["out"] = out.rearrange("b k j p c -> b k p j c")
    hybrid_layer(nc, dram)


def kernel(**inputs):
    import concourse.bacc as bacc
    from concourse.bass_utils import run_bass_kernel_spmd

    arrays = {n: np.ascontiguousarray(a) for n, a in pack(inputs).items()}
    nc = bacc.Bacc("TRN2", target_bir_lowering=False, num_devices=1)
    program(nc, arrays)
    r = run_bass_kernel_spmd(nc, [{"in_" + n: a for n, a in arrays.items()}], core_ids=[0])
    return r.results[0]["out"].reshape(B, T, P)
```

```python
from contextlib import ExitStack

import numpy as np

import concourse.bass as bass
from concourse import mybir

ALU = mybir.AluOpType
ACT = mybir.ActivationFunctionType
AX = mybir.AxisListType
F32 = mybir.dt.float32
F16 = mybir.dt.float16
BF16 = mybir.dt.bfloat16
U32 = mybir.dt.uint32

P = 128
B, T = 4, 1024
HALF = 512
HALVES = (slice(0, HALF), slice(HALF, T))
NT = HALF // P
TT = T // P
NS = 16
H, HD = 16, 8
E, F = 8, 512
FC = F // P
G = 4
GH = H // G
KC = T // P
EPS = 1e-5
COLUMNS = (0, 2, 4, 6, 1, 3, 5, 7)
WS = 64.0
BC3 = 3 * 2 * NS

VEC_SIZES = (("ln_g", 1), ("ln_b", 1), ("w1_b", 1), ("v1_b", 1), ("w2_b", 1), ("conv", 3), ("d_skip", 1),
             ("b_dt", 1), ("a_log", NS), ("bsk", 1), ("bsq", 1), ("bg", 1), ("bsv", HD), ("bv", 1), ("bo", 1),
             ("alpha", 1), ("b1m", FC), ("b2m", 1), ("temp", H), ("head_mask", GH))
VEC = {}
NV = 0
for _name, _n in VEC_SIZES:
    VEC[_name] = NV
    NV += _n

SSM_MATS = ("w1", "v1", "w2", "wdt")
RET_MATS = ("wsk", "wsq", "wg", "wv")
ATT_MATS = ("wq", "wk")


class Count:
    def __init__(self, sem, per=1, start=0):
        self.sem, self.per, self.start = sem, per, start

    def at(self, i, n=0):
        return i * self.per + (self.start + n + 1)

    def before(self, i, n, k):
        assert self.start >= k
        return i * self.per + (self.start + n + 1 - k)


class Stage:

    def __init__(self, nc, name):
        self.nc, self.name, self.ctx = nc, name, ExitStack()

    def __enter__(self):
        return self

    def __exit__(self, *a):
        return self.ctx.__exit__(*a)

    def sb(self, name, shape, dt=F32):
        return self.ctx.enter_context(self.nc.sbuf_tensor(f"{self.name}_{name}", shape, dt))

    def ps(self, name, shape, dt=F32):
        return self.ctx.enter_context(self.nc.psum_tensor(f"{self.name}_{name}", shape, dt))

    def sem(self, name):
        return self.ctx.enter_context(self.nc.semaphore(f"{self.name}_{name}"))

    def count(self, name, per=1, start=0):
        return Count(self.sem(name), per, start)


class Layer:

    def __init__(self, nc, dram):
        self.nc, self.dram = nc, dram

    def col(self, name, k=0, n=1):
        return self.vec[:, VEC[name] + k:VEC[name] + k + n]


def load_constants(t, whole):
    nc, d = t.nc, t.dram
    t.x_t = whole.sb("x_t", [P, B, T])
    t.vec = whole.sb("vec", [P, NV])
    t.ident = whole.sb("ident", [P, P])
    t.minus_half = whole.sb("minus_half", [P, P])
    t.eps = whole.sb("eps", [P, NT])
    t.one_eps = whole.sb("one_eps", [P, NT])
    t.eps_squared = whole.sb("eps_squared", [P, NT])
    t.scale = whole.sb("scale", [P, F])
    t.blend = whole.sb("blend", [P, 3])
    t.w_gate = whole.sb("w_gate", [P, E])
    t.b_gate = whole.sb("b_gate", [1, E])
    t.ones_row = whole.sb("ones_row", [1, P])
    with Stage(nc, "load") as s:
        loaded, clipped = s.sem("loaded"), s.sem("clipped")
        with nc.Block() as block:

            @block.sync
            def _(sp):
                for dst, src in ((t.vec, d["vecs"]), (t.ident, d["ident"]), (t.w_gate, d["w_gate"]),
                                 (t.b_gate, d["b_gate"])):
                    sp.dma_start(dst[:, :], src).then_inc(loaded, 16)
                sp.wait_ge(loaded, 16 * 4)

            @block.vector
            def _(dve):
                dve.memset(t.minus_half[:, :], -0.5)
                dve.memset(t.eps[:, :], EPS)
                dve.memset(t.one_eps[:, :], 1 + EPS)
                dve.memset(t.eps_squared[:, :], EPS * EPS)
                dve.memset(t.scale[:, :], WS)
                dve.memset(t.ones_row[:, :], 1.0)
                dve.wait_ge(loaded, 16 * 4)
                dve.tensor_scalar(t.blend[:, 0:1], t.col("alpha"), 0.1, 1.0, ALU.max, ALU.min).then_inc(clipped, 1)
                dve.wait_ge(clipped, 1)
                dve.tensor_scalar(t.blend[:, 1:2], t.blend[:, 0:1], -1.0, 1.0, ALU.mult, ALU.add)
                dve.tensor_scalar(t.blend[:, 2:3], t.blend[:, 0:1], WS, None, ALU.mult)


def input_layernorms(t):
    nc, d = t.nc, t.dram
    N = 4
    with Stage(nc, "ln1") as s:
        x_half = s.sb("x_half", [P, N, HALF])
        stats = s.sb("stats", [P, N, NT, 6])
        mv = s.sb("mv", [P, N, NT, 2])
        rstd = s.sb("rstd", [P, N, NT])
        rtmp = s.sb("rtmp", [P, N, 2, NT])
        z_tok = s.sb("z_tok", [P, N, HALF])
        tok_ps = [s.ps(f"tok_ps{n}", [P, HALF]) for n in range(N)]
        z_ps = [s.ps(f"z_ps{n}", [P, HALF]) for n in range(N)]
        RS = 3
        x_loaded = [s.sem(f"x_loaded{n}") for n in range(N)]
        turned = s.count("turned", N, N)
        kept = s.count("kept", N, N)
        got_mv = s.count("got_mv", N)
        rstd_steps = s.count("rstd_steps", N * RS)
        normed = s.count("normed", N, N)
        z_turned = s.count("z_turned", N, N)
        z_copied = s.count("z_copied", N, N)
        with nc.Block() as block:

            @block.sync
            def _(sp):
                with sp.Fori(0, B // 2) as i:
                    for n in range(N):
                        sp.wait_ge(z_turned.sem, z_turned.before(i, n, N))
                        sp.dma_start(x_half[:, n, :], d["x"][i * 2 + n // 2, n % 2]).then_inc(x_loaded[n], 16)

            @block.tensor
            def _(pe):
                pe.sem_inc(turned.sem, turned.start)
                pe.sem_inc(z_turned.sem, z_turned.start)

                def turn_x(i, n):
                    pe.wait_ge(x_loaded[n], i * 16 + 16)
                    pe.wait_ge(kept.sem, kept.before(i, n, N))
                    for j in range(NT):
                        cols = slice(j * P, (j + 1) * P)
                        last = pe.transpose(tok_ps[n][:, cols], x_half[:, n, cols], t.ident[:, :])
                    last.then_inc(turned.sem, 1)

                def turn_z(i, n):
                    pe.wait_ge(normed.sem, normed.at(i, n))
                    pe.wait_ge(z_copied.sem, z_copied.before(i, n, N))
                    for j in range(NT):
                        cols = slice(j * P, (j + 1) * P)
                        last = pe.transpose(z_ps[n][:, cols], z_tok[:, n, cols], t.ident[:, :])
                    last.then_inc(z_turned.sem, 1)

                with pe.Fori(0, B // 2) as i:
                    for n in range(N):
                        turn_x(i, n)
                    for n in range(N):
                        turn_z(i, n)

            @block.vector
            def _(dve):
                dve.sem_inc(normed.sem, normed.start)

                def statistics(i, n):
                    dve.wait_ge(x_loaded[n], i * 16 + 16)
                    dve.wait_ge(normed.sem, normed.before(i, n, N))
                    for j in range(NT):
                        dve.bn_stats(stats[:, n, j, :], x_half[:, n, j * P:(j + 1) * P])
                    dve.drain()
                    for j in range(NT):
                        last = dve.bn_aggr(mv[:, n, j, :], stats[:, n, j, :])
                    last.then_inc(got_mv.sem, 1)

                def normalise(i, n):
                    dve.wait_ge(rstd_steps.sem, rstd_steps.at(i, n * RS + RS - 1))
                    dve.wait_ge(z_turned.sem, z_turned.before(i, n, N))
                    for j in range(NT):
                        last = dve.tensor_scalar(z_tok[:, n, j * P:(j + 1) * P], x_half[:, n, j * P:(j + 1) * P], mv[:, n, j, 0:1],
                                                 rstd[:, n, j:j + 1], ALU.subtract, ALU.mult)
                    last.then_inc(normed.sem, 1)

                with dve.Fori(0, B // 2) as i:
                    for n in range(N + 2):
                        if n < N:
                            statistics(i, n)
                        if n >= 2:
                            normalise(i, n - 2)

            @block.gpsimd
            def _(pool):
                with pool.Fori(0, B // 2) as i:
                    for n in range(N):
                        scaled, product_of_both = rtmp[:, n, 0, :], rtmp[:, n, 1, :]
                        steps = ((scaled, mv[:, n, :, 1], t.one_eps[:, :], ALU.mult),
                                 (product_of_both, scaled, t.eps_squared[:, :], ALU.add),
                                 (rstd[:, n, :], product_of_both, t.minus_half[:, 0:NT], ALU.pow))
                        pool.wait_ge(got_mv.sem, got_mv.at(i, n))
                        pool.wait_ge(normed.sem, normed.before(i, n, N))
                        for m, (out, a, b, op) in enumerate(steps):
                            if m:
                                pool.wait_ge(rstd_steps.sem, rstd_steps.at(i, n * RS + m - 1))
                            pool.tensor_tensor(out, a, b, op).then_inc(rstd_steps.sem, 1)

            @block.scalar
            def _(act):
                act.sem_inc(kept.sem, kept.start)
                act.sem_inc(z_copied.sem, z_copied.start)

                def take_x(i, n):
                    act.wait_ge(turned.sem, turned.at(i, n))
                    act.activation(t.x_t[:, i * 2 + n // 2, HALVES[n % 2]], tok_ps[n][:, :],
                                   ACT.Copy).then_inc(kept.sem, 1)

                def copy_z(i, n):
                    z = t.z_t[:, i * 2 + n // 2, HALVES[n % 2]]
                    act.wait_ge(z_turned.sem, z_turned.at(i, n))
                    act.activation(z, z_ps[n][:, :], ACT.Identity, bias=t.col("ln_b"),
                                   scale=t.col("ln_g")).then_inc(z_copied.sem, 1)

                with act.Fori(0, B // 2) as i:
                    for n in range(N):
                        take_x(i, n)
                    for n in range(N):
                        copy_z(i, n)


def product(pe, out, w, rhs, start=True, stop=True):
    for h in HALVES:
        last = pe.matmul(out[:, h], w, rhs[:, h], start=start, stop=stop)
    return last


def product_of_parts(pe, out, w_hi, w_lo, x_hi, x_lo, start=True, stop=True):
    parts = ((w_hi, x_hi), (w_hi, x_lo), (w_lo, x_hi))
    for i, (w, x) in enumerate(parts):
        for h in HALVES:
            last = pe.matmul(out[:, h], w, x[:, h], start=start and i == 0, stop=stop and i == len(parts) - 1)
    return last


def scan_buffers(t, s):
    t.ssm_mats = s.sb("mats", [P, len(SSM_MATS), P])
    t.ssm_w = {n: t.ssm_mats[:, i, :] for i, n in enumerate(SSM_MATS)}
    t.u_t, t.v_t, t.dt_t, t.du_t = (s.sb(n, [P, B, T]) for n in ("u_t", "v_t", "dt_t", "du_t"))
    t.bc = s.sb("bc", [BC3, B, T], BF16)
    t.sel = s.sb("sel", [BC3, 2 * NS, P], BF16)


def scan_inputs(t):
    nc, d = t.nc, t.dram
    with Stage(nc, "conv") as q:
        wbc = q.sb("wbc", [P, BC3])
        pick = q.sb("pick", [BC3, 2 * NS])
        x1 = q.sb("x1", [P, T + 2])
        y0, y1, y2 = (q.sb(n, [P, T]) for n in ("y0", "y1", "y2"))
        size, decay, log, relu = (q.sb(n, [P, T]) for n in ("size", "decay", "log", "relu"))
        hi, mid = q.sb("hi", [BC3, T], BF16), q.sb("mid", [BC3, T], BF16)
        rest = q.sb("rest", [BC3, T])
        x1_ps, v_ps, dt_ps, bc_ps = (q.ps(n, [P, T]) for n in ("x1_ps", "v_ps", "dt_ps", "bc_ps"))
        w_ready, wbc_ready, padded = q.sem("w_ready"), q.sem("wbc_ready"), q.sem("padded")
        x1_made, v_made, dt_made, bc_made = (q.count(n) for n in ("x1_made", "v_made", "dt_made", "bc_made"))
        x1_copied, v_silu = q.count("x1_copied", 1, 1), q.count("v_silu", 1, 1)
        conv_steps = q.count("conv_steps", 3, 3)
        u_made = q.count("u_made", 1, 1)
        soft_steps = q.count("soft_steps", 3, 3)
        rectified = q.count("rectified", 1, 1)
        dt_done = q.count("dt_done", 1, 1)
        split_steps = q.count("split_steps", 6, 6)
        with nc.Block() as block:

            @block.sync
            def _(sp):
                sp.dma_start(t.ssm_mats[:, :, :], d["ssm_mats"]).then_inc(w_ready, 16)
                sp.dma_start(wbc[:, :], d["wbc"]).then_inc(wbc_ready, 16)
                sp.dma_start(pick[:, :], d["pick"]).then_inc(wbc_ready, 16)

            @block.tensor
            def _(pe):
                pe.wait_ge(w_ready, 16)

                def for_u(b):
                    pe.wait_ge(x1_copied.sem, x1_copied.before(b, 0, 1))
                    product(pe, x1_ps, t.ssm_w["w1"], t.z_t[:, b, :]).then_inc(x1_made.sem, 1)

                def for_v(b):
                    pe.wait_ge(v_silu.sem, v_silu.before(b, 0, 1))
                    product(pe, v_ps, t.ssm_w["v1"], t.z_t[:, b, :]).then_inc(v_made.sem, 1)

                def from_u(b):
                    pe.wait_ge(u_made.sem, u_made.at(b))
                    pe.wait_ge(soft_steps.sem, soft_steps.before(b, 0, 3))
                    pe.wait_ge(rectified.sem, rectified.before(b, 0, 1))
                    product(pe, dt_ps, t.ssm_w["wdt"], t.u_t[:, b, :]).then_inc(dt_made.sem, 1)
                    pe.wait_ge(split_steps.sem, split_steps.before(b, 1, 6))
                    product(pe, bc_ps[0:BC3, :], wbc[:, :], t.u_t[:, b, :]).then_inc(bc_made.sem, 1)

                for_u(0)
                for_v(0)
                pe.wait_ge(wbc_ready, 32)
                with pe.Fori(0, B - 1) as b:
                    for_u(b + 1)
                    from_u(b)
                    for_v(b + 1)
                from_u(B - 1)

            @block.scalar
            def _(act):
                act.sem_inc(x1_copied.sem, 1)
                act.sem_inc(v_silu.sem, 1)
                act.sem_inc(u_made.sem, 1)
                act.sem_inc(soft_steps.sem, soft_steps.start)

                def copy_x1(b):
                    act.wait_ge(x1_made.sem, x1_made.at(b))
                    act.wait_ge(conv_steps.sem, conv_steps.before(b, 2, 3))
                    act.activation(x1[:, 1:T + 1], x1_ps[:, :], ACT.Identity,
                                   bias=t.col("w1_b")).then_inc(x1_copied.sem, 1)

                def silus(b):
                    act.wait_ge(v_made.sem, v_made.at(b))
                    act.activation(t.v_t[:, b, :], v_ps[:, :], ACT.Silu, bias=t.col("v1_b")).then_inc(v_silu.sem, 1)
                    act.wait_ge(conv_steps.sem, conv_steps.at(b, 2))
                    act.activation(t.u_t[:, b, :], y2[:, :], ACT.Silu).then_inc(u_made.sem, 1)

                def softplus(b):
                    act.wait_ge(dt_made.sem, dt_made.at(b))
                    act.activation(size[:, :], dt_ps[:, :], ACT.Abs, bias=t.col("b_dt")).then_inc(soft_steps.sem, 1)
                    act.wait_ge(soft_steps.sem, soft_steps.at(b, 0))
                    act.activation(decay[:, :], size[:, :], ACT.Exp, scale=-1.0).then_inc(soft_steps.sem, 1)
                    act.wait_ge(soft_steps.sem, soft_steps.at(b, 1))
                    act.wait_ge(dt_done.sem, dt_done.before(b, 0, 1))
                    act.activation(log[:, :], decay[:, :], ACT.Ln, bias=1.0).then_inc(soft_steps.sem, 1)

                copy_x1(0)
                silus(0)
                with act.Fori(0, B - 1) as b:
                    copy_x1(b + 1)
                    softplus(b)
                    silus(b + 1)
                softplus(B - 1)

            @block.vector
            def _(dve):
                for c in (conv_steps, rectified, dt_done, split_steps):
                    dve.sem_inc(c.sem, c.start)
                dve.memset(x1[:, 0:1], 0.0)
                dve.memset(x1[:, T + 1:T + 2], 0.0).then_inc(padded, 1)
                dve.wait_ge(padded, 1)

                def convolve(b):
                    dve.wait_ge(x1_copied.sem, x1_copied.at(b))
                    dve.tensor_scalar(y0[:, :], x1[:, 0:T], t.col("conv", 0), None,
                                      ALU.mult).then_inc(conv_steps.sem, 1)
                    dve.wait_ge(conv_steps.sem, conv_steps.at(b, 0))
                    dve.scalar_tensor_tensor(y1[:, :], x1[:, 1:T + 1], t.col("conv", 1), y0[:, :], ALU.mult,
                                             ALU.add).then_inc(conv_steps.sem, 1)
                    dve.wait_ge(conv_steps.sem, conv_steps.at(b, 1))
                    dve.wait_ge(u_made.sem, u_made.before(b, 0, 1))
                    dve.scalar_tensor_tensor(y2[:, :], x1[:, 2:T + 2], t.col("conv", 2), y1[:, :], ALU.mult,
                                             ALU.add).then_inc(conv_steps.sem, 1)

                def split_b_and_c(b):
                    dve.wait_ge(bc_made.sem, bc_made.at(b))
                    dve.tensor_copy(hi[:, :], bc_ps[0:BC3, :]).then_inc(split_steps.sem, 1)
                    dve.wait_ge(split_steps.sem, split_steps.at(b, 0))
                    dve.tensor_tensor(rest[:, :], bc_ps[0:BC3, :], hi[:, :], ALU.subtract).then_inc(split_steps.sem, 1)
                    dve.wait_ge(split_steps.sem, split_steps.at(b, 1))
                    dve.tensor_copy(mid[:, :], rest[:, :]).then_inc(split_steps.sem, 1)
                    dve.wait_ge(split_steps.sem, split_steps.at(b, 2))
                    dve.tensor_tensor(t.bc[:, b, :], rest[:, :], mid[:, :], ALU.subtract).then_inc(split_steps.sem, 1)
                    dve.wait_ge(split_steps.sem, split_steps.at(b, 3))
                    dve.tensor_scalar(t.bc[0:32, b, :], hi[0:32, :], 1.0, None, ALU.mult).then_inc(split_steps.sem, 1)
                    dve.tensor_scalar(t.bc[32:64, b, :], mid[32:64, :], 1.0, None, ALU.mult).then_inc(split_steps.sem, 1)

                def rectify(b):
                    dve.wait_ge(soft_steps.sem, soft_steps.at(b, 0))
                    dve.wait_ge(dt_done.sem, dt_done.before(b, 0, 1))
                    dve.tensor_scalar(relu[:, :], dt_ps[:, :], t.col("b_dt"), 0.0, ALU.add,
                                      ALU.max).then_inc(rectified.sem, 1)

                def steps_of_time(b):
                    dve.wait_ge(rectified.sem, rectified.at(b))
                    dve.wait_ge(soft_steps.sem, soft_steps.at(b, 2))
                    dve.tensor_tensor(t.dt_t[:, b, :], relu[:, :], log[:, :], ALU.add).then_inc(dt_done.sem, 1)

                convolve(0)
                dve.wait_ge(wbc_ready, 32)
                dve.tensor_copy(t.sel[:, :, :],
                                pick[:, :].rearrange("p (n o) -> p n o", o=1).broadcast_to([BC3, 2 * NS, P]))
                with dve.Fori(0, B - 1) as b:
                    convolve(b + 1)
                    rectify(b)
                    split_b_and_c(b)
                    steps_of_time(b)
                rectify(B - 1)
                split_b_and_c(B - 1)
                steps_of_time(B - 1)

            @block.gpsimd
            def _(pool):
                with pool.Fori(0, B) as b:
                    pool.wait_ge(dt_done.sem, dt_done.at(b))
                    pool.sem_inc(padded, 1)
                    pool.tensor_tensor(t.du_t[:, b, :], t.dt_t[:, b, :], t.u_t[:, b, :], ALU.mult)


def pipelined(eng, first, per, body):
    for n in range(first):
        body(0, n)
    with eng.Fori(0, B - 1) as b:
        for n in range(first, first + per):
            body(b, n)
    for n in range(first, first + per):
        body(B - 1, n)


def there(b, n, per):
    return n < per or not isinstance(b, int) or b < B - 1


def selective_scan(t):
    nc = t.nc
    LAG = 3
    TAIL = NS + LAG + 1
    with Stage(nc, "scan") as s:
        a_neg = s.sb("a_neg", [P, NS])
        dt_b = s.sb("dt_b", [P, T])
        decay = s.sb("decay", [P, 4, T])
        drive = s.sb("drive", [P, 2, T])
        state = s.sb("state", [P, 2, T])
        c_rep = s.sb("c_rep", [P, 4, T])
        hc = s.sb("hc", [P, 4, T])
        y_sb = s.sb("y_sb", [P, T])
        yv = s.sb("yv", [P, T])
        b_ps = [s.ps(f"b_ps{k}", [P, T]) for k in range(2)]
        c_ps, y_ps = (s.ps(n, [P, T]) for n in ("c_ps", "y_ps"))
        a_steps = s.sem("a_steps")
        b_spread = s.count("b_spread", NS)
        c_spread = s.count("c_spread", NS)
        summed = s.count("summed", NS, 4)
        dt_staged = s.count("dt_staged")
        decayed = s.count("decayed", NS, 1)
        c_copied = s.count("c_copied", NS, 1)
        driven = s.count("driven", NS, 2)
        scanned = s.count("scanned", NS, 4)
        weighed = s.count("weighed", NS, 4)
        y_steps = s.count("y_steps", 2, 2)
        projected = s.count("projected", 1, 1)
        added = s.count("added", 1, 1)
        with nc.Block() as block:

            @block.tensor
            def _(pe):
                pe.sem_inc(summed.sem, summed.start)
                pe.sem_inc(projected.sem, projected.start)

                def spread(b, n):
                    at, m = b + n // NS, n % NS
                    pe.wait_ge(driven.sem, driven.before(b, n, 2))
                    if n == TAIL + 1:
                        pe.wait_ge(added.sem, added.at(b))
                    product(pe, b_ps[n % 2], t.sel[:, m, :], t.bc[:, at, :]).then_inc(b_spread.sem, 1)
                    pe.wait_ge(c_copied.sem, c_copied.before(b, n, 1))
                    product(pe, c_ps, t.sel[:, NS + m, :], t.bc[:, at, :]).then_inc(c_spread.sem, 1)

                def add_state(b, n):
                    pe.wait_ge(weighed.sem, weighed.at(b, n))
                    if n % NS == 0:
                        pe.wait_ge(y_steps.sem, y_steps.before(b, 2 * (n // NS), 2))
                    product(pe, y_ps, t.ident[:, :], hc[:, n % 4, :], start=n % NS == 0,
                            stop=n % NS == NS - 1).then_inc(summed.sem, 1)

                def body(b, n):
                    steps = [(spread, n), (add_state, n - LAG)]
                    if n == TAIL + 1:
                        steps.reverse()
                    for step, m in steps:
                        if m >= 0 and there(b, m, NS):
                            step(b, m)
                    if n == TAIL:
                        pe.wait_ge(y_steps.sem, y_steps.at(b, 1))
                        if there(b, n, NS):
                            pe.wait_ge(driven.sem, driven.at(b, n - 1))
                        product(pe, b_ps[(TAIL + 1) % 2], t.ssm_w["w2"], yv[:, :]).then_inc(projected.sem, 1)

                pipelined(pe, TAIL + 2 - NS, NS, body)

            @block.scalar
            def _(act):
                act.sem_inc(c_copied.sem, c_copied.start)
                act.activation(a_neg[:, :], t.col("a_log", 0, NS), ACT.Exp).then_inc(a_steps, 1)
                act.wait_ge(a_steps, 1)
                act.mul(a_neg[:, :], a_neg[:, :], -1.0).then_inc(a_steps, 1)
                act.wait_ge(a_steps, 2)
                act.sem_inc(decayed.sem, decayed.start)
                with act.Fori(0, B) as b:
                    act.wait_ge(decayed.sem, decayed.before(b, 0, 1))
                    act.activation(dt_b[:, :], t.dt_t[:, b, :], ACT.Copy).then_inc(dt_staged.sem, 1)
                    act.wait_ge(dt_staged.sem, dt_staged.at(b))
                    for n in range(NS):
                        act.wait_ge(scanned.sem, scanned.before(b, n, 4))
                        act.activation(decay[:, n % 4, :], dt_b[:, :], ACT.Exp,
                                       scale=a_neg[:, n:n + 1]).then_inc(decayed.sem, 1)
                        act.wait_ge(c_spread.sem, c_spread.at(b, n))
                        act.wait_ge(weighed.sem, weighed.before(b, n, 4))
                        act.activation(c_rep[:, n % 4, :], c_ps[:, :], ACT.Copy).then_inc(c_copied.sem, 1)

            @block.vector
            def _(dve):
                dve.sem_inc(driven.sem, driven.start)
                dve.sem_inc(scanned.sem, scanned.start)
                dve.sem_inc(y_steps.sem, y_steps.start)
                dve.sem_inc(added.sem, added.start)

                def body(b, n):
                    if n == TAIL - 1:
                        dve.wait_ge(summed.sem, summed.at(b, NS - 1))
                        dve.scalar_tensor_tensor(y_sb[:, :], t.u_t[:, b, :], t.col("d_skip"), y_ps[:, :], ALU.mult,
                                                 ALU.add).then_inc(y_steps.sem, 1)
                    if there(b, n, NS):
                        dve.wait_ge(b_spread.sem, b_spread.at(b, n))
                        dve.wait_ge(scanned.sem, scanned.before(b, n, 2))
                        dve.tensor_tensor(drive[:, n % 2, :], b_ps[n % 2][:, :], t.du_t[:, b + n // NS, :],
                                          ALU.mult).then_inc(driven.sem, 1)
                    k = n - 1
                    if k >= 0 and there(b, k, NS):
                        dve.wait_ge(driven.sem, driven.at(b, k))
                        dve.wait_ge(decayed.sem, decayed.at(b, k))
                        dve.wait_ge(weighed.sem, weighed.before(b, k, 2))
                        dve.tensor_tensor_scan(state[:, k % 2, :], decay[:, k % 4, :], drive[:, k % 2, :], 0.0,
                                               ALU.mult, ALU.add).then_inc(scanned.sem, 1)
                    if n == TAIL - 1:
                        dve.wait_ge(y_steps.sem, y_steps.at(b, 0))
                        dve.wait_ge(projected.sem, projected.before(b, 0, 1))
                        dve.tensor_tensor(yv[:, :], y_sb[:, :], t.v_t[:, b, :], ALU.mult).then_inc(y_steps.sem, 1)
                    if n == TAIL:
                        dve.wait_ge(projected.sem, projected.at(b))
                        dve.scalar_tensor_tensor(t.x_t[:, b, :], b_ps[(TAIL + 1) % 2][:, :], t.col("w2_b"),
                                                 t.x_t[:, b, :], ALU.add, ALU.add).then_inc(added.sem, 1)

                pipelined(dve, TAIL + 2 - NS, NS, body)

            @block.gpsimd
            def _(pool):
                pool.sem_inc(weighed.sem, weighed.start)
                with pool.Fori(0, B) as b:
                    for n in range(NS):
                        pool.wait_ge(scanned.sem, scanned.at(b, n))
                        pool.wait_ge(c_copied.sem, c_copied.at(b, n))
                        pool.wait_ge(summed.sem, summed.before(b, n, 4))
                        pool.tensor_tensor(hc[:, n % 4, :], state[:, n % 2, :], c_rep[:, n % 4, :],
                                           ALU.mult).then_inc(weighed.sem, 1)


def ffn(t, name):
    nc, d = t.nc, t.dram
    with Stage(nc, name) as s:
        M = 3 * FC
        LAG = 2
        x_half = s.sb("x_half", [P, 2, HALF])
        stats, mv = s.sb("stats", [P, 2, NT, 6]), s.sb("mv", [P, 2, NT, 2])
        veps, rstd = s.sb("veps", [P, 2, NT]), s.sb("rstd", [P, 2, NT])
        z_tok = s.sb("z_tok", [P, 2, HALF])
        z_hi, z_lo = s.sb("z_hi", [P, B, T], F16), s.sb("z_lo", [P, B, T], F16)
        z_sum = s.sb("z_sum", [P, 2])
        logits, best, which = s.sb("logits", [1, E]), s.sb("best", [1, 8]), s.sb("which", [1, 8], U32)
        gap, th, share_row = s.sb("gap", [1, 1]), s.sb("th", [1, 1]), s.sb("share_row", [1, 2])
        share = s.sb("share", [P, 2])
        w1m, w2m = s.sb("w1m", [P, F]), s.sb("w2m", [P, FC * P])
        w1p = [[s.sb(f"w1p{k}{i}", [P, F], F16) for i in range(2)] for k in range(3)]
        w2p = [[s.sb(f"w2p{k}{i}", [P, FC * P], F16) for i in range(2)] for k in range(3)]
        w1e, w2e = ([s.sb(f"{n}{k}", [P, F]) for k in range(2)] for n in ("w1e", "w2e"))
        w1x = [s.sb(f"w1x{k}", [P, F]) for k in range(2)]
        w2x = [s.sb(f"w2x{k}", [P, F]) for k in range(2)]
        be = [s.sb(f"be{k}", [P, FC + 1]) for k in range(2)]
        bias = s.sb("bias", [P, 3])
        hid = s.sb("hid", [P, 2, T])
        hid_hi, hid_lo = s.sb("hid_hi", [P, 3, T], F16), s.sb("hid_lo", [P, 3, T], F16)
        y = s.sb("y", [P, T])
        h_ps = [s.ps(f"h_ps{k}", [P, T]) for k in range(2)]
        o_ps = s.ps("o_ps", [P, T])
        tok_ps, z_ps = (s.ps(n, [P, HALF]) for n in ("tok_ps", "z_ps"))

        def x_place(b, k):
            return (tok_ps, z_ps if isinstance(b, int) and b == 0 else tok_ps)[k]

        def z_place(b, k):
            return h_ps[0][:, HALVES[k]] if isinstance(b, int) and b == 0 else (z_ps, tok_ps)[k]


        x_staged = s.count("x_staged", 2)
        turned = s.count("turned", 2, 2)
        got_mv = s.count("got_mv", 2)
        rstd_steps = s.count("rstd_steps", 4)
        normed = s.count("normed", 2, 2)
        z_turned = s.count("z_turned", 2, 2)
        z_copied = s.count("z_copied", 2)
        z_rest = s.count("z_rest", 2, 1)
        scored = s.count("scored")
        gate_steps = s.count("gate_steps", 7, 7)
        tanh_done = s.count("tanh_done")
        spread = s.count("spread")
        m_loaded, m_steps = s.sem("m_loaded"), s.sem("m_steps")
        e_loaded, be_loaded = ([s.sem(f"{n}{k}") for k in range(2)] for n in ("e_loaded", "be_loaded"))
        loading, seen = s.sem("loading"), s.sem("seen")
        upped = s.count("upped", M, M)
        gelued = s.count("gelued", M, 2)
        hid_split = s.count("hid_split", 2 * M, 4)
        downed = s.count("downed", M, M)
        weighed = s.count("weighed", 2, 2)
        w_split = s.count("w_split", 2 * 3, 6)
        biased = s.count("biased", 3, 3)
        y_made = s.count("y_made", 1, 1)
        added = s.count("added", 1, 1)
        with nc.Block() as block:

            @block.sync
            def _(sp):
                sp.dma_start(w1m[:, :], d["w1m"]).then_inc(m_loaded, 16)
                sp.dma_start(w2m[:, :], d["w2m"]).then_inc(m_loaded, 16)
                with sp.Fori(0, B) as b:
                    sp.wait_ge(gate_steps.sem, gate_steps.at(b, 2))
                    sp.wait_ge(w_split.sem, w_split.before(b, 5, 6))
                    sp.sem_inc(loading, 1)
                    for k in range(2):
                        e = sp.value_load(which[0:1, k:k + 1], min_val=0, max_val=E - 1)
                        sp.dma_start(w1e[k][:, :], d["w1e"][e]).then_inc(e_loaded[k], 16)
                        sp.dma_start(w2e[k][:, :], d["w2e"][e]).then_inc(e_loaded[k], 16)
                    sp.wait_ge(added.sem, added.before(b, 0, 1))
                    sp.sem_inc(loading, 1)
                    for k in range(2):
                        e = sp.value_load(which[0:1, k:k + 1], min_val=0, max_val=E - 1)
                        sp.dma_start(be[k][:, :], d["be"][e]).then_inc(be_loaded[k], 16)

            @block.gpsimd
            def _(pool):
                pool.sem_inc(w_split.sem, w_split.start)
                pool.sem_inc(added.sem, added.start)

                def deviation(b, k):
                    pool.wait_ge(got_mv.sem, got_mv.at(b, k))
                    pool.tensor_tensor(veps[:, k, :], mv[:, k, :, 1], t.eps[:, :], ALU.add).then_inc(rstd_steps.sem, 1)
                    pool.wait_ge(rstd_steps.sem, rstd_steps.at(b, 2 * k))
                    pool.tensor_tensor(rstd[:, k, :], veps[:, k, :], t.minus_half[:, 0:NT],
                                       ALU.pow).then_inc(rstd_steps.sem, 1)

                def low_parts(b, k):
                    pool.wait_ge(w_split.sem, w_split.before(b, 3 * k + 1, 6))
                    pool.wait_ge(weighed.sem, weighed.at(b, k))
                    pool.tensor_tensor(w1x[k][:, :], w1e[k][:, :], t.scale[:, :], ALU.mult).then_inc(w_split.sem, 1)
                    pool.wait_ge(w_split.sem, w_split.at(b, 3 * k))
                    pool.wait_ge(downed.sem, downed.before(b, (k + 2) * FC - 1, M))
                    pool.tensor_tensor(w1p[k + 1][1][:, :], w1x[k][:, :], w1p[k + 1][0][:, :],
                                       ALU.subtract).then_inc(w_split.sem, 1)
                    pool.tensor_tensor(w2p[k + 1][1][:, :], w2x[k][:, :], w2p[k + 1][0][:, :],
                                       ALU.subtract).then_inc(w_split.sem, 1)

                def body(b, last):
                    for k in range(2):
                        low_parts(b, k)
                        if not last:
                            deviation(b + 1, k)
                    pool.wait_ge(y_made.sem, y_made.at(b))
                    pool.sem_inc(seen, 1)
                    pool.tensor_tensor(t.x_t[:, b, :], t.x_t[:, b, :], y[:, :], ALU.add).then_inc(added.sem, 1)

                for k in range(2):
                    deviation(0, k)
                with pool.Fori(0, B - 1) as b:
                    body(b, False)
                body(B - 1, True)

            @block.tensor
            def _(pe):
                pe.sem_inc(turned.sem, turned.start)
                pe.sem_inc(z_turned.sem, z_turned.start)
                pe.sem_inc(upped.sem, upped.start)
                pe.sem_inc(downed.sem, downed.start)

                def turn_x(b, k):
                    pe.wait_ge(x_staged.sem, x_staged.at(b, k))
                    if k == 0:
                        pe.wait_ge(gate_steps.sem, gate_steps.before(b, 6, 7))
                    elif x_place(b, 1) is tok_ps:
                        pe.wait_ge(normed.sem, normed.at(b, 0))
                    for j in range(NT):
                        cols = slice(j * P, (j + 1) * P)
                        last = pe.transpose(x_place(b, k)[:, cols], x_half[:, k, cols], t.ident[:, :])
                    last.then_inc(turned.sem, 1)

                def turn_z(b, k):
                    pe.wait_ge(normed.sem, normed.at(b, k))
                    if k == 0:
                        pe.wait_ge(gate_steps.sem, gate_steps.before(b, 0, 7))
                    for j in range(NT):
                        cols = slice(j * P, (j + 1) * P)
                        last = pe.transpose(z_place(b, k)[:, cols], z_tok[:, k, cols], t.ident[:, :])
                    last.then_inc(z_turned.sem, 1)

                def gate(b):
                    pe.wait_ge(z_rest.sem, z_rest.at(b, 0))
                    pe.wait_ge(z_copied.sem, z_copied.at(b, 1))
                    for k in range(2):
                        last = pe.matmul(z_ps[0:1, 0:E], z_sum[:, k:k + 1], t.w_gate[:, :], start=k == 0,
                                         stop=k == 1)
                    last.then_inc(scored.sem, 1)

                def spread_shares(b):
                    pe.wait_ge(z_rest.sem, z_rest.at(b, 1))
                    pe.wait_ge(gate_steps.sem, gate_steps.at(b, 5))
                    pe.matmul(tok_ps[:, 0:2], t.ones_row[:, :], share_row[:, :], start=True,
                              stop=True).then_inc(spread.sem, 1)

                STEPS = {2: ((turn_x, 0),), 5: ((turn_x, 1), (turn_z, 0)), 8: ((turn_z, 1),), 10: ((gate,),),
                         13: ((spread_shares,),)}

                def body(b, m):
                    if there(b, m, M):
                        k, c = divmod(m % M, FC)
                        if k and c == 0:
                            pe.wait_ge(w_split.sem, w_split.at(b, 3 * k - 2))
                        if m == 0:
                            pe.wait_ge(m_steps, 6)
                        pe.wait_ge(z_rest.sem, z_rest.at(b + m // M, 1))
                        pe.wait_ge(gelued.sem, gelued.before(b, m, 2))
                        w_hi, w_lo = (w[:, c * P:(c + 1) * P] for w in w1p[k])
                        product_of_parts(pe, h_ps[m % 2], w_hi, w_lo, z_hi[:, b + m // M, :],
                                         z_lo[:, b + m // M, :]).then_inc(upped.sem, 1)
                    n = m - LAG
                    if n >= 0:
                        k, c = divmod(n, FC)
                        if k and c == 0:
                            pe.wait_ge(w_split.sem, w_split.at(b, 3 * k - 1))
                        if n == 0:
                            pe.wait_ge(y_made.sem, y_made.before(b, 0, 1))
                        pe.wait_ge(hid_split.sem, hid_split.at(b, 2 * n + 1))
                        w_hi, w_lo = (w[:, c * P:(c + 1) * P] for w in w2p[k])
                        product_of_parts(pe, o_ps, w_hi, w_lo, hid_hi[:, n % 3, :], hid_lo[:, n % 3, :],
                                         start=n == 0, stop=n == M - 1).then_inc(downed.sem, 1)
                    if m in STEPS and there(b, M, M):
                        for step, *k in STEPS[m]:
                            step(b + 1, *k)

                for turn in (turn_x, turn_z):
                    for k in range(2):
                        turn(0, k)
                gate(0)
                body(0, 0)
                spread_shares(0)
                body(0, 1)
                with pe.Fori(0, B - 1) as b:
                    for m in range(LAG, M + LAG):
                        body(b, m)
                for m in range(LAG, M + LAG):
                    body(B - 1, m)

            @block.scalar
            def _(act):
                act.sem_inc(gelued.sem, gelued.start)

                def stage_x(b):
                    for k in range(2):
                        act.wait_ge(turned.sem, turned.before(b, k, 2))
                        act.activation(x_half[:, k, :], t.x_t[:, b, HALVES[k]], ACT.Copy).then_inc(x_staged.sem, 1)

                def high_part(b, k):
                    act.wait_ge(z_turned.sem, z_turned.at(b, k))
                    act.activation(z_hi[:, b, HALVES[k]], z_place(b, k)[:, :], ACT.Copy,
                                   accum_out=z_sum[:, k:k + 1]).then_inc(z_copied.sem, 1)

                def shares(b):
                    act.wait_ge(gate_steps.sem, gate_steps.at(b, 3))
                    act.activation(th[:, :], gap[:, :], ACT.Tanh, scale=0.5).then_inc(tanh_done.sem, 1)

                STEPS = {1: (stage_x,), 6: (high_part, 0), 9: (high_part, 1), 11: (shares,)}

                def body(b, last):
                    for m in range(M):
                        k, c = divmod(m, FC)
                        act.wait_ge(upped.sem, upped.at(b, m))
                        act.wait_ge(hid_split.sem, hid_split.before(b, 2 * m + 1, 4))
                        if k and c == 0:
                            act.wait_ge(be_loaded[k - 1], b * 16 + 16)
                        b1 = t.col("b1m", c) if k == 0 else be[k - 1][:, c:c + 1]
                        act.activation(hid[:, m % 2, :], h_ps[m % 2][:, :], ACT.Gelu_apprx_tanh,
                                       bias=b1, scale=1.0 / WS).then_inc(gelued.sem, 1)
                        if m in STEPS and not last:
                            STEPS[m][0](b + 1, *STEPS[m][1:])

                stage_x(0)
                high_part(0, 0)
                high_part(0, 1)
                shares(0)
                with act.Fori(0, B - 1) as b:
                    body(b, False)
                body(B - 1, True)

            @block.vector
            def _(dve):
                for c in (normed, z_rest, gate_steps, weighed, biased, hid_split, y_made):
                    dve.sem_inc(c.sem, c.start)

                def statistics(b, k):
                    dve.wait_ge(turned.sem, turned.at(b, k))
                    for j in range(NT):
                        dve.bn_stats(stats[:, k, j, :], x_place(b, k)[:, j * P:(j + 1) * P])
                    dve.drain()
                    for j in range(NT):
                        last = dve.bn_aggr(mv[:, k, j, :], stats[:, k, j, :])
                    last.then_inc(got_mv.sem, 1)

                def normalise(b, k):
                    dve.wait_ge(rstd_steps.sem, rstd_steps.at(b, 2 * k + 1))
                    dve.wait_ge(z_turned.sem, z_turned.before(b, k, 2))
                    for j in range(NT):
                        cols = slice(j * P, (j + 1) * P)
                        last = dve.tensor_scalar(z_tok[:, k, cols], x_place(b, k)[:, cols], mv[:, k, j, 0:1],
                                                 rstd[:, k, j:j + 1], ALU.subtract, ALU.mult)
                    last.then_inc(normed.sem, 1)

                def low_part(b, k):
                    dve.wait_ge(z_copied.sem, z_copied.at(b, k))
                    dve.tensor_tensor(z_lo[:, b, HALVES[k]], z_place(b, k)[:, :], z_hi[:, b, HALVES[k]],
                                      ALU.subtract).then_inc(z_rest.sem, 1)

                def choose(b):
                    dve.wait_ge(scored.sem, scored.at(b))
                    dve.scalar_tensor_tensor(logits[:, :], z_ps[0:1, 0:E], 1.0 / T, t.b_gate[:, :], ALU.mult,
                                             ALU.add).then_inc(gate_steps.sem, 1)
                    dve.drain()
                    dve.max(best[:, :], logits[:, :]).then_inc(gate_steps.sem, 1)
                    dve.drain()
                    dve.max_index(which[:, :], best[:, :], logits[:, :]).then_inc(gate_steps.sem, 1)
                    dve.tensor_tensor(gap[:, :], best[:, 0:1], best[:, 1:2], ALU.subtract).then_inc(gate_steps.sem, 1)

                def share_rows(b):
                    dve.wait_ge(tanh_done.sem, tanh_done.at(b))
                    for k in range(2):
                        dve.tensor_scalar(share_row[:, k:k + 1], th[:, :], (WS / 2, -WS / 2)[k], WS / 2, ALU.mult,
                                          ALU.add).then_inc(gate_steps.sem, 1)

                def take_shares(b):
                    dve.wait_ge(spread.sem, spread.at(b))
                    dve.tensor_scalar(share[:, :], tok_ps[:, 0:2], t.blend[:, 1:2], None,
                                      ALU.mult).then_inc(gate_steps.sem, 1)

                def dense_weights():
                    dve.wait_ge(m_loaded, 32)
                    dve.tensor_scalar(w1m[:, :], w1m[:, :], WS, None, ALU.mult).then_inc(m_steps, 1)
                    dve.tensor_scalar(w2m[:, :], w2m[:, :], t.blend[:, 2:3], None, ALU.mult).then_inc(m_steps, 1)
                    dve.wait_ge(m_steps, 2)
                    for w, (hi, lo) in ((w1m, w1p[0]), (w2m, w2p[0])):
                        dve.tensor_scalar(hi[:, :], w[:, :], 1.0, None, ALU.mult).then_inc(m_steps, 1)
                    dve.wait_ge(m_steps, 4)
                    for w, (hi, lo) in ((w1m, w1p[0]), (w2m, w2p[0])):
                        dve.tensor_tensor(lo[:, :], w[:, :], hi[:, :], ALU.subtract).then_inc(m_steps, 1)

                def high_parts(b, k):
                    dve.wait_ge(e_loaded[k], b * 32 + 32)
                    dve.wait_ge(w_split.sem, w_split.before(b, 3 * k + 2, 6))
                    dve.wait_ge(downed.sem, downed.before(b, (k + 2) * FC - 1, M))
                    dve.wait_ge(gate_steps.sem, gate_steps.at(b, 6))
                    dve.tensor_scalar(w1p[k + 1][0][:, :], w1e[k][:, :], WS, None, ALU.mult)
                    dve.tensor_scalar(w2x[k][:, :], w2e[k][:, :], share[:, k:k + 1], None, ALU.mult)
                    dve.tensor_scalar(w2p[k + 1][0][:, :], w2e[k][:, :], share[:, k:k + 1], None,
                                      ALU.mult).then_inc(weighed.sem, 1)

                def output_bias(b, k):
                    if k == 0:
                        dve.wait_ge(y_made.sem, y_made.before(b, 0, 1))
                        dve.tensor_scalar(bias[:, 0:1], t.col("b2m"), t.blend[:, 2:3], None,
                                          ALU.mult).then_inc(biased.sem, 1)
                    dve.wait_ge(be_loaded[k], b * 16 + 16)
                    dve.wait_ge(biased.sem, biased.at(b, k))
                    dve.scalar_tensor_tensor(bias[:, k + 1:k + 2], be[k][:, FC:FC + 1], share[:, k:k + 1],
                                             bias[:, k:k + 1], ALU.mult, ALU.add).then_inc(biased.sem, 1)

                OWN_STEPS = {2: (high_parts, 0), 5: (high_parts, 1), 7: (output_bias, 0), 8: (output_bias, 1)}
                NEXT_STEPS = {2: ((statistics, 0),), 3: ((normalise, 0),), 5: ((statistics, 1),),
                              6: ((normalise, 1),), 7: ((low_part, 0),), 10: ((low_part, 1), (choose,)),
                              11: ((share_rows,),), 13: ((take_shares,),)}

                def body(b, m):
                    if m == M + LAG - 1:
                        dve.wait_ge(biased.sem, biased.at(b, 2))
                        dve.wait_ge(downed.sem, downed.at(b, M - 1))
                        dve.wait_ge(added.sem, added.before(b, 0, 1))
                        dve.tensor_scalar(y[:, :], o_ps[:, :], bias[:, 2:3], 1.0 / WS, ALU.add,
                                          ALU.mult).then_inc(y_made.sem, 1)
                    if m in OWN_STEPS:
                        OWN_STEPS[m][0](b, *OWN_STEPS[m][1:])
                    if there(b, m, M):
                        dve.wait_ge(gelued.sem, gelued.at(b, m))
                        dve.wait_ge(downed.sem, downed.before(b, m, 3))
                        dve.tensor_copy(hid_hi[:, m % 3, :], hid[:, m % 2, :]).then_inc(hid_split.sem, 1)
                        dve.wait_ge(hid_split.sem, hid_split.at(b, 2 * m))
                        dve.tensor_tensor(hid_lo[:, m % 3, :], hid[:, m % 2, :], hid_hi[:, m % 3, :],
                                          ALU.subtract).then_inc(hid_split.sem, 1)
                    if m in NEXT_STEPS and there(b, M, M):
                        for step, *k in NEXT_STEPS[m]:
                            step(b + 1, *k)

                for step in (statistics, normalise):
                    for k in range(2):
                        step(0, k)
                dense_weights()
                for k in range(2):
                    low_part(0, k)
                choose(0)
                share_rows(0)
                body(0, 0)
                take_shares(0)
                body(0, 1)
                with dve.Fori(0, B - 1) as b:
                    for m in range(LAG, M + LAG):
                        body(b, m)
                for m in range(LAG, M + LAG):
                    body(B - 1, m)


def retention(t):
    nc, d = t.nc, t.dram
    SUM_AT = 7
    with Stage(nc, "ret") as q:
        x_half = q.sb("x_half", [P, 2, HALF])
        stats, mv = q.sb("stats", [P, 2, NT, 6]), q.sb("mv", [P, 2, NT, 2])
        veps, rstd = q.sb("veps", [P, 2, NT]), q.sb("rstd", [P, 2, NT])
        z_tok = q.sb("z_tok", [P, 2, HALF])
        z_hi, z_lo = q.sb("z_hi", [P, B, T], F16), q.sb("z_lo", [P, B, T], F16)
        W = len(RET_MATS) + HD
        w_all = q.sb("w_all", [P, W, P])
        w_hi, w_lo = q.sb("w_hi", [P, W, P], F16), q.sb("w_lo", [P, W, P], F16)
        head_sum = q.sb("head_sum", [P, 2, 2 * H])
        bg_neg = q.sb("bg_neg", [P, 1])
        bsk_small = q.sb("bsk_small", [P, 1])
        bsv_large = q.sb("bsv_large", [P, HD])
        k_sb, q_sb, g_sb = (q.sb(n, [P, T]) for n in ("k_sb", "q_sb", "g_sb"))
        kv = q.sb("kv", [P, 2, T])
        mem = q.sb("mem", [P, 2, T])
        qm = q.sb("qm", [P, HD, T])
        a_ps = q.ps("a_ps", [P, T])
        v_ps = [q.ps(f"v_ps{k}", [P, T]) for k in range(2)]
        h_ps = q.ps("h_ps", [P, T])
        w_loaded, w_steps = q.sem("w_loaded"), q.sem("w_steps")
        x_staged = q.count("x_staged", 2)
        turned = q.count("turned", 2, 2)
        got_mv = q.count("got_mv", 2)
        rstd_steps = q.count("rstd_steps", 4)
        normed = q.count("normed", 2, 2)
        z_turned = q.count("z_turned", 2, 2)
        z_copied = q.count("z_copied", 2)
        z_rest = q.count("z_rest", 2)
        made = q.count("made", 4, 4)
        copied = q.count("copied", 4, 4)
        v_made = q.count("v_made", HD)
        kv_done = q.count("kv_done", HD, 2)
        scanned = q.count("scanned", HD, HD)
        weighed = q.count("weighed", HD, HD)
        summed = q.count("summed", 2, 2)
        h_copied = q.count("h_copied", 1, 1)
        with nc.Block() as block:

            @block.sync
            def _(sp):
                sp.dma_start(w_all[:, 0:len(RET_MATS), :], d["ret_mats"]).then_inc(w_loaded, 16)
                sp.dma_start(w_all[:, len(RET_MATS):W, :], d["wsv"]).then_inc(w_loaded, 16)
                sp.dma_start(head_sum[:, :, :], d["head_sum"]).then_inc(w_loaded, 16)
                sp.wait_ge(w_loaded, 48)

            @block.tensor
            def _(pe):
                for c in (made, summed, turned, z_turned):
                    pe.sem_inc(c.sem, c.start)

                def turn_x(b):
                    for k in range(2):
                        pe.wait_ge(x_staged.sem, x_staged.at(b, k))
                        pe.wait_ge(copied.sem, copied.before(b, 0, 1))
                        for j in range(k * NT, (k + 1) * NT):
                            last = pe.transpose(a_ps[:, j * P:(j + 1) * P], x_half[:, k, (j % NT) * P:(j % NT + 1) * P],
                                                t.ident[:, :])
                        last.then_inc(turned.sem, 1)

                def turn_z(b):
                    for k in range(2):
                        pe.wait_ge(normed.sem, normed.at(b, k))
                        for j in range(k * NT, (k + 1) * NT):
                            last = pe.transpose(a_ps[:, j * P:(j + 1) * P], z_tok[:, k, (j % NT) * P:(j % NT + 1) * P],
                                                t.ident[:, :])
                        last.then_inc(z_turned.sem, 1)

                def of_z(b, out, i):
                    return product_of_parts(pe, out, w_hi[:, i, :], w_lo[:, i, :], z_hi[:, b, :], z_lo[:, b, :])

                def whole_batch(b, i, name):
                    pe.wait_ge(z_rest.sem, z_rest.at(b, 1))
                    pe.wait_ge(copied.sem, copied.before(b, i, 1))
                    of_z(b, a_ps, RET_MATS.index(name)).then_inc(made.sem, 1)

                def v_by_tokens(b):
                    pe.wait_ge(copied.sem, copied.before(b, 3, 1))
                    wv = RET_MATS.index("wv")
                    for j in range(TT):
                        cols = slice(j * P, (j + 1) * P)
                        for i, (z, w) in enumerate(((z_hi, w_hi), (z_hi, w_lo), (z_lo, w_hi))):
                            last = pe.matmul(a_ps[:, cols], z[:, b, cols], w[:, wv, :], start=i == 0, stop=i == 2)
                    last.then_inc(made.sem, 1)

                def body(b, n):
                    if there(b, n, HD):
                        at, m = b + n // HD, n % HD
                        if m == 0:
                            whole_batch(at, 0, "wsk")
                        pe.wait_ge(kv_done.sem, kv_done.before(b, n, 2))
                        of_z(at, v_ps[n % 2], len(RET_MATS) + m).then_inc(v_made.sem, 1)
                        if m == 0:
                            whole_batch(at, 1, "wg")
                        if m == 1:
                            whole_batch(at, 2, "wsq")
                        if m == 3:
                            v_by_tokens(at)
                    if n == 4 and there(b, HD, HD):
                        turn_x(b + 1)
                    if n == 7 and there(b, HD, HD):
                        turn_z(b + 1)
                    if n in (SUM_AT, SUM_AT + 4):
                        odd = n // (SUM_AT + 4)
                        pe.wait_ge(weighed.sem, weighed.at(b, 4 * odd + 3))
                        if not odd:
                            pe.wait_ge(h_copied.sem, h_copied.before(b, 0, 1))
                        for h in HALVES:
                            for c in range(4):
                                last = pe.matmul(h_ps[32 * c:32 * c + 32, h], head_sum[:, odd, :],
                                                 qm[:, 4 * odd + c, h], start=not odd, stop=bool(odd))
                        last.then_inc(summed.sem, 1)

                turn_x(0)
                turn_z(0)
                pe.wait_ge(w_steps, 2)
                pipelined(pe, SUM_AT + 5 - HD, HD, body)

            @block.scalar
            def _(act):
                act.sem_inc(copied.sem, copied.start)
                act.sem_inc(h_copied.sem, h_copied.start)

                def stage_x(b):
                    for k in range(2):
                        act.wait_ge(turned.sem, turned.before(b, k, 2))
                        act.activation(x_half[:, k, :], t.x_t[:, b, HALVES[k]], ACT.Copy).then_inc(x_staged.sem, 1)

                def high_parts(b):
                    for k in range(2):
                        act.wait_ge(z_turned.sem, z_turned.at(b, k))
                        act.activation(z_hi[:, b, HALVES[k]], a_ps[:, HALVES[k]], ACT.Copy).then_inc(z_copied.sem, 1)

                def inputs(b):
                    act.wait_ge(made.sem, made.at(b, 0))
                    act.wait_ge(kv_done.sem, kv_done.before(b, 1, 2))
                    act.activation(k_sb[:, :], a_ps[:, :], ACT.Identity, bias=bsk_small[:, 0:1],
                                   scale=1.0 / WS ** 2).then_inc(copied.sem, 1)
                    act.wait_ge(made.sem, made.at(b, 1))
                    act.wait_ge(scanned.sem, scanned.before(b, HD - 1, HD))
                    act.activation(g_sb[:, :], a_ps[:, :], ACT.Sigmoid, bias=bg_neg[:, 0:1],
                                   scale=-1.0 / WS).then_inc(copied.sem, 1)
                    act.wait_ge(made.sem, made.at(b, 2))
                    act.wait_ge(weighed.sem, weighed.before(b, HD - 1, HD))
                    act.activation(q_sb[:, :], a_ps[:, :], ACT.Identity, bias=t.col("bsq"),
                                   scale=1.0 / WS).then_inc(copied.sem, 1)
                    act.wait_ge(made.sem, made.at(b, 3))
                    act.activation(t.v_tok[:, b, :, :].rearrange("p a c -> p (a c)"), a_ps[:, :],
                                   ACT.Copy, scale=1.0 / WS).then_inc(copied.sem, 1)

                def output(b):
                    act.wait_ge(summed.sem, summed.at(b, 1))
                    act.activation(t.h_seq[:, b, :], h_ps[:, :], ACT.Copy).then_inc(h_copied.sem, 1)

                stage_x(0)
                act.wait_ge(w_loaded, 48)
                act.activation(w_hi[:, :, :], w_all[:, :, :], ACT.Copy, scale=WS).then_inc(w_steps, 1)
                high_parts(0)
                inputs(0)
                with act.Fori(0, B - 1) as b:
                    stage_x(b + 1)
                    high_parts(b + 1)
                    inputs(b + 1)
                    output(b)
                output(B - 1)

            @block.vector
            def _(dve):
                dve.sem_inc(kv_done.sem, kv_done.start)
                dve.sem_inc(scanned.sem, scanned.start)
                dve.sem_inc(normed.sem, normed.start)

                def statistics(b):
                    for k in range(2):
                        dve.wait_ge(turned.sem, turned.at(b, k))
                        for j in range(NT):
                            cols = slice((k * NT + j) * P, (k * NT + j + 1) * P)
                            dve.bn_stats(stats[:, k, j, :], a_ps[:, cols])
                        dve.drain()
                        for j in range(NT):
                            last = dve.bn_aggr(mv[:, k, j, :], stats[:, k, j, :])
                        last.then_inc(got_mv.sem, 1)

                def normalise(b):
                    for k in range(2):
                        dve.wait_ge(rstd_steps.sem, rstd_steps.at(b, 2 * k + 1))
                        dve.wait_ge(z_turned.sem, z_turned.before(b, k, 2))
                        for j in range(NT):
                            cols = slice((k * NT + j) * P, (k * NT + j + 1) * P)
                            last = dve.tensor_scalar(z_tok[:, k, j * P:(j + 1) * P], a_ps[:, cols], mv[:, k, j, 0:1],
                                                     rstd[:, k, j:j + 1], ALU.subtract, ALU.mult)
                        last.then_inc(normed.sem, 1)

                def low_parts(b):
                    for k in range(2):
                        dve.wait_ge(z_copied.sem, z_copied.at(b, k))
                        dve.tensor_tensor(z_lo[:, b, HALVES[k]], a_ps[:, HALVES[k]], z_hi[:, b, HALVES[k]],
                                          ALU.subtract).then_inc(z_rest.sem, 1)

                def weights():
                    dve.tensor_scalar(bg_neg[:, :], t.col("bg"), -1.0, None, ALU.mult)
                    dve.tensor_scalar(bsk_small[:, :], t.col("bsk"), 1.0 / WS, None, ALU.mult)
                    dve.tensor_scalar(bsv_large[:, :], t.col("bsv", 0, HD), WS, None, ALU.mult)
                    dve.wait_ge(w_loaded, 48)
                    dve.wait_ge(w_steps, 1)
                    dve.scalar_tensor_tensor(w_lo[:, :, :], w_all[:, :, :], WS, w_hi[:, :, :], ALU.mult,
                                             ALU.subtract).then_inc(w_steps, 1)

                def outer(b, n):
                    if n % HD == 0:
                        dve.wait_ge(copied.sem, copied.at(b + n // HD, 0))
                    dve.wait_ge(v_made.sem, v_made.at(b, n))
                    dve.wait_ge(scanned.sem, scanned.before(b, n, 2))
                    m = n % HD
                    dve.scalar_tensor_tensor(kv[:, n % 2, :], v_ps[n % 2][:, :], bsv_large[:, m:m + 1], k_sb[:, :],
                                             ALU.add, ALU.mult).then_inc(kv_done.sem, 1)

                def scan(b, n):
                    if n % HD == 0:
                        dve.wait_ge(copied.sem, copied.at(b + n // HD, 1))
                    dve.wait_ge(kv_done.sem, kv_done.at(b, n))
                    dve.wait_ge(weighed.sem, weighed.before(b, n, 2))
                    dve.tensor_tensor_scan(mem[:, n % 2, :], g_sb[:, :], kv[:, n % 2, :], 0.0, ALU.mult,
                                           ALU.add).then_inc(scanned.sem, 1)

                def body(b, n):
                    following = there(b, HD, HD)
                    if n == 4 and following:
                        statistics(b + 1)
                    if n == 5 and following:
                        normalise(b + 1)
                    if n == HD:
                        scan(b, n - 1)
                        if following:
                            outer(b, n)
                        return
                    if there(b, n, HD):
                        outer(b, n)
                    if n == 7 and following:
                        low_parts(b + 1)
                    if n >= 1 and there(b, n - 1, HD):
                        scan(b, n - 1)

                statistics(0)
                weights()
                normalise(0)
                low_parts(0)
                pipelined(dve, 1, HD, body)

            @block.gpsimd
            def _(pool):
                pool.sem_inc(weighed.sem, weighed.start)

                def deviation(b):
                    for k in range(2):
                        pool.wait_ge(got_mv.sem, got_mv.at(b, k))
                        pool.tensor_tensor(veps[:, k, :], mv[:, k, :, 1], t.eps[:, :],
                                           ALU.add).then_inc(rstd_steps.sem, 1)
                        pool.wait_ge(rstd_steps.sem, rstd_steps.at(b, 2 * k))
                        pool.tensor_tensor(rstd[:, k, :], veps[:, k, :], t.minus_half[:, 0:NT],
                                           ALU.pow).then_inc(rstd_steps.sem, 1)

                def body(b, last):
                    pool.wait_ge(copied.sem, copied.at(b, 2))
                    for n in range(HD):
                        if n == 3 and not last:
                            deviation(b + 1)
                        pool.wait_ge(scanned.sem, scanned.at(b, n))
                        pool.wait_ge(summed.sem, summed.before(b, n // 4, 2))
                        pool.tensor_tensor(qm[:, n, :], mem[:, n % 2, :], q_sb[:, :],
                                           ALU.mult).then_inc(weighed.sem, 1)

                deviation(0)
                with pool.Fori(0, B - 1) as b:
                    body(b, False)
                body(B - 1, True)


def queries_and_keys(t, s):
    nc, d = t.nc, t.dram
    t.part = part = s.sb("part", [P, B, 2, 2, T], F16)
    with Stage(nc, "qk") as q:
        mats = q.sb("mats", [P, 2, P])
        rows = q.sb("rows", [P, 2, P])
        temp = q.sb("temp", [P, 4, H])
        h_b = q.sb("h_b", [P, T])
        raw = q.sb("raw", [P, 2, TT, P])
        sq = q.sb("sq", [P, 2, TT, P])
        ss = q.sb("ss", [P, 2, 2, TT * H])
        rn = q.sb("rn", [P, 2, 2, TT * H])
        rt = q.sb("rt", [P, TT * H])
        unit = q.sb("unit", [P, 2, TT, P])
        tok_ps = [q.ps(f"tok_ps{x}", [P, TT, P]) for x in range(2)]
        u_ps = [q.ps(f"u_ps{x}", [P, T]) for x in range(2)]
        w_loaded, temp_steps = q.sem("w_loaded"), q.sem("temp_steps")
        h_staged = q.count("h_staged", 1)
        made = q.count("made", 2, 2)
        raw_done = q.count("raw_done", 2, 2)
        squared = q.count("squared", 2, 2)
        sums = q.count("sums", 2 * 2, 4)
        rooted = q.count("rooted", 2, 2)
        inverted = q.count("inverted", 2, 2)
        scaled = q.count("scaled", 1, 1)
        unit_done = q.count("unit_done", 2, 2)
        turned = q.count("turned", 2, 2)
        hi_done = q.count("hi_done", 2, 2)
        lo_done = q.count("lo_done", 2, 2)

        with nc.Block() as block:

            @block.sync
            def _(sp):
                sp.dma_start(mats[:, :, :], d["att_mats"]).then_inc(w_loaded, 16)
                sp.dma_start(rows[:, :, :], d["bqk"]).then_inc(w_loaded, 16)

            @block.tensor
            def _(pe):
                pe.sem_inc(made.sem, made.start)
                pe.sem_inc(turned.sem, turned.start)
                pe.wait_ge(w_loaded, 32)

                def project(b):
                    pe.wait_ge(h_staged.sem, h_staged.at(b))
                    for x in range(2):
                        pe.wait_ge(raw_done.sem, raw_done.before(b, x, 2))
                        for j in range(TT):
                            last = pe.matmul(tok_ps[x][:, j, :], h_b[:, j * P:(j + 1) * P], mats[:, x, :], start=True,
                                             stop=True)
                        last.then_inc(made.sem, 1)

                def turn(b):
                    for x in range(2):
                        pe.wait_ge(unit_done.sem, unit_done.at(b, x))
                        pe.wait_ge(lo_done.sem, lo_done.before(b, x, 2))
                        for j in range(TT):
                            last = pe.transpose(u_ps[x][:, j * P:(j + 1) * P], unit[:, x, j, :], t.ident[:, :])
                        last.then_inc(turned.sem, 1)

                project(0)
                with pe.Fori(0, B - 1) as b:
                    project(b + 1)
                    turn(b)
                turn(B - 1)

            @block.scalar
            def _(act):
                act.sem_inc(squared.sem, squared.start)
                act.sem_inc(rooted.sem, rooted.start)
                act.sem_inc(hi_done.sem, hi_done.start)
                act.activation(temp[:, 0, :], t.col("temp", 0, H), ACT.Abs).then_inc(temp_steps, 1)
                act.wait_ge(temp_steps, 1)
                act.activation(temp[:, 1, :], temp[:, 0, :], ACT.Exp, scale=-1.0).then_inc(temp_steps, 1)
                act.wait_ge(temp_steps, 2)
                act.activation(temp[:, 2, :], temp[:, 1, :], ACT.Ln, bias=1.0).then_inc(temp_steps, 1)

                def stage_h(b):
                    act.wait_ge(made.sem, made.before(b, 1, 2))
                    act.activation(h_b[:, :], t.h_seq[:, b, :], ACT.Copy).then_inc(h_staged.sem, 1)

                def norms(b):
                    for x in range(2):
                        act.wait_ge(raw_done.sem, raw_done.at(b, x))
                        act.wait_ge(sums.sem, sums.before(b, 2 * x, 4))
                        act.activation(sq[:, x, :, :], raw[:, x, :, :], ACT.Square).then_inc(squared.sem, 1)
                    for x in range(2):
                        act.wait_ge(sums.sem, sums.at(b, 2 * x + 1))
                        act.wait_ge(inverted.sem, inverted.before(b, x, 2))
                        act.activation(rn[:, x, 1, :], ss[:, x, 1, :], ACT.Sqrt).then_inc(rooted.sem, 1)

                def high_parts(b):
                    for x in range(2):
                        act.wait_ge(turned.sem, turned.at(b, x))
                        act.activation(part[:, b, x, 0, :], u_ps[x][:, :], ACT.Copy).then_inc(hi_done.sem, 1)

                stage_h(0)
                norms(0)
                with act.Fori(0, B - 1) as b:
                    stage_h(b + 1)
                    norms(b + 1)
                    high_parts(b)
                high_parts(B - 1)

            @block.vector
            def _(dve):
                for c in (raw_done, sums, inverted, scaled, unit_done, lo_done):
                    dve.sem_inc(c.sem, c.start)
                dve.wait_ge(temp_steps, 3)
                dve.scalar_tensor_tensor(temp[:, 3, :], t.col("temp", 0, H), 0.0, temp[:, 2, :], ALU.max,
                                         ALU.add).then_inc(temp_steps, 1)
                dve.wait_ge(temp_steps, 4)
                dve.wait_ge(w_loaded, 32)
                heat = temp[:, 3, :].rearrange("p (o h) -> p o h", o=1).broadcast_to([P, TT, H])

                def units(b):
                    for x in range(2):
                        dve.wait_ge(made.sem, made.at(b, x))
                        dve.wait_ge(squared.sem, squared.before(b, x, 2))
                        dve.wait_ge(unit_done.sem, unit_done.before(b, x, 2))
                        bias = rows[:, x, :].rearrange("p (o c) -> p o c", o=1).broadcast_to([P, TT, P])
                        dve.tensor_tensor(raw[:, x, :, :], tok_ps[x][:, :, :], bias,
                                          ALU.add).then_inc(raw_done.sem, 1)
                    for x in range(2):
                        dve.wait_ge(squared.sem, squared.at(b, x))
                        dve.tensor_reduce(ss[:, x, 0, :],
                                          sq[:, x, :, :].rearrange("p a (h c) -> p (a h) c", c=HD), AX.X,
                                          ALU.add).then_inc(sums.sem, 1)
                        dve.wait_ge(sums.sem, sums.at(b, 2 * x))
                        dve.wait_ge(rooted.sem, rooted.before(b, x, 2))
                        dve.tensor_scalar(ss[:, x, 1, :], ss[:, x, 0, :], 1e-24, None,
                                          ALU.max).then_inc(sums.sem, 1)
                    for x in range(2):
                        dve.wait_ge(rooted.sem, rooted.at(b, x))
                        dve.wait_ge(unit_done.sem, unit_done.before(b, x, 2))
                        dve.reciprocal(rn[:, x, 0, :], rn[:, x, 1, :]).then_inc(inverted.sem, 1)
                    dve.wait_ge(inverted.sem, inverted.at(b, 0))
                    dve.tensor_tensor(rt[:, :].rearrange("p (a h) -> p a h", h=H),
                                      rn[:, 0, 0, :].rearrange("p (a h) -> p a h", h=H), heat,
                                      ALU.mult).then_inc(scaled.sem, 1)
                    dve.wait_ge(scaled.sem, scaled.at(b))
                    for x in range(2):
                        dve.wait_ge(inverted.sem, inverted.at(b, x))
                        dve.wait_ge(turned.sem, turned.before(b, x, 2))
                        factor = (rt[:, :], rn[:, 1, 0, :])[x].rearrange("p (n o) -> p n o", o=1).broadcast_to([P, TT * H, HD])
                        dve.tensor_tensor(unit[:, x, :, :].rearrange("p a (h c) -> p (a h) c", c=HD),
                                          raw[:, x, :, :].rearrange("p a (h c) -> p (a h) c", c=HD), factor,
                                          ALU.mult).then_inc(unit_done.sem, 1)

                def low_parts(b):
                    for x in range(2):
                        dve.wait_ge(hi_done.sem, hi_done.at(b, x))
                        dve.tensor_tensor(part[:, b, x, 1, :], u_ps[x][:, :], part[:, b, x, 0, :],
                                          ALU.subtract).then_inc(lo_done.sem, 1)

                units(0)
                with dve.Fori(0, B - 1) as b:
                    units(b + 1)
                    low_parts(b)
                low_parts(B - 1)


def attention(t):
    nc, d = t.nc, t.dram
    RING = 4
    OUT_AT = 15
    with Stage(nc, "att") as q:
        q_st, k_st = (q.sb(n, [P, 2, T], F16) for n in ("q_st", "k_st"))
        km = q.sb("km", [P, 2, GH, T], F16)
        va = q.sb("va", [P, 2, KC, GH, 32])
        prob = q.sb("prob", [P, RING, GH, HALF])
        o_sb, num, den, att = (t.h_seq[:, i, :] for i in range(B))
        wo = q.sb("wo", [P, P])
        bias = q.sb("bias", [P, 1])
        s_ps = [q.ps(f"s_ps{k}", [P, 2, HALF]) for k in range(3)]
        o_ps = [q.ps(f"o_ps{k}", [P, HALF]) for k in range(2)]
        U = 2 * KC
        w_loaded, bias_steps = q.sem("w_loaded"), q.sem("bias_steps")
        blank = q.sem("blank")
        keyed = q.count("keyed", G)
        scored = q.count("scored", G * U * 2)
        exped = q.count("exped", G * U * 2, 3)
        used = q.count("used", G * U, RING)
        out_done = q.count("out_done", G * 2, 2)
        sending = q.sem("sending")
        moved = [q.sem(f"{n}_moved") for n in ("num", "den")]
        early_moved = [q.sem(f"early_{n}_moved") for n in ("num", "den")]
        recips = q.count("recips", G + 1)
        normed = q.count("normed", G + 1, G + 1)
        projected = q.count("projected", 1, 1)
        added = q.count("added", 1, 1)
        stacked = [q.sem(f"stacked{k}") for k in range(2)]
        MOVES = GH * 16
        STACK_MOVES = 2 * 4 * 16

        def wait_for_stack(eng, b, g):
            eng.wait_ge(stacked[g % 2], (b * 2 + g // 2 + 1) * STACK_MOVES)

        with nc.Block() as block:

            @block.gpsimd
            def _(pool):
                pool.memset(va[:, :, :, :, HD:32], 1.0).then_inc(blank, 1)

            @block.tensor
            def _(pe):
                pe.sem_inc(used.sem, used.start)
                pe.wait_ge(w_loaded, 16)
                pe.matmul(s_ps[0][:, 0, 0:1], wo[:, :], t.col("bv"), start=True, stop=True).then_inc(bias_steps, 1)
                pe.wait_ge(bias_steps, 2)

                def project(b, k):
                    for h in range(2):
                        pe.wait_ge(normed.sem, normed.before(b, G - 1 + h, G + 1))
                        last = pe.matmul(s_ps[k][:, h, :], wo[:, :], att[:, HALVES[h]], start=True, stop=True)
                    last.then_inc(projected.sem, 1)

                with pe.Fori(0, B) as b:

                    def scores(g, u, pair):
                        half, kc = divmod(u, KC)
                        n = (g * U + u) * 2 + pair
                        pe.wait_ge(exped.sem, exped.before(b, n, 3 if n >= 2 else 2))
                        if n == 2 * OUT_AT:
                            project(b, n % 3)
                            pe.wait_ge(added.sem, added.before(b, 0, 1))
                        for i in range(2):
                            j = 2 * pair + i
                            last = pe.matmul(s_ps[n % 3][:, i, :], km[:, g % 2, j, kc * P:(kc + 1) * P],
                                             q_st[:, g % 2, HALVES[half]], start=True, stop=True)
                        last.then_inc(scored.sem, 1)

                    def values(g, u, pair):
                        half, kc = divmod(u, KC)
                        if kc == 0 and pair == 0:
                            pe.wait_ge(out_done.sem, out_done.before(b, g * 2 + half, 2))
                        pe.wait_ge(exped.sem, exped.at(b, (g * U + u) * 2 + pair))
                        for j in (2 * pair, 2 * pair + 1):
                            last = pe.matmul(o_ps[half][32 * j:32 * j + 32, :], va[:, g % 2, kc, j, :],
                                             prob[:, u % RING, j, :], start=kc == 0, stop=kc == KC - 1)
                        if pair == 1:
                            last.then_inc(used.sem, 1)

                    for g in range(G):
                        wait_for_stack(pe, b, g)
                        pe.wait_ge(keyed.sem, keyed.at(b, g))
                        for u in range(U):
                            for pair in range(2):
                                scores(g, u, pair)
                                if (g, u) >= (0, 2):
                                    values(*divmod(g * U + u - 2, U), pair)
                    for u in (U - 2, U - 1):
                        for pair in range(2):
                            values(G - 1, u, pair)
                pe.wait_ge(exped.sem, exped.at(B - 1, G * U * 2 - 1))
                project(B, 0)

            @block.scalar
            def _(act):
                act.sem_inc(exped.sem, exped.start)
                with act.Fori(0, B) as b:
                    for g in range(G):
                        for u in range(U):
                            for pair in range(2):
                                n = (g * U + u) * 2 + pair
                                act.wait_ge(scored.sem, scored.at(b, n))
                                if pair == 0:
                                    act.wait_ge(used.sem, used.before(b, g * U + u, RING))
                                act.activation(prob[:, u % RING, 2 * pair:2 * pair + 2, :], s_ps[n % 3][:, :, :],
                                               ACT.Exp).then_inc(exped.sem, 1)

            @block.vector
            def _(dve):
                dve.memset(att, 0.0).then_inc(normed.sem, G + 1)
                dve.sem_inc(out_done.sem, out_done.start)
                dve.sem_inc(projected.sem, projected.start)
                dve.sem_inc(added.sem, added.start)
                dve.wait_ge(bias_steps, 1)
                dve.tensor_tensor(bias[:, :], s_ps[0][:, 0, 0:1], t.col("bo"), ALU.add).then_inc(bias_steps, 1)
                dve.wait_ge(blank, 1)

                def keys_and_values(b, g):
                    b, g = b + g // G, g % G
                    dve.tensor_copy(
                        va[:, g % 2, :, :, 0:HD],
                        t.v_tok[:, b, :, :].rearrange("p k (g j c) -> p g k j c", g=G, c=HD)[:, g, :, :, :])
                    wait_for_stack(dve, b, g)
                    for j in range(GH):
                        last = dve.tensor_scalar(km[:, g % 2, j, :], k_st[:, g % 2, :], t.col("head_mask", j), None,
                                                 ALU.mult)
                    last.then_inc(keyed.sem, 1)

                def divide(b, g, event, cols, moves, value):
                    mine = slice(32 * g, 32 * g + 32)
                    dve.wait_ge(moves[1], value)
                    dve.reciprocal(den[mine, cols], den[mine, cols]).then_inc(recips.sem, 1)
                    dve.wait_ge(recips.sem, recips.at(b, event))
                    dve.wait_ge(moves[0], value)
                    if g == 0:
                        dve.wait_ge(projected.sem, projected.at(b))
                    dve.tensor_tensor(att[mine, cols], num[mine, cols], den[mine, cols],
                                      ALU.mult).then_inc(normed.sem, 1)

                def body(b, n):
                    g = n - 2
                    if g >= 0:
                        for half in range(2):
                            dve.wait_ge(used.sem, used.at(b, g * U + half * KC + KC - 1))
                            dve.tensor_copy(o_sb[:, HALVES[half]], o_ps[half][:, :]).then_inc(out_done.sem, 1)
                            if g == G - 1 and half == 0:
                                divide(b, g, g, HALVES[0], early_moved, (b + 1) * MOVES)
                    if there(b, n, G):
                        keys_and_values(b, n)
                    if g >= 0:
                        last = g == G - 1
                        divide(b, g, G if last else g, HALVES[1] if last else slice(0, T), moved,
                               (b * G + g + 1) * MOVES)
                    if g == G - 1:
                        dve.wait_ge(projected.sem, projected.at(b + 1))
                        k = 0 if isinstance(b, int) and b == B - 1 else 2 * OUT_AT % 3
                        dve.scalar_tensor_tensor(t.x_t[:, b, :], s_ps[k][:, :, :].rearrange("p h c -> p (h c)"),
                                                 bias[:, 0:1], t.x_t[:, b, :], ALU.add, ALU.add).then_inc(added.sem, 1)

                pipelined(dve, 2, G, body)

            @block.sync
            def _(sp):
                sp.dma_start(wo[:, :], d["wo"]).then_inc(w_loaded, 16)

                def stack(b, g):
                    for x, to in enumerate((q_st, k_st)):
                        for row in range(4):
                            half = (row % 2, row // 2)[x]
                            sp.dma_start(to[32 * row:32 * row + 32, g % 2, :],
                                         t.part[32 * g:32 * g + 32, b, x, half, :]).then_inc(stacked[g % 2], 16)

                def move(b, g, half, cols, signals):
                    sp.wait_ge(out_done.sem, out_done.at(b, 2 * g + half))
                    sp.sem_inc(sending, 1)
                    for i, to in ((1, den), (0, num)):
                        for j in range(GH):
                            at, frm = HD * (GH * g + j), 32 * j + HD * i
                            sp.dma_start(to[at:at + HD, cols], o_sb[frm:frm + HD, cols]).then_inc(signals[i], 16)

                def body(b, n):
                    g = n - 2
                    if g >= 0:
                        if g < G - 1:
                            move(b, g, 1, slice(0, T), moved)
                        else:
                            move(b, g, 0, HALVES[0], early_moved)
                            move(b, g, 1, HALVES[1], moved)
                    if there(b, n, G):
                        stack(b + n // G, n % G)

                pipelined(sp, 2, G, body)


def store(t):
    nc, d = t.nc, t.dram
    with Stage(nc, "store") as s:
        x_half = s.sb("x_half", [P, 2, HALF])
        out = s.sb("out", [P, B, 2, NT, P])
        ps = [s.ps(f"ps{k}", [P, NT, P]) for k in range(2)]
        staged = s.count("staged", 2)
        turned = s.count("turned", 2, 2)
        copied = s.count("copied", 2, 2)
        stored = s.sem("stored")
        with nc.Block() as block:

            @block.scalar
            def _(act):
                with act.Fori(0, B) as b:
                    for k in range(2):
                        act.wait_ge(turned.sem, turned.before(b, k, 2))
                        act.activation(x_half[:, k, :], t.x_t[:, b, HALVES[k]], ACT.Copy).then_inc(staged.sem, 1)

            @block.tensor
            def _(pe):
                pe.sem_inc(turned.sem, turned.start)
                with pe.Fori(0, B) as b:
                    for k in range(2):
                        pe.wait_ge(staged.sem, staged.at(b, k))
                        pe.wait_ge(copied.sem, copied.before(b, k, 2))
                        for j in range(NT):
                            last = pe.transpose(ps[k][:, j, :], x_half[:, k, j * P:(j + 1) * P], t.ident[:, :])
                        last.then_inc(turned.sem, 1)

            @block.vector
            def _(dve):
                dve.sem_inc(copied.sem, copied.start)
                with dve.Fori(0, B) as b:
                    for k in range(2):
                        dve.wait_ge(turned.sem, turned.at(b, k))
                        dve.tensor_copy(out[:, b, k, :, :], ps[k][:, :, :]).then_inc(copied.sem, 1)

            @block.sync
            def _(sp):
                with sp.Fori(0, B) as b:
                    for k in range(2):
                        sp.wait_ge(copied.sem, copied.at(b, k))
                        sp.dma_start(d["out"][b, k], out[:, b, k, :, :]).then_inc(stored, 16)
                sp.wait_ge(stored, 16 * B * 2)


def hybrid_layer(nc, dram):
    t = Layer(nc, dram)
    with Stage(nc, "all") as whole:
        load_constants(t, whole)
        with Stage(nc, "ssm") as s:
            scan_buffers(t, s)
            with Stage(nc, "pre") as pre:
                t.z_t = pre.sb("z_t", [P, B, T])
                input_layernorms(t)
                scan_inputs(t)
            selective_scan(t)
        ffn(t, "ffn1")
        with Stage(nc, "hv") as s:
            t.h_seq = s.sb("h_seq", [P, B, T])
            t.v_tok = s.sb("v_tok", [P, B, TT, P])
            retention(t)
            queries_and_keys(t, s)
            attention(t)
        ffn(t, "ffn2")
        store(t)


def pack(i):
    a = {k: np.asarray(v) for k, v in i.items()}
    A = lambda n: a["L0_attn_a_" + n]
    R = lambda n: a["L0_attn_b_" + n]
    M = lambda n: a["L0_ffn_" + n]
    cols = {
        "ln_g": A("ln_g"), "ln_b": A("ln_b"), "w1_b": A("w1_b"), "v1_b": A("v1_b"), "w2_b": A("w2_b"),
        "conv": A("conv_w")[:, 0, :], "d_skip": A("D_skip"), "b_dt": A("b_dt"), "a_log": A("A_log"),
        "bsk": R("bsk"), "bsq": R("bsq"), "bg": np.repeat(R("bg"), HD),
        "bsv": np.repeat(R("bsv").reshape(H, HD)[:, COLUMNS], HD, axis=0), "bv": R("bv"), "bo": R("bo"),
        "alpha": np.full((P,), M("alpha")), "b1m": M("b1m").reshape(FC, P).T, "b2m": M("b2m"),
        "temp": np.tile(R("temp").reshape(1, H), (P, 1)),
        "head_mask": np.tile(np.repeat(np.eye(GH, dtype=np.float32), HD, axis=0), (P // (GH * HD), 1)),
    }
    vecs = np.concatenate([cols[n].reshape(P, k) for n, k in VEC_SIZES], axis=1)
    bc = np.concatenate([A("W_B"), A("W_C")], axis=1)
    wsv = R("Wsv").T.reshape(P, H, HD)[:, :, COLUMNS]
    head_sum = np.zeros((H, HD, 2, 2, H), np.float32)
    for h in range(H):
        for e in range(2):
            head_sum[h, :, e, e, h] = 1
    by_column = lambda w: w.T.reshape(H, HD, P).transpose(1, 0, 2).reshape(P, P)
    return {
        "x": A("x").reshape(B, 2, NT, P, P).transpose(0, 1, 3, 2, 4),
        "vecs": vecs,
        "ident": np.eye(P, dtype=np.float32),
        "w_gate": M("w_gate"),
        "b_gate": M("b_gate").reshape(1, E),
        "w1m": M("W1m"),
        "w2m": M("W2m").reshape(FC, P, P).transpose(1, 0, 2).reshape(P, FC * P),
        "ssm_mats": np.stack([A("w1_w"), A("v1_w"), A("w2_w"), A("W_dt")], axis=1),
        "wbc": np.tile(bc, (1, 3)),
        "pick": np.tile(np.eye(2 * NS, dtype=np.float32), (3, 1)),
        "ret_mats": np.stack([R("Wsk").T, R("Wsq").T, np.repeat(R("Wg").T, HD, axis=1), R("Wv").T], axis=1),
        "wsv": np.repeat(wsv.transpose(0, 2, 1)[:, :, :, None], HD, axis=3).reshape(P, HD, P),
        "head_sum": head_sum.reshape(P, 2, 2 * H),
        "att_mats": np.stack([by_column(R("Wq")), by_column(R("Wk"))], axis=1),
        "bqk": np.tile(np.stack([R("bq"), R("bk")])[None], (P, 1, 1)),
        "wo": R("Wo").T,
        "w1e": M("W1e"),
        "w2e": M("W2e").reshape(E, FC, P, P).transpose(0, 2, 1, 3).reshape(E, P, FC * P),
        "be": np.concatenate([M("b1e").reshape(E, FC, P).transpose(0, 2, 1), M("b2e").reshape(E, P, 1)], axis=2),
    }


def program(nc, arrays):
    dram = {n: nc.dram_tensor("in_" + n, a.shape, F32, kind="ExternalInput").ap() for n, a in arrays.items()}
    out = nc.dram_tensor("out", (B, 2, NT, P, P), F32, kind="ExternalOutput").ap()
    dram["x"] = dram["x"].rearrange("b k p j c -> b k p (j c)")
    dram["out"] = out.rearrange("b k j p c -> b k p j c")
    hybrid_layer(nc, dram)


def kernel(**inputs):
    import concourse.bacc as bacc
    from concourse.bass_utils import run_bass_kernel_spmd

    arrays = {n: np.ascontiguousarray(a) for n, a in pack(inputs).items()}
    nc = bacc.Bacc("TRN2", target_bir_lowering=False, num_devices=1)
    program(nc, arrays)
    r = run_bass_kernel_spmd(nc, [{"in_" + n: a for n, a in arrays.items()}], core_ids=[0])
    return r.results[0]["out"].reshape(B, T, P)
```
